# Optimizing a Trainium2 kernel written in Bass

```python
import numpy as np
import jax
import jax.numpy as jnp

def _softmax(x, axis=-1):
    return jax.nn.softmax(x, axis=axis)

def _gelu(x):
    return jax.nn.gelu(x, approximate=True)

def _silu(x):
    return jax.nn.silu(x)

def _sigmoid(x):
    return jax.nn.sigmoid(x)

def _layernorm(x, axis=-1, eps=1e-05):
    m = jnp.mean(x, axis=axis, keepdims=True)
    v = jnp.var(x, axis=axis, keepdims=True)
    return (x - m) / jnp.sqrt(v + eps)

def _scatter_add(tgt, idx, src, axis=0):
    return tgt.at[idx].add(src)

def _segment_sum(src, seg, n):
    return jax.ops.segment_sum(src, seg, n)
kernel_name = 'mk_adaln_attn_ffn_d1_seqx_r4_c9ca4f'

def setup_inputs(seed: int=0):
    np.random.seed(seed)
    _w = jnp.asarray

    def _rec_inputs():
        import jax
        import jax.numpy as jnp
        _rk = jax.random.key(seed)
        x = -0.000125 + 0.9999 * jax.random.normal(jax.random.fold_in(_rk, 1), (4, 512, 512), jnp.float32)
        _lenS = 512 - jax.random.randint(jax.random.fold_in(_rk, 7), (4,), 0, max(1, 512 // 4) + 1, jnp.int32)
        _lenS2 = 512 - jax.random.randint(jax.random.fold_in(_rk, 8), (4,), 0, max(1, 512 // 4) + 1, jnp.int32)
        fside_BxSxS_0 = -1.52775e-05 + 0.999936 * jax.random.normal(jax.random.fold_in(_rk, 11), (4, 512, 512), jnp.float32)
        cond_512 = -5.03954e-05 + 1.00559 * jax.random.normal(jax.random.fold_in(_rk, 12), (4, 128), jnp.float32)
        return (x, fside_BxSxS_0, cond_512)
    x, fside_BxSxS_0, cond_512 = _rec_inputs()

    def _L0_cond_setup():
        import jax, jax.numpy as jnp
        from jax import lax
        import numpy as np
        B, T, C, TD = (8, 512, 512, 128)

        def _bi_wkv(r, k, v, w, u, time_emb):
            tf = jax.nn.sigmoid(jnp.sum(time_emb, axis=-1))[:, None, None]
            decay = jnp.exp(-jnp.exp(w.astype(jnp.float32)))[None, :] * (0.5 + 0.5 * tf[:, :, 0])
            kf = k.astype(jnp.float32)
            vf = v.astype(jnp.float32)
            ek = jnp.exp(jnp.minimum(kf, 30.0))
            ekv = ek * vf

            def step(carry, x):
                a, b = carry
                ekv_t, ek_t = x
                a = a * decay + ekv_t
                b = b * decay + ek_t
                return ((a, b), (a, b))
            ekv_t = jnp.swapaxes(ekv, 0, 1)
            ek_t = jnp.swapaxes(ek, 0, 1)
            init = (jnp.zeros_like(decay), jnp.zeros_like(decay))
            _, (nf, df) = lax.scan(step, init, (ekv_t, ek_t))
            _, (nb, db) = lax.scan(step, init, (ekv_t, ek_t), reverse=True)
            nf = jnp.swapaxes(nf, 0, 1)
            df = jnp.swapaxes(df, 0, 1)
            nb = jnp.swapaxes(nb, 0, 1)
            db = jnp.swapaxes(db, 0, 1)
            euk = jnp.exp(jnp.minimum(u.astype(jnp.float32)[None, None, :] + kf, 30.0))
            num = nf + nb - ekv + euk * vf
            den = df + db - ek + euk
            base = jax.nn.sigmoid(r.astype(jnp.float32)) * (num / jnp.maximum(den, 1e-08))
            out = base * (0.8 + 0.2 * tf)
            return out.astype(r.dtype)
        key = jax.random.key(seed)
        ks = jax.random.split(key, 6)
        return {'r': jax.random.normal(ks[0], (B, T, C), dtype=jnp.float32), 'k': jax.random.normal(ks[1], (B, T, C), dtype=jnp.float32), 'v': jax.random.normal(ks[2], (B, T, C), dtype=jnp.float32), 'w': jax.random.normal(ks[3], (C,), dtype=jnp.float32), 'u': jax.random.normal(ks[4], (C,), dtype=jnp.float32), 'time_emb': jax.random.normal(ks[5], (B, TD), dtype=jnp.float32)}
    _L0_cond_all = _L0_cond_setup()
    _L0_cond_in = {k: v for k, v in _L0_cond_all.items() if k in ('w', 'u')}
    del _L0_cond_all

    def _L0_attn_setup():
        import jax, jax.numpy as jnp
        import numpy as np
        DIM = 512
        B, T = (8, 512)

        def _layernorm(x, g, b, eps=1e-05):
            m = jnp.mean(x, axis=-1, keepdims=True)
            v = jnp.mean(jnp.square(x - m), axis=-1, keepdims=True)
            return (x - m) / jnp.sqrt(v + eps) * g + b

        def _shift(x):
            return jnp.pad(x[:, :-1, :], ((0, 0), (1, 0), (0, 0)))
        key = jax.random.key(seed)
        ks = jax.random.split(key, 16)
        d = DIM
        s = 0.02
        inp = {'x': jax.random.normal(ks[0], (B, T, d), dtype=jnp.float32), 'ln1_g': jnp.ones((d,), jnp.float32), 'ln1_b': jnp.zeros((d,), jnp.float32), 'ln2_g': jnp.ones((d,), jnp.float32), 'ln2_b': jnp.zeros((d,), jnp.float32), 'tm_w': jnp.zeros((d,), jnp.float32), 'tm_u': jnp.zeros((d,), jnp.float32), 'tm_mu_r': jax.random.uniform(ks[1], (d,), jnp.float32), 'tm_mu_k': jax.random.uniform(ks[2], (d,), jnp.float32), 'tm_mu_v': jax.random.uniform(ks[3], (d,), jnp.float32), 'tm_Wr': jax.random.normal(ks[4], (d, d), jnp.float32) * s, 'tm_Wk': jax.random.normal(ks[5], (d, d), jnp.float32) * s, 'tm_Wv': jax.random.normal(ks[6], (d, d), jnp.float32) * s, 'tm_Wout': jax.random.normal(ks[7], (d, d), jnp.float32) * s, 'cm_mu_r': jax.random.uniform(ks[8], (d,), jnp.float32), 'cm_mu_k': jax.random.uniform(ks[9], (d,), jnp.float32), 'cm_Wr': jax.random.normal(ks[10], (d, d), jnp.float32) * s, 'cm_Wk': jax.random.normal(ks[11], (d, d), jnp.float32) * s, 'cm_Wv': jax.random.normal(ks[12], (d, d), jnp.float32) * s}
        return inp
    _L0_attn_all = _L0_attn_setup()
    _L0_attn_in = {k: v for k, v in _L0_attn_all.items() if k in ('ln1_g', 'ln1_b', 'ln2_g', 'ln2_b', 'tm_w', 'tm_u', 'tm_mu_r', 'tm_mu_k', 'tm_mu_v', 'tm_Wr', 'tm_Wk', 'tm_Wv', 'tm_Wout', 'cm_mu_r', 'cm_mu_k', 'cm_Wr', 'cm_Wk', 'cm_Wv')}
    del _L0_attn_all

    def _L0_cond2_setup():
        import jax, jax.numpy as jnp
        from jax import lax
        import numpy as np
        B, T, C, TD = (8, 512, 512, 128)

        def _bi_wkv(r, k, v, w, u, time_emb):
            tf = jax.nn.sigmoid(jnp.sum(time_emb, axis=-1))[:, None, None]
            decay = jnp.exp(-jnp.exp(w.astype(jnp.float32)))[None, :] * (0.5 + 0.5 * tf[:, :, 0])
            kf = k.astype(jnp.float32)
            vf = v.astype(jnp.float32)
            ek = jnp.exp(jnp.minimum(kf, 30.0))
            ekv = ek * vf

            def step(carry, x):
                a, b = carry
                ekv_t, ek_t = x
                a = a * decay + ekv_t
                b = b * decay + ek_t
                return ((a, b), (a, b))
            ekv_t = jnp.swapaxes(ekv, 0, 1)
            ek_t = jnp.swapaxes(ek, 0, 1)
            init = (jnp.zeros_like(decay), jnp.zeros_like(decay))
            _, (nf, df) = lax.scan(step, init, (ekv_t, ek_t))
            _, (nb, db) = lax.scan(step, init, (ekv_t, ek_t), reverse=True)
            nf = jnp.swapaxes(nf, 0, 1)
            df = jnp.swapaxes(df, 0, 1)
            nb = jnp.swapaxes(nb, 0, 1)
            db = jnp.swapaxes(db, 0, 1)
            euk = jnp.exp(jnp.minimum(u.astype(jnp.float32)[None, None, :] + kf, 30.0))
            num = nf + nb - ekv + euk * vf
            den = df + db - ek + euk
            base = jax.nn.sigmoid(r.astype(jnp.float32)) * (num / jnp.maximum(den, 1e-08))
            out = base * (0.8 + 0.2 * tf)
            return out.astype(r.dtype)
        key = jax.random.key(seed)
        ks = jax.random.split(key, 6)
        return {'r': jax.random.normal(ks[0], (B, T, C), dtype=jnp.float32), 'k': jax.random.normal(ks[1], (B, T, C), dtype=jnp.float32), 'v': jax.random.normal(ks[2], (B, T, C), dtype=jnp.float32), 'w': jax.random.normal(ks[3], (C,), dtype=jnp.float32), 'u': jax.random.normal(ks[4], (C,), dtype=jnp.float32), 'time_emb': jax.random.normal(ks[5], (B, TD), dtype=jnp.float32)}
    _L0_cond2_all = _L0_cond2_setup()
    _L0_cond2_in = {k: v for k, v in _L0_cond2_all.items() if k in ('w', 'u')}
    del _L0_cond2_all

    def _L0_ffn_setup():
        import jax, jax.numpy as jnp
        import numpy as np
        H, LAT, INTER, E, G, TOPK_G, TOP_K = (512, 256, 256, 32, 4, 2, 8)
        SHARED_INTER = 1024
        ROUTED_SCALE = 2.5
        B, S = (2, 256)

        def relu2(x):
            return jnp.square(jax.nn.relu(x))
        key = jax.random.key(seed)
        ks = jax.random.split(key, 9)
        w = 0.02
        return {'hidden_states': jax.random.normal(ks[0], (B, S, H), jnp.float32), 'gate_w': jax.random.normal(ks[1], (E, H), jnp.float32) * w, 'gate_bias': jax.random.normal(ks[2], (E,), jnp.float32) * w, 'fc1_w': jax.random.normal(ks[3], (LAT, H), jnp.float32) * w, 'fc2_w': jax.random.normal(ks[4], (H, LAT), jnp.float32) * w, 'w1': jax.random.normal(ks[5], (E, INTER, LAT), jnp.float32) * w, 'w2': jax.random.normal(ks[6], (E, LAT, INTER), jnp.float32) * w, 'shared_up_w': jax.random.normal(ks[7], (SHARED_INTER, H), jnp.float32) * w, 'shared_down_w': jax.random.normal(ks[8], (H, SHARED_INTER), jnp.float32) * w}
    _L0_ffn_all = _L0_ffn_setup()
    _L0_ffn_in = {k: v for k, v in _L0_ffn_all.items() if k in ('gate_w', 'gate_bias', 'fc1_w', 'fc2_w', 'w1', 'w2', 'shared_up_w', 'shared_down_w')}
    del _L0_ffn_all
    return {'x': x, 'fside_BxSxS_0': fside_BxSxS_0, 'cond_512': cond_512, 'L0_cond_w': _L0_cond_in['w'], 'L0_cond_u': _L0_cond_in['u'], 'L0_attn_ln1_g': _L0_attn_in['ln1_g'], 'L0_attn_ln1_b': _L0_attn_in['ln1_b'], 'L0_attn_ln2_g': _L0_attn_in['ln2_g'], 'L0_attn_ln2_b': _L0_attn_in['ln2_b'], 'L0_attn_tm_w': _L0_attn_in['tm_w'], 'L0_attn_tm_u': _L0_attn_in['tm_u'], 'L0_attn_tm_mu_r': _L0_attn_in['tm_mu_r'], 'L0_attn_tm_mu_k': _L0_attn_in['tm_mu_k'], 'L0_attn_tm_mu_v': _L0_attn_in['tm_mu_v'], 'L0_attn_tm_Wr': _L0_attn_in['tm_Wr'], 'L0_attn_tm_Wk': _L0_attn_in['tm_Wk'], 'L0_attn_tm_Wv': _L0_attn_in['tm_Wv'], 'L0_attn_tm_Wout': _L0_attn_in['tm_Wout'], 'L0_attn_cm_mu_r': _L0_attn_in['cm_mu_r'], 'L0_attn_cm_mu_k': _L0_attn_in['cm_mu_k'], 'L0_attn_cm_Wr': _L0_attn_in['cm_Wr'], 'L0_attn_cm_Wk': _L0_attn_in['cm_Wk'], 'L0_attn_cm_Wv': _L0_attn_in['cm_Wv'], 'L0_cond2_w': _L0_cond2_in['w'], 'L0_cond2_u': _L0_cond2_in['u'], 'L0_ffn_gate_w': _L0_ffn_in['gate_w'], 'L0_ffn_gate_bias': _L0_ffn_in['gate_bias'], 'L0_ffn_fc1_w': _L0_ffn_in['fc1_w'], 'L0_ffn_fc2_w': _L0_ffn_in['fc2_w'], 'L0_ffn_w1': _L0_ffn_in['w1'], 'L0_ffn_w2': _L0_ffn_in['w2'], 'L0_ffn_shared_up_w': _L0_ffn_in['shared_up_w'], 'L0_ffn_shared_down_w': _L0_ffn_in['shared_down_w']}

def reference(x, fside_BxSxS_0, cond_512, L0_cond_w, L0_cond_u, L0_attn_ln1_g, L0_attn_ln1_b, L0_attn_ln2_g, L0_attn_ln2_b, L0_attn_tm_w, L0_attn_tm_u, L0_attn_tm_mu_r, L0_attn_tm_mu_k, L0_attn_tm_mu_v, L0_attn_tm_Wr, L0_attn_tm_Wk, L0_attn_tm_Wv, L0_attn_tm_Wout, L0_attn_cm_mu_r, L0_attn_cm_mu_k, L0_attn_cm_Wr, L0_attn_cm_Wk, L0_attn_cm_Wv, L0_cond2_w, L0_cond2_u, L0_ffn_gate_w, L0_ffn_gate_bias, L0_ffn_fc1_w, L0_ffn_fc2_w, L0_ffn_w1, L0_ffn_w2, L0_ffn_shared_up_w, L0_ffn_shared_down_w):
    import jax
    import jax.numpy as jnp

    def _L0_cond_ref(r, k, v, w, u, time_emb):
        import jax, jax.numpy as jnp
        from jax import lax
        import numpy as np
        B, T, C, TD = (8, 512, 512, 128)

        def _bi_wkv(r, k, v, w, u, time_emb):
            tf = jax.nn.sigmoid(jnp.sum(time_emb, axis=-1))[:, None, None]
            decay = jnp.exp(-jnp.exp(w.astype(jnp.float32)))[None, :] * (0.5 + 0.5 * tf[:, :, 0])
            kf = k.astype(jnp.float32)
            vf = v.astype(jnp.float32)
            ek = jnp.exp(jnp.minimum(kf, 30.0))
            ekv = ek * vf

            def step(carry, x):
                a, b = carry
                ekv_t, ek_t = x
                a = a * decay + ekv_t
                b = b * decay + ek_t
                return ((a, b), (a, b))
            ekv_t = jnp.swapaxes(ekv, 0, 1)
            ek_t = jnp.swapaxes(ek, 0, 1)
            init = (jnp.zeros_like(decay), jnp.zeros_like(decay))
            _, (nf, df) = lax.scan(step, init, (ekv_t, ek_t))
            _, (nb, db) = lax.scan(step, init, (ekv_t, ek_t), reverse=True)
            nf = jnp.swapaxes(nf, 0, 1)
            df = jnp.swapaxes(df, 0, 1)
            nb = jnp.swapaxes(nb, 0, 1)
            db = jnp.swapaxes(db, 0, 1)
            euk = jnp.exp(jnp.minimum(u.astype(jnp.float32)[None, None, :] + kf, 30.0))
            num = nf + nb - ekv + euk * vf
            den = df + db - ek + euk
            base = jax.nn.sigmoid(r.astype(jnp.float32)) * (num / jnp.maximum(den, 1e-08))
            out = base * (0.8 + 0.2 * tf)
            return out.astype(r.dtype)
        return _bi_wkv(r, k, v, w, u, time_emb)

    def _L0_attn_ref(x, ln1_g, ln1_b, ln2_g, ln2_b, tm_w, tm_u, tm_mu_r, tm_mu_k, tm_mu_v, tm_Wr, tm_Wk, tm_Wv, tm_Wout, cm_mu_r, cm_mu_k, cm_Wr, cm_Wk, cm_Wv):
        import jax, jax.numpy as jnp
        import numpy as np
        DIM = 512
        B, T = (8, 512)

        def _layernorm(x, g, b, eps=1e-05):
            m = jnp.mean(x, axis=-1, keepdims=True)
            v = jnp.mean(jnp.square(x - m), axis=-1, keepdims=True)
            return (x - m) / jnp.sqrt(v + eps) * g + b

        def _shift(x):
            return jnp.pad(x[:, :-1, :], ((0, 0), (1, 0), (0, 0)))
        h = _layernorm(x, ln1_g, ln1_b)
        hp = _shift(h)
        xr = tm_mu_r * h + (1.0 - tm_mu_r) * hp
        xk = tm_mu_k * h + (1.0 - tm_mu_k) * hp
        xv = tm_mu_v * h + (1.0 - tm_mu_v) * hp
        r = jax.nn.sigmoid(jnp.einsum('btc,dc->btd', xr, tm_Wr))
        k = jnp.einsum('btc,dc->btd', xk, tm_Wk)
        v = jnp.einsum('btc,dc->btd', xv, tm_Wv)
        ek = jnp.exp(tm_u + k)
        wkv = ek * v / (ek + 1e-08)
        x = x + jnp.einsum('btc,dc->btd', r * wkv, tm_Wout)
        h2 = _layernorm(x, ln2_g, ln2_b)
        h2p = _shift(h2)
        xr2 = cm_mu_r * h2 + (1.0 - cm_mu_r) * h2p
        xk2 = cm_mu_k * h2 + (1.0 - cm_mu_k) * h2p
        r2 = jax.nn.sigmoid(jnp.einsum('btc,dc->btd', xr2, cm_Wr))
        k2 = jnp.square(jax.nn.relu(jnp.einsum('btc,dc->btd', xk2, cm_Wk)))
        x = x + r2 * jnp.einsum('btc,dc->btd', k2, cm_Wv)
        return x

    def _L0_cond2_ref(r, k, v, w, u, time_emb):
        import jax, jax.numpy as jnp
        from jax import lax
        import numpy as np
        B, T, C, TD = (8, 512, 512, 128)

        def _bi_wkv(r, k, v, w, u, time_emb):
            tf = jax.nn.sigmoid(jnp.sum(time_emb, axis=-1))[:, None, None]
            decay = jnp.exp(-jnp.exp(w.astype(jnp.float32)))[None, :] * (0.5 + 0.5 * tf[:, :, 0])
            kf = k.astype(jnp.float32)
            vf = v.astype(jnp.float32)
            ek = jnp.exp(jnp.minimum(kf, 30.0))
            ekv = ek * vf

            def step(carry, x):
                a, b = carry
                ekv_t, ek_t = x
                a = a * decay + ekv_t
                b = b * decay + ek_t
                return ((a, b), (a, b))
            ekv_t = jnp.swapaxes(ekv, 0, 1)
            ek_t = jnp.swapaxes(ek, 0, 1)
            init = (jnp.zeros_like(decay), jnp.zeros_like(decay))
            _, (nf, df) = lax.scan(step, init, (ekv_t, ek_t))
            _, (nb, db) = lax.scan(step, init, (ekv_t, ek_t), reverse=True)
            nf = jnp.swapaxes(nf, 0, 1)
            df = jnp.swapaxes(df, 0, 1)
            nb = jnp.swapaxes(nb, 0, 1)
            db = jnp.swapaxes(db, 0, 1)
            euk = jnp.exp(jnp.minimum(u.astype(jnp.float32)[None, None, :] + kf, 30.0))
            num = nf + nb - ekv + euk * vf
            den = df + db - ek + euk
            base = jax.nn.sigmoid(r.astype(jnp.float32)) * (num / jnp.maximum(den, 1e-08))
            out = base * (0.8 + 0.2 * tf)
            return out.astype(r.dtype)
        return _bi_wkv(r, k, v, w, u, time_emb)

    def _L0_ffn_ref(hidden_states, gate_w, gate_bias, fc1_w, fc2_w, w1, w2, shared_up_w, shared_down_w):
        import jax, jax.numpy as jnp
        import numpy as np
        H, LAT, INTER, E, G, TOPK_G, TOP_K = (512, 256, 256, 32, 4, 2, 8)
        SHARED_INTER = 1024
        ROUTED_SCALE = 2.5
        B, S = (2, 256)

        def relu2(x):
            return jnp.square(jax.nn.relu(x))
        orig_shape = hidden_states.shape
        x = hidden_states.reshape(-1, H)
        T = x.shape[0]
        logits = jnp.einsum('th,eh->te', x.astype(jnp.float32), gate_w)
        scores = jax.nn.sigmoid(logits)
        sb = scores + gate_bias
        grp = sb.reshape(T, G, E // G)
        group_scores = jax.lax.top_k(grp, 2)[0].sum(-1)
        _, gidx = jax.lax.top_k(group_scores, TOPK_G)
        gmask = jax.nn.one_hot(gidx, G, dtype=sb.dtype).sum(1)
        masked = jnp.where(gmask[:, :, None] > 0, grp, -jnp.inf).reshape(T, E)
        _, topi = jax.lax.top_k(masked, TOP_K)
        wsel = jnp.take_along_axis(scores, topi, axis=1)
        wsel = wsel / wsel.sum(-1, keepdims=True) * ROUTED_SCALE
        cw = jnp.zeros((T, E), jnp.float32).at[jnp.arange(T)[:, None], topi].add(wsel)
        x_lat = x @ fc1_w.T
        h = relu2(jnp.einsum('tl,eil->eti', x_lat, w1))
        h = h * cw.T[:, :, None]
        y_lat = jnp.einsum('eti,eli->tl', h, w2)
        routed = y_lat @ fc2_w.T
        shared = relu2(x @ shared_up_w.T) @ shared_down_w.T
        return (shared + routed).reshape(orig_shape)
    x = x + _L0_attn_ref(_L0_cond_ref(x, fside_BxSxS_0, fside_BxSxS_0, L0_cond_w, L0_cond_u, cond_512), L0_attn_ln1_g, L0_attn_ln1_b, L0_attn_ln2_g, L0_attn_ln2_b, L0_attn_tm_w, L0_attn_tm_u, L0_attn_tm_mu_r, L0_attn_tm_mu_k, L0_attn_tm_mu_v, L0_attn_tm_Wr, L0_attn_tm_Wk, L0_attn_tm_Wv, L0_attn_tm_Wout, L0_attn_cm_mu_r, L0_attn_cm_mu_k, L0_attn_cm_Wr, L0_attn_cm_Wk, L0_attn_cm_Wv)
    x = x + _L0_ffn_ref(_L0_cond2_ref(x, fside_BxSxS_0, fside_BxSxS_0, L0_cond2_w, L0_cond2_u, cond_512), L0_ffn_gate_w, L0_ffn_gate_bias, L0_ffn_fc1_w, L0_ffn_fc2_w, L0_ffn_w1, L0_ffn_w2, L0_ffn_shared_up_w, L0_ffn_shared_down_w)
    return x

_drawn_inputs = setup_inputs


def setup_inputs(seed=0):
    import zlib

    import numpy as np

    out = dict(_drawn_inputs(seed))
    spreads = {'L0_attn_ln1_g': (1.0, 0.2),
     'L0_attn_ln1_b': (0.0, 0.1),
     'L0_attn_ln2_g': (1.0, 0.2),
     'L0_attn_ln2_b': (0.0, 0.1),
     'L0_attn_tm_w': (0.0, 0.1),
     'L0_attn_tm_u': (0.0, 0.1)}
    factors = {}
    for name, (base, spread) in spreads.items():
        noise = np.random.default_rng([zlib.crc32(name.encode()), seed]).standard_normal(out[name].shape)
        drawn = base * np.exp(spread * noise) if base else spread * noise
        out[name] = jnp.asarray(drawn.astype(out[name].dtype))
    for name, factor in factors.items():
        out[name] = (out[name] * factor).astype(out[name].dtype)
    return out
```

```python
import math
from contextlib import ExitStack

import concourse.bass as bass
from concourse import mybir

F32 = mybir.dt.float32
ALU = mybir.AluOpType
ACT = mybir.ActivationFunctionType
AX = mybir.AxisListType

P = 128
VECTORS = ['cond_w', 'cond2_w', 'cond_u', 'cond2_u', 'tm_u', 'ln1_g', 'ln1_b', 'ln2_g', 'ln2_b',
           'mu_r', 'mu_k', 'mu_v', 'cm_mu_r', 'cm_mu_k']
SQUARES = ['Wr', 'Wk', 'Wv', 'Wout', 'cWr', 'cWk', 'cWv']
KEY_CAP = 30.0
DEN_FLOOR = 1e-8
LN_EPS = 1e-5
ROUTED_SCALE = 2.5
GATE_SHIFT = -math.log(1e-8)


class Steps:

    def __init__(self, eng, sem):
        self.eng, self.sem, self.base, self.n = eng, sem, 0, 0

    def did(self, instruction):
        instruction.then_inc(self.sem, 1)
        self.n += 1

    def wait(self):
        self.eng.wait_ge(self.sem, self.base + self.n)

    def rebase(self, base):
        self.base, self.n = base, 0


def build(nc, A):
    B, C, T = A['xT'].shape
    K = C // P
    E = A['gateT'].shape[1]
    LAT = A['fc1T'].shape[1]
    KL = LAT // P
    INTER = A['w1T'].shape[2]
    KI = INTER // P
    SH = A['upT'].shape[1]
    KS = SH // P
    TT = T // P
    NT = B * TT
    G = 4
    EG = E // G
    TOPG, TOPK = 2, 8
    assert T == 512 and C == 512 and B == 4 and K == 4

    q2_dram = nc.dram_tensor("q2_scratch", [B, C, T], F32).ap()
    xs_dram = nc.dram_tensor("xs_scratch", [B, C, T], F32).ap()

    ctx = ExitStack()
    with ctx:
        limit = 212800 // 4
        arena = ctx.enter_context(nc.sbuf_tensor("arena", [P, limit], F32))
        psum = ctx.enter_context(nc.psum_tensor("banks", [P, 8, 512], F32))
        top = [0]

        def place(*dims):
            n = math.prod(dims)
            at = top[0]
            top[0] += (n + 7) // 8 * 8
            assert top[0] <= limit, (top[0], limit)
            v = arena[:, at:at + n]
            if len(dims) == 1:
                return v
            names = 'abcd'[:len(dims)]
            return v.rearrange(f"p ({' '.join(names)}) -> p {' '.join(names)}",
                               **{c: d for c, d in zip(names, dims)})

        def sem(name):
            return ctx.enter_context(nc.semaphore(name))

        ones = place(P)
        vec = place(len(VECTORS), K)
        small = place(64)
        tf = small[:, 0:4]
        out_scale = small[:, 4:8]
        decay_b = small[:, 8:12]
        eps_col = small[:, 12:13]
        tmu = small[:, 16:20]
        wexp = small[:, 24:32]
        wexp3 = wexp.rearrange("p (w k) -> p w k", w=2)
        condT = small[:, 32:36]
        decay = place(2, K, B)
        rest = place(2, K, B)
        scratch32 = place(2, K, B)
        ini = place(2, 2)
        XN = place(B, K, T)
        kept = top[0]

        W = {n: place(K, C) for n in SQUARES}
        H = place(K, T + 1)
        MR, MK, MV = (place(K, T) for _ in range(3))
        NR, NK = (place(K, T) for _ in range(2))
        PROD = place(K, T)
        R2S, K2S = (place(K, T) for _ in range(2))
        SRt, SKt = (place(T) for _ in range(2))
        XA = place(2, T)
        XF = place(2, T)
        QF = place(2, T)
        RS, TMP = (place(T) for _ in range(2))
        KV = place(2, T)
        EK, EV = (place(T) for _ in range(2))
        EU, EUV = (place(2, T) for _ in range(2))
        F = place(2, 2, T)
        INV = place(T)

        def V(name, k):
            return vec[:, VECTORS.index(name), k:k + 1]

        def bank(n):
            return psum[:, n, :]

        S = {n: sem(n) for n in '''
            params_loaded ones_ready cond_summed cond_ready coeffs_ready
            keys_clipped keys_exp ev_ready fwd_done scaled bwd_done den_ready num_ready inv_ready fin_done
            q2_stored0 q2_stored1 k_loaded0 k_loaded1
            xa_loaded0 xa_loaded1 sigx_ready y_ready y_tile
            z1_ready sq1_ready mean1_done var1_done rs1_ready norm1_ready h1_ready mix1_ready
            z2_ready sq2_ready mean2_done var2_done rs2_ready norm2_ready h2_ready mix2_ready
            r_mm k_mm v_mm o_mm r2_mm k2_mm v2_mm
            r_evac k_evac v_evac o_evac r2_evac k2_evac k2_ready v2_evac
            xf_loaded0 xf_loaded1 qf_loaded0 qf_loaded1 xnew_ready xnew_sig xs_ready xs_stored0 xs_stored1
            dve_step act_step pool_step sp_settled pool_settled
            p2_weights p2_w2 xs_loaded0 xs_loaded1 gate_mm gate_evac lat_mm lat_evac up_mm up_relu up_ready down_mm down_evac
            route_ready ident_ready w1_loaded0 w1_loaded1 w2_loaded0 w2_loaded1
            h_mm h_relu h_ready ylat_mm ylat_acc
            acc_zero yT_mm yT_ready fc2_mm out_ready out_stored0 out_stored1 mask_ready logits_ready sig_ready
            '''.split()}
        w_loaded = {n: sem("loaded_" + n) for n in SQUARES}

        def item(i, half, b, k, w, par, stored):
            return dict(i=i, half=half, b=b, k=k, w=w, par=par, stored=stored, prev=None)

        first_items = [item(k, k // 2, 0, k, 0, k % 2, 0) for k in range(K)]
        ORDER = [(1, 0)] + [(0, k) for k in range(K)] + [(1, k) for k in range(1, K)]

        def body_items(b):
            return [item(K + 8 * b + j, 2 + 4 * b + j // 2, b if w else b + 1, k, w, j % 2,
                         2 * b + (1 if j in (2, 4, 6, 7) else 0)) for j, (w, k) in enumerate(ORDER)]

        def last_items(b):
            return [item(K + 8 * b + k, 2 + 4 * b + k // 2, b, k, 1, k % 2, 2 * b + k // 2) for k in range(K)]

        def view(dram, b):
            return dram[b].rearrange("(k p) t -> p k t", p=P)

        top[0] = kept
        UPW = place(K, SH)
        FC1 = place(K, LAT)
        GATE = place(K, E)
        DOWNW = place(KS, C)
        XS = place(B, K, T)
        HS = place(KS, T)
        XL = place(KL, B * T)
        ACC = place(NT, LAT)
        IDENT = place(P)
        W1 = place(2, KL, INTER)
        W2 = place(2, KI, LAT)
        HE = place(2, KI, T)
        FC2 = place(KL, C)
        YL = place(KL, T)
        BIAS = place(E)
        SC, SB, GT, EQ, PRE, RM, CW = (place(NT, E) for _ in range(7))
        M8 = place(NT * G, 8)
        GS, GM, OFF = (place(NT, G) for _ in range(3))
        RK, RE = (place(NT, G, G) for _ in range(2))
        LOWER = place(G, G)
        T8 = place(NT, 8)
        CNT, TOT = (place(NT) for _ in range(2))

        def part2_sp(sp):
            ld = lambda dst, name, p=P: sp.dma_start(dst, A[name].rearrange("(k p) d -> p k d", p=p))
            sp.wait_ge(S['v_mm'], 4 * B)
            ld(UPW, 'upT').then_inc(S['p2_weights'], 16)
            sp.wait_ge(S['xs_stored0'], 16 * 2 * B)
            sp.wait_ge(S['xs_stored1'], 16 * 2 * B)
            sp.wait_ge(S['v2_mm'], 4 * B)
            ld(GATE, 'gateT').then_inc(S['p2_weights'], 16)
            ld(FC1, 'fc1T').then_inc(S['p2_weights'], 16)
            for b in range(B):
                sp.dma_start(XS[:, b], view(xs_dram, b)).then_inc(S['xs_loaded0'], 16)
            sp.dma_start(BIAS, A['bias'].partition_broadcast(P)).then_inc(S['p2_w2'], 16)
            ld(DOWNW, 'downT').then_inc(S['p2_w2'], 16)
            ld(FC2, 'fc2T').then_inc(S['p2_w2'], 16)
            with sp.Fori(0, E // 2) as h:
                for q in range(2):
                    e = 2 * h + q
                    sp.wait_ge(S['ylat_acc'], NT * e)
                    sp.sem_inc(S['sp_settled'], 1)
                    sp.dma_start(W1[:, q], A['w1T'][bass.ds(e, 1)].rearrange("o (k p) i -> p (o k) i", p=P))\
                      .then_inc(S[f'w1_loaded{q}'], 16)
                    sp.dma_start(W2[:, q], A['w2T'][bass.ds(e, 1)].rearrange("o (k p) i -> p (o k) i", p=P))\
                      .then_inc(S[f'w2_loaded{q}'], 16)
            for b in range(B):
                for m in range(K):
                    sp.wait_ge(S['out_ready'], 4 * b + m + 1)
                    sp.dma_start(view(A['out'], b)[:, m, :], XN[:, b, m]).then_inc(S['out_stored0'], 16)
            sp.wait_ge(S['out_stored0'], 16 * B * K)

        def part3_pool(pool):
            pool.wait_ge(S['xs_stored0'], 16 * 2 * B)
            pool.wait_ge(S['xs_stored1'], 16 * 2 * B)
            pool.wait_ge(S['v2_mm'], 4 * B)
            pool.memset(IDENT, 0.0).then_inc(S['ident_ready'], 1)
            pool.wait_ge(S['ident_ready'], 1)
            pool.affine_select(out=IDENT, in_=IDENT, compare_op=ALU.not_equal, fill=1.0, base=0,
                               pattern=[[-1, P]], channel_multiplier=1).then_inc(S['ident_ready'], 1)

        def part2_pe(pe):
            def product(out, w, x, m, kt):
                for k in range(kt):
                    ins = pe.matmul(out, w[:, k, m * P:(m + 1) * P], x[k], start=(k == 0), stop=(k == kt - 1))
                return ins

            def dyn(buf, b, k):
                return buf[:, bass.ds(b, 1), k].rearrange("p o t -> p (o t)")

            pe.wait_ge(S['p2_weights'], 48)
            pe.wait_ge(S['xs_loaded0'], 16 * B)
            for b in range(B):
                for tt in range(TT):
                    n = b * TT + tt
                    for k in range(K):
                        ins = pe.matmul(bank(7)[:, n * E:(n + 1) * E], XS[:, b, k, tt * P:(tt + 1) * P], GATE[:, k],
                                        start=(k == 0), stop=(k == K - 1))
            ins.then_inc(S['gate_mm'], 1)
            with pe.Fori(0, B) as b:
                for m in range(KL):
                    pe.wait_ge(S['lat_evac'], KL * b)
                    product(bank(5 + m), FC1, [dyn(XS, b, k) for k in range(K)], m, K).then_inc(S['lat_mm'], 1)
            pe.wait_ge(S['p2_w2'], 48)
            with pe.Fori(0, B) as b:
                for m in range(KS):
                    pe.wait_ge(S['up_relu'], KS * b + (m - 3 + 1 if m >= 3 else 0))
                    product(bank(m % 3), UPW, [dyn(XS, b, k) for k in range(K)], m, K).then_inc(S['up_mm'], 1)
                pe.wait_ge(S['up_ready'], KS // 2 * (b + 1))
                for m in range(K):
                    pe.wait_ge(S['down_evac'], 4 * b + (m - 2 + 1 if m >= 2 else 0))
                    product(bank(3 + m % 2), DOWNW, [HS[:, k] for k in range(KS)], m, KS).then_inc(S['down_mm'], 1)

            def h_tiles(e, q, t):
                n = KI * (B * e + t)
                for m in range(KI):
                    pe.wait_ge(S['h_relu'], n + m - 3 if t >= 2 else KI * B * e)
                    product(bank((t % 2) * 2 + m), W1[:, q], [XL[:, k, t * T:(t + 1) * T] for k in range(KL)], m, KL)\
                        .then_inc(S['h_mm'], 1)

            def y_tiles(e, q, t):
                pe.wait_ge(S['h_ready'], B * e + t + 1)
                for tt in range(TT):
                    n = NT * e + TT * t + tt
                    if tt % 2 == 0:
                        pe.wait_ge(S['ylat_acc'], NT + n - 2 * TT + 2)
                    out = bank(4 + (t % 2) * 2 + tt // 2)[:, (tt % 2) * LAT:(tt % 2 + 1) * LAT]
                    for k in range(KI):
                        ins = pe.matmul(out, HE[:, t % 2, k, tt * P:(tt + 1) * P], W2[:, q, k],
                                        start=(k == 0), stop=(k == KI - 1))
                    ins.then_inc(S['ylat_mm'], 1)

            pe.wait_ge(S['down_evac'], K * B)
            with pe.Fori(0, E // 2) as h:
                for q in range(2):
                    e = 2 * h + q
                    pe.wait_ge(S[f'w1_loaded{q}'], 16 * h + 16)
                    h_tiles(e, q, 0)
                    pe.wait_ge(S[f'w2_loaded{q}'], 16 * h + 16)
                    for t in range(1, B):
                        h_tiles(e, q, t)
                        y_tiles(e, q, t - 1)
                    y_tiles(e, q, B - 1)
            pe.wait_ge(S['ident_ready'], 2)
            pe.wait_ge(S['ylat_acc'], NT * (E + 1))
            for b in range(B):
                if b:
                    pe.wait_ge(S['yT_ready'], b)
                for k in range(KL):
                    for tt in range(TT):
                        ins = pe.transpose(bank(k)[:, tt * P:(tt + 1) * P], ACC[:, b * TT + tt, k * P:(k + 1) * P], IDENT)
                ins.then_inc(S['yT_mm'], 1)
                pe.wait_ge(S['yT_ready'], b + 1)
                for m in range(K):
                    if b:
                        pe.wait_ge(S['out_ready'], 4 * (b - 1) + m + 1)
                    product(bank(2 + m), FC2, [YL[:, k] for k in range(KL)], m, KL).then_inc(S['fc2_mm'], 1)

        def part2_act(act, step):
            act.wait_ge(S['logits_ready'], 1)
            act.activation(SC, SC, ACT.Sigmoid).then_inc(S['sig_ready'], 1)
            with act.Fori(0, B) as b:
                for m in range(KS):
                    act.wait_ge(S['up_mm'], KS * b + m + 1)
                    act.activation(HS[:, m], bank(m % 3), ACT.Relu).then_inc(S['up_relu'], 1)
                    if m % 2:
                        act.wait_ge(S['up_relu'], KS * b + m + 1)
                        act.activation(HS[:, m - 1:m + 1], HS[:, m - 1:m + 1], ACT.Square).then_inc(S['up_ready'], 1)
            with act.Fori(0, E) as e:
                for t in range(B):
                    if t >= 2:
                        act.wait_ge(S['ylat_mm'], NT * e + TT * (t - 1))
                    else:
                        act.wait_ge(S['ylat_mm'], NT * e)
                    for m in range(KI):
                        act.wait_ge(S['h_mm'], KI * (B * e + t) + m + 1)
                        act.activation(HE[:, t % 2, m], bank((t % 2) * 2 + m), ACT.Relu).then_inc(S['h_relu'], 1)
                    act.wait_ge(S['h_relu'], KI * (B * e + t) + KI)
                    act.activation(HE[:, t % 2], HE[:, t % 2], ACT.Square).then_inc(S['h_ready'], 1)

        def part2_dve(dve, step):
            def did(ins):
                step.did(ins)
                step.wait()

            dve.wait_ge(S['xs_stored0'], 16 * 2 * B)
            dve.wait_ge(S['xs_stored1'], 16 * 2 * B)
            dve.memset(ACC, 0.0).then_inc(S['ylat_acc'], NT)
            dve.memset(LOWER, 0.0)
            dve.memset(RM, 1.0)
            did(dve.memset(CNT, 0.0))
            for g in range(1, G):
                dve.memset(LOWER[:, g, 0:g], 1.0)
            did(dve.memset(RM[:, :, 0], 0.0))
            dve.wait_ge(S['gate_mm'], 1)
            dve.tensor_copy(SC.rearrange("p n e -> p (n e)"), bank(7)).then_inc(S['logits_ready'], 1)
            with dve.Fori(0, B) as b:
                for m in range(KL):
                    dve.wait_ge(S['lat_mm'], KL * b + m + 1)
                    dve.tensor_copy(XL[:, m, bass.ds(b * T, T)], bank(5 + m)).then_inc(S['lat_evac'], 1)
            dve.wait_ge(S['sig_ready'], 1)
            dve.wait_ge(S['p2_w2'], 48)
            bias = BIAS.rearrange("p (o e) -> p o e", o=1).to_broadcast([P, NT, E])
            did(dve.tensor_tensor(SB, SC, bias, ALU.add))
            groups = SB.rearrange("p n (g e) -> p (n g) e", g=G)
            for j in range(NT * G):
                ins = dve.max(M8[:, j], groups[:, j])
            did(ins)
            did(dve.tensor_tensor(GS.rearrange("p n g -> p (n g)"), M8[:, :, 0], M8[:, :, 1], ALU.add))
            own = GS.rearrange("p n (g o) -> p n g o", o=1).to_broadcast([P, NT, G, G])
            other = GS.rearrange("p n (o g) -> p n o g", o=1).to_broadcast([P, NT, G, G])
            dve.tensor_tensor(RK, other, own, ALU.is_gt)
            did(dve.tensor_tensor(RE, other, own, ALU.is_equal))
            low = LOWER.rearrange("p (o g) h -> p o g h", o=1).to_broadcast([P, NT, G, G])
            did(dve.tensor_tensor(RE, RE, low, ALU.mult))
            did(dve.tensor_tensor(RK, RK, RE, ALU.add))
            did(dve.tensor_reduce(GM, RK, AX.X, ALU.add))
            did(dve.tensor_scalar(GM, GM, float(TOPG), None, ALU.is_lt))
            did(dve.tensor_scalar(OFF, GM, 1e30, -1e30, ALU.mult, ALU.add))
            spread = lambda v: v.rearrange("p n (g o) -> p (n g) o", o=1).to_broadcast([P, NT * G, EG])
            did(dve.tensor_tensor(groups, groups, spread(GM), ALU.mult))
            did(dve.tensor_tensor(groups, groups, spread(OFF), ALU.add))
            for j in range(NT):
                ins = dve.max(T8[:, j], SB[:, j])
            did(ins)
            eighth = T8[:, :, TOPK - 1:TOPK].to_broadcast([P, NT, E])
            dve.tensor_tensor(GT, SB, eighth, ALU.is_gt)
            did(dve.tensor_tensor(EQ, SB, eighth, ALU.is_equal))
            dve.tensor_reduce(CNT, GT, AX.X, ALU.add)
            flat = lambda v: v.rearrange("p n e -> p (n e)")
            did(dve.tensor_tensor_scan(flat(PRE), flat(RM), flat(EQ), 0.0, ALU.mult, ALU.add))
            did(dve.tensor_scalar(CNT, CNT, -1.0, float(TOPK), ALU.mult, ALU.add))
            over = lambda v: v.rearrange("p (n o) -> p n o", o=1).to_broadcast([P, NT, E])
            did(dve.tensor_tensor(PRE, PRE, over(CNT), ALU.is_le))
            did(dve.tensor_tensor(EQ, EQ, PRE, ALU.mult))
            did(dve.tensor_tensor(GT, GT, EQ, ALU.add))
            did(dve.tensor_tensor(CW, GT, SC, ALU.mult))
            did(dve.tensor_reduce(TOT, CW, AX.X, ALU.add))
            did(dve.reciprocal(TOT, TOT))
            did(dve.tensor_scalar(TOT, TOT, ROUTED_SCALE, None, ALU.mult))
            did(dve.tensor_tensor(CW, CW, over(TOT), ALU.mult))
            with dve.Fori(0, B) as b:
                for m in range(K):
                    dve.wait_ge(S['down_mm'], 4 * b + m + 1)
                    x = XN[:, bass.ds(b, 1), m].rearrange("p o t -> p (o t)")
                    dve.tensor_tensor(x, x, bank(3 + m % 2), ALU.add).then_inc(S['down_evac'], 1)
            with dve.Fori(0, E) as e:
                for n in range(NT):
                    t, tt = divmod(n, TT)
                    dve.wait_ge(S['ylat_mm'], NT * e + (n // 2) * 2 + 2)
                    dve.wait_ge(S['ylat_acc'], NT * e + n + 1)
                    y = bank(4 + (t % 2) * 2 + tt // 2)[:, (tt % 2) * LAT:(tt % 2 + 1) * LAT]
                    dve.scalar_tensor_tensor(ACC[:, n], y, CW[:, n, bass.ds(e, 1)], ACC[:, n],
                                             ALU.mult, ALU.add).then_inc(S['ylat_acc'], 1)
            for b in range(B):
                dve.wait_ge(S['yT_mm'], b + 1)
                if b:
                    dve.wait_ge(S['fc2_mm'], 4 * b)
                for k in range(KL):
                    ins = dve.tensor_copy(YL[:, k], bank(k))
                ins.then_inc(S['yT_ready'], 1)
                for m in range(K):
                    dve.wait_ge(S['fc2_mm'], 4 * b + m + 1)
                    dve.tensor_tensor(XN[:, b, m], XN[:, b, m], bank(2 + m), ALU.add).then_inc(S['out_ready'], 1)

        block = ctx.enter_context(nc.Block())

        @block.sync
        def _(sp):
            sp.dma_start(vec, A['vectors'].rearrange("p (v k) -> p v k", k=K)).then_inc(S['params_loaded'], 16)
            sp.dma_start(condT, A['condT']).then_inc(S['params_loaded'], 16)

            def settle():
                sp.sem_inc(S['sp_settled'], 1)

            def load_key(it):
                par = it['par']
                if not (isinstance(it['i'], int) and it['i'] < 2):
                    sp.wait_ge(S['ev_ready'], it['i'] - 1)
                settle()
                sp.dma_start(KV[:, par], view(A['fT'], it['b'])[:, it['k'], :]).then_inc(S[f'k_loaded{par}'], 16)

            def store_q2(it):
                par = it['par']
                sp.wait_ge(S['fin_done'], it['i'] + 1)
                settle()
                sp.dma_start(view(q2_dram, it['b'])[:, it['k'], :], F[:, par, 0]).then_inc(S[f'q2_stored{par}'], 16)

            def load_x(b, k):
                if not (isinstance(b, int) and b == 0 and k < 2):
                    sp.wait_ge(S['y_tile'], 4 * b + k - 1)
                settle()
                sp.dma_start(XA[:, k % 2], view(A['xT'], b)[:, k, :]).then_inc(S[f'xa_loaded{k % 2}'], 16)

            def load_final(b, m):
                first = isinstance(b, int) and b == 0 and m < 2
                if m == 0:
                    sp.wait_ge(S['q2_stored0'], 16 * (2 * b + 2))
                    sp.wait_ge(S['q2_stored1'], 16 * (2 * b + 2))
                    settle()
                if not first:
                    sp.wait_ge(S['xnew_ready'], 4 * b + max(0, m - 1))
                settle()
                sp.dma_start(XF[:, m % 2], view(A['xT'], b)[:, m, :]).then_inc(S[f'xf_loaded{m % 2}'], 16)
                if not first:
                    sp.wait_ge(S[f'xs_stored{m % 2}'], 16 * (2 * b + m // 2))
                settle()
                sp.dma_start(QF[:, m % 2], view(q2_dram, b)[:, m, :]).then_inc(S[f'qf_loaded{m % 2}'], 16)

            def store_xs(b, m):
                sp.wait_ge(S['xs_ready'], 4 * b + m + 1)
                settle()
                sp.dma_start(view(xs_dram, b)[:, m, :], QF[:, m % 2]).then_inc(S[f'xs_stored{m % 2}'], 16)

            def final(b):
                for m in range(K):
                    store_xs(b, m)
                    if m + 2 < K:
                        load_final(b, m + 2)

            def iteration(b, prev, nxt, before):
                items = body_items(b) if nxt else last_items(b)
                for n, it in enumerate(items):
                    if n + 1 < len(items):
                        load_key(items[n + 1])
                    earlier = items[n - 1] if n else before
                    if earlier is not None and earlier['w'] == 1:
                        store_q2(earlier)
                    if nxt and n == 2:
                        load_x(b + 1, 0)
                        load_x(b + 1, 1)
                    if nxt and n == 5:
                        load_x(b + 1, 2)
                        load_x(b + 1, 3)
                    if prev and n == (5 if nxt else 1):
                        load_final(b - 1, 0)
                        load_final(b - 1, 1)
                if nxt:
                    load_key(last_items(b + 1)[0])
                else:
                    store_q2(items[-1])
                if prev:
                    final(b - 1)

            for it in first_items[:2]:
                load_key(it)
            for n in SQUARES[:3]:
                sp.dma_start(W[n], A[n].rearrange("(k p) d -> p k d", p=P)).then_inc(w_loaded[n], 16)
            for it in first_items[2:]:
                load_key(it)
            load_key(body_items(0)[0])
            load_x(0, 0)
            load_x(0, 1)
            for n in SQUARES[3:]:
                sp.dma_start(W[n], A[n].rearrange("(k p) d -> p k d", p=P)).then_inc(w_loaded[n], 16)
            load_x(0, 2)
            load_x(0, 3)
            iteration(0, False, True, None)
            with sp.Fori(1, B - 1) as b:
                iteration(b, True, True, body_items(b - 1)[-1])
            iteration(B - 1, True, False, body_items(B - 2)[-1])
            load_final(B - 1, 0)
            load_final(B - 1, 1)
            final(B - 1)
            part2_sp(sp)

        @block.gpsimd
        def _(pool):
            step = Steps(pool, S['pool_step'])
            pool.wait_ge(S['params_loaded'], 32)

            def settle():
                pool.sem_inc(S['pool_settled'], 1)

            def pre(it):
                i, k, w, par = it['i'], it['k'], it['w'], it['par']
                pool.wait_ge(S[f'k_loaded{par}'], 16 * it['half'] + 16)
                pool.wait_ge(S['fwd_done'], i)
                settle()
                pool.tensor_scalar(EK, KV[:, par], KEY_CAP, None, ALU.min)
                pool.tensor_scalar(EU[:, par], KV[:, par], V('cond2_u' if w else 'cond_u', k), KEY_CAP,
                                   ALU.add, ALU.min).then_inc(S['keys_clipped'], 1)

            def mid(it):
                i, par = it['i'], it['par']
                pool.wait_ge(S['keys_exp'], i + 1)
                pool.tensor_tensor(EV, EK, KV[:, par], ALU.mult)
                pool.tensor_tensor(EUV[:, par], EU[:, par], KV[:, par], ALU.mult).then_inc(S['ev_ready'], 1)

            def post(it):
                i, par = it['i'], it['par']
                pool.wait_ge(S['bwd_done'], i + 1)
                step.did(pool.tensor_tensor(F[:, par, 1], F[:, par, 1], EU[:, par], ALU.add))
                step.wait()
                settle()
                pool.tensor_scalar(F[:, par, 1], F[:, par, 1], DEN_FLOOR, None, ALU.max).then_inc(S['den_ready'], 1)
                pool.tensor_tensor(F[:, par, 0], F[:, par, 0], EUV[:, par], ALU.add).then_inc(S['num_ready'], 1)

            def slots(items, following):
                for n, it in enumerate(items):
                    nx = items[n + 1] if n + 1 < len(items) else following
                    if nx is not None:
                        pre(nx)
                        mid(nx)
                    post(it)

            pre(first_items[0])
            mid(first_items[0])
            slots(first_items, last_items(0)[0])
            slots(body_items(0), last_items(1)[0])
            base = step.n
            with pool.Fori(1, B - 1) as b:
                step.rebase(base + 8 * (b - 1))
                slots(body_items(b), last_items(b + 1)[0])
                assert step.n == 8
            step.rebase(base + 8 * (B - 2))
            slots(last_items(B - 1), None)
            part3_pool(pool)

        @block.scalar
        def _(act):
            step = Steps(act, S['act_step'])
            act.wait_ge(S['params_loaded'], 32)
            ww = vec[:, 0:2, :].rearrange("p w k -> p (w k)")
            step.did(act.activation(wexp, ww, ACT.Exp))
            step.wait()
            step.did(act.activation(wexp, wexp, ACT.Exp, scale=-1.0))
            act.wait_ge(S['cond_summed'], 1)
            act.activation(tf, bank(7)[:, 0:B], ACT.Sigmoid).then_inc(S['cond_ready'], 1)

            def pre(it):
                i, par = it['i'], it['par']
                act.wait_ge(S['keys_clipped'], i + 1)
                act.activation(EK, EK, ACT.Exp)
                act.activation(EU[:, par], EU[:, par], ACT.Exp).then_inc(S['keys_exp'], 1)

            def mid(it):
                i, par = it['i'], it['par']
                act.wait_ge(S['fwd_done'], i + 1)
                act.activation(F[:, par], F[:, par], ACT.Identity,
                               scale=rest[:, it['w'], it['k'], bass.ds(it['b'], 1)]).then_inc(S['scaled'], 1)

            def post(it):
                i, par = it['i'], it['par']
                act.wait_ge(S['den_ready'], i + 1)
                act.wait_ge(S['fin_done'], i)
                step.did(act.activation(INV, F[:, par, 1], ACT.Ln))
                step.wait()
                act.activation(INV, INV, ACT.Exp, scale=-1.0).then_inc(S['inv_ready'], 1)

            def slot(it, nx):
                mid(it)
                if nx is not None:
                    pre(nx)
                post(it)

            def gates(b, m):
                act.wait_ge(S['v_evac'], 4 * b + m)
                act.wait_ge(S['r_mm'], 4 * b + m + 1)
                act.activation(SRt, bank(0), ACT.Sigmoid).then_inc(S['r_evac'], 1)
                act.wait_ge(S['k_mm'], 4 * b + m + 1)
                act.activation(SKt, bank(1), ACT.Sigmoid, bias=tmu[:, m:m + 1]).then_inc(S['k_evac'], 1)

            def square(which, b):
                act.wait_ge(S[f'z{which}_ready'], b + 1)
                dst = MR if which == 1 else NR
                act.activation(dst, H[:, :, 1:T + 1], ACT.Square).then_inc(S[f'sq{which}_ready'], 1)

            def rsqrt(which, b):
                act.wait_ge(S[f'var{which}_done'], b + 1)
                step.did(act.activation(RS, bank(6), ACT.Ln, bias=eps_col))
                step.wait()
                act.activation(RS, RS, ACT.Exp, scale=-0.5).then_inc(S[f'rs{which}_ready'], 1)

            def affine(which, b):
                act.wait_ge(S[f'norm{which}_ready'], b + 1)
                for k in range(K):
                    ins = act.activation(H[:, k, 1:T + 1], H[:, k, 1:T + 1], ACT.Identity,
                                         scale=V(f'ln{which}_g', k), bias=V(f'ln{which}_b', k))
                ins.then_inc(S[f'h{which}_ready'], 1)

            def sig_x(b):
                for k in range(K):
                    act.wait_ge(S[f'xa_loaded{k % 2}'], 16 * (2 * b + k // 2 + 1))
                    act.activation(XA[:, k % 2], XA[:, k % 2], ACT.Sigmoid).then_inc(S['sigx_ready'], 1)

            def receptance2(b, m):
                act.wait_ge(S['r2_mm'], 4 * b + m + 1)
                if m == 0:
                    act.wait_ge(S['xnew_ready'], 4 * b)
                act.activation(R2S[:, m], bank(3 + m % 2), ACT.Sigmoid).then_inc(S['r2_evac'], 1)

            def key2(b, m):
                act.wait_ge(S['k2_mm'], 4 * b + m + 1)
                if m == 0:
                    act.wait_ge(S['v2_mm'], 4 * b)
                act.activation(K2S[:, m], bank(3 + m % 2), ACT.Relu).then_inc(S['k2_evac'], 1)
                if m % 2:
                    act.wait_ge(S['k2_evac'], 4 * b + m + 1)
                    act.activation(K2S[:, m - 1:m + 1], K2S[:, m - 1:m + 1], ACT.Square).then_inc(S['k2_ready'], 1)

            def sig_new(b):
                for m in range(K):
                    act.wait_ge(S['xnew_ready'], 4 * b + m + 1)
                    if not (isinstance(b, int) and b == 0 and m == 0):
                        act.wait_ge(S['xs_ready'], 4 * b + max(0, m - 1))
                    act.activation((TMP, RS)[m % 2], XN[:, bass.ds(b, 1), m].rearrange("p o t -> p (o t)"), ACT.Sigmoid).then_inc(S['xnew_sig'], 1)

            def front(b):
                sig_x(b)
                square(1, b)
                rsqrt(1, b)
                affine(1, b)

            def iteration(b, prev, nxt):
                items = body_items(b) if nxt else last_items(b)
                nexts = items[1:] + [last_items(b + 1)[0] if nxt else None]
                gates(b, 0)
                if prev:
                    square(2, b - 1)
                slot(items[0], nexts[0])
                gates(b, 1)
                if prev:
                    rsqrt(2, b - 1)
                    affine(2, b - 1)
                slot(items[1], nexts[1])
                gates(b, 2)
                slot(items[2], nexts[2])
                gates(b, 3)
                slot(items[3], nexts[3])
                if nxt:
                    slot(items[4], nexts[4])
                    sig_x(b + 1)
                if prev:
                    for m in range(K):
                        receptance2(b - 1, m)
                if nxt:
                    slot(items[5], nexts[5])
                if prev:
                    for m in range(K):
                        key2(b - 1, m)
                if nxt:
                    square(1, b + 1)
                    rsqrt(1, b + 1)
                    affine(1, b + 1)
                    slot(items[6], nexts[6])
                    slot(items[7], nexts[7])
                if prev:
                    sig_new(b - 1)

            pre(first_items[0])
            for it, nx in zip(first_items, first_items[1:] + [last_items(0)[0]]):
                slot(it, nx)
            front(0)
            iteration(0, False, True)
            base, one = step.n, 8 + 2
            with act.Fori(1, B - 1) as b:
                step.rebase(base + one * (b - 1))
                iteration(b, True, True)
                assert step.n == one, step.n
            step.rebase(base + one * (B - 2))
            iteration(B - 1, True, False)
            square(2, B - 1)
            rsqrt(2, B - 1)
            affine(2, B - 1)
            for m in range(K):
                receptance2(B - 1, m)
            for m in range(K):
                key2(B - 1, m)
            sig_new(B - 1)
            part2_act(act, step)

        @block.vector
        def _(dve):
            step = Steps(dve, S['dve_step'])
            dve.memset(H[:, :, 0:1], 0.0)
            dve.memset(eps_col, LN_EPS)
            dve.memset(ones, 1.0).then_inc(S['ones_ready'], 1)
            dve.wait_ge(S['params_loaded'], 32)
            dve.wait_ge(S['ones_ready'], 1)
            dve.tensor_scalar(tmu, vec[:, VECTORS.index('tm_u')], GATE_SHIFT, None, ALU.add)
            dve.wait_ge(S['cond_ready'], 1)
            dve.memset(ones, 1.0 / C).then_inc(S['ones_ready'], 1)
            step.did(dve.tensor_scalar(decay_b, tf, 0.5, 0.5, ALU.mult, ALU.add))
            step.did(dve.tensor_scalar(out_scale, tf, -0.2, -0.8, ALU.mult, ALU.add))
            step.wait()
            for b in range(B):
                step.did(dve.tensor_scalar(decay[:, :, :, b], wexp3, decay_b[:, b:b + 1], None, ALU.mult))
            step.wait()
            step.did(dve.tensor_scalar(scratch32, decay, -1.0, 1.0, ALU.mult, ALU.add))
            step.did(dve.tensor_scalar(rest, decay, 1.0, None, ALU.add))
            step.wait()
            step.did(dve.tensor_tensor(rest, rest, scratch32, ALU.mult))
            step.wait()

            def dcol(it):
                return decay[:, it['w'], it['k'], bass.ds(it['b'], 1)]

            def xn(b, m):
                return XN[:, bass.ds(b, 1), m].rearrange("p o t -> p (o t)")

            def xn_all(b):
                return XN[:, bass.ds(b, 1)].rearrange("p o k t -> p (o k) t")

            def fwd(it):
                i, par = it['i'], it['par']
                dve.wait_ge(S['ev_ready'], i + 1)
                if not (isinstance(i, int) and i < 2):
                    dve.wait_ge(S['fin_done'], i - 1)
                if not (isinstance(it['stored'], int) and it['stored'] == 0):
                    dve.wait_ge(S[f'q2_stored{par}'], 16 * it['stored'])
                d = dcol(it).to_broadcast([P, T])
                dve.tensor_tensor_scan(F[:, par, 0], d, EV, 0.0, ALU.mult, ALU.add)
                step.did(dve.tensor_tensor_scan(F[:, par, 1], d, EK, 0.0, ALU.mult, ALU.add))
                step.wait()
                dve.tensor_scalar(ini[:, par], F[:, par, :, T - 1], dcol(it), None, ALU.mult)\
                   .then_inc(S['fwd_done'], 1)

            def bwd(it):
                i, par = it['i'], it['par']
                dve.wait_ge(S['scaled'], i + 1)
                d = dcol(it).to_broadcast([P, T])
                for n in range(2):
                    ins = dve.tensor_tensor_scan(F[:, par, n, ::-1], d, F[:, par, n, ::-1],
                                                 ini[:, par, n:n + 1], ALU.mult, ALU.add)
                ins.then_inc(S['bwd_done'], 1)

            def fin(it):
                i, par = it['i'], it['par']
                dve.wait_ge(S['inv_ready'], i + 1)
                step.did(dve.tensor_tensor(F[:, par, 1], F[:, par, 1], INV, ALU.mult))
                dve.wait_ge(S['num_ready'], i + 1)
                step.did(dve.tensor_tensor(F[:, par, 0], F[:, par, 0], INV, ALU.mult))
                step.wait()
                dst = F[:, par, 0] if it['w'] else xn(it['b'], it['k'])
                dve.scalar_tensor_tensor(dst, F[:, par, 1], 2.0, F[:, par, 0], ALU.subtract, ALU.mult)\
                   .then_inc(S['fin_done'], 1)

            def slot(it):
                fwd(it)
                if it['prev'] is not None:
                    fin(it['prev'])
                bwd(it)

            def product(b, m):
                dve.wait_ge(S['k_evac'], 4 * b + m + 1)
                step.did(dve.tensor_tensor(PROD[:, m], SRt, SKt, ALU.mult))
                dve.wait_ge(S['v_mm'], 4 * b + m + 1)
                step.wait()
                dve.tensor_tensor(PROD[:, m], PROD[:, m], bank(2), ALU.mult).then_inc(S['v_evac'], 1)

            def y_stage(b):
                for k in range(K):
                    dve.wait_ge(S['sigx_ready'], 4 * b + k + 1)
                    if k == 0:
                        dve.wait_ge(S['fin_done'], K if isinstance(b, int) and b == 0 else 8 * b + 1)
                    ins = dve.scalar_tensor_tensor(xn(b, k), XA[:, k % 2], out_scale[:, bass.ds(b, 1)], xn(b, k),
                                                   ALU.mult, ALU.mult)
                    ins.then_inc(S['y_tile'], 1)

            def residual(b):
                for m in range(K):
                    dve.wait_ge(S['o_mm'], 4 * b + m + 1)
                    dve.tensor_tensor(xn(b, m), xn(b, m), bank(3 + m % 2), ALU.add).then_inc(S['o_evac'], 1)

            def center(which, b):
                dve.wait_ge(S[f'mean{which}_done'], b + 1)
                mean = psum[:, 5:6, :].to_broadcast([P, K, T])
                dve.tensor_tensor(H[:, :, 1:T + 1], xn_all(b), mean, ALU.subtract).then_inc(S[f'z{which}_ready'], 1)

            def normalise(which, b):
                dve.wait_ge(S[f'rs{which}_ready'], b + 1)
                step.did(dve.scalar_tensor_tensor(TMP, bank(6), eps_col, RS, ALU.add, ALU.mult))
                step.wait()
                step.did(dve.tensor_tensor(TMP, TMP, RS, ALU.mult))
                step.wait()
                step.did(dve.tensor_scalar(TMP, TMP, -0.5, 1.5, ALU.mult, ALU.add))
                step.wait()
                step.did(dve.tensor_tensor(RS, RS, TMP, ALU.mult))
                step.wait()
                rs = RS.rearrange("p (o t) -> p o t", o=1).to_broadcast([P, K, T])
                dve.tensor_tensor(H[:, :, 1:T + 1], H[:, :, 1:T + 1], rs, ALU.mult)\
                   .then_inc(S[f'norm{which}_ready'], 1)

            def mixes(which, b):
                dve.wait_ge(S[f'h{which}_ready'], b + 1)
                names, outs = ((['mu_r', 'mu_k', 'mu_v'], [MR, MK, MV]) if which == 1 else
                               (['cm_mu_r', 'cm_mu_k'], [NR, NK]))
                diff = outs[-1]
                step.did(dve.tensor_tensor(diff, H[:, :, 1:T + 1], H[:, :, 0:T], ALU.subtract))
                step.wait()
                for name, out in zip(names, outs):
                    for k in range(K):
                        ins = dve.scalar_tensor_tensor(out[:, k], diff[:, k], V(name, k), H[:, k, 0:T],
                                                       ALU.mult, ALU.add)
                    ins.then_inc(S[f'mix{which}_ready'], 1)

            def final_a(b, m):
                dve.wait_ge(S['v2_mm'], 4 * b + m + 1)
                dve.wait_ge(S['r2_evac'], 4 * b + m + 1)
                dve.tensor_tensor(R2S[:, m], R2S[:, m], bank(3 + m % 2), ALU.mult).then_inc(S['v2_evac'], 1)

            def x_new(b, m):
                dve.wait_ge(S['v2_evac'], 4 * b + m + 1)
                step.did(dve.tensor_tensor(xn(b, m), xn(b, m), R2S[:, m], ALU.add))
                dve.wait_ge(S[f'xf_loaded{m % 2}'], 16 * (2 * b + m // 2 + 1))
                step.wait()
                dve.tensor_tensor(xn(b, m), xn(b, m), XF[:, m % 2], ALU.add).then_inc(S['xnew_ready'], 1)

            def x_side(b, m):
                dve.wait_ge(S['xnew_sig'], 4 * b + m + 1)
                dve.wait_ge(S[f'qf_loaded{m % 2}'], 16 * (2 * b + m // 2 + 1))
                dve.scalar_tensor_tensor(QF[:, m % 2], (TMP, RS)[m % 2], out_scale[:, bass.ds(b, 1)], QF[:, m % 2],
                                         ALU.mult, ALU.mult).then_inc(S['xs_ready'], 1)

            def final_b(b):
                x_new(b, 0)
                x_new(b, 1)
                x_side(b, 0)
                x_new(b, 2)
                x_side(b, 1)
                x_new(b, 3)
                x_side(b, 2)
                x_side(b, 3)

            def chain(items, before):
                for n, it in enumerate(items):
                    it['prev'] = items[n - 1] if n else before
                return items

            def iteration(b, prev, nxt, before):
                items = chain(body_items(b) if nxt else last_items(b), before)
                if prev:
                    residual(b - 1)
                    center(2, b - 1)
                slot(items[0])
                product(b, 0)
                if prev:
                    normalise(2, b - 1)
                slot(items[1])
                product(b, 1)
                if prev:
                    mixes(2, b - 1)
                slot(items[2])
                product(b, 2)
                slot(items[3])
                product(b, 3)
                if nxt:
                    slot(items[4])
                    fin(items[4])
                    items[5]['prev'] = None
                    y_stage(b + 1)
                    slot(items[5])
                    center(1, b + 1)
                else:
                    fin(items[3])
                if prev:
                    final_a(b - 1, 0)
                    final_a(b - 1, 1)
                if nxt:
                    normalise(1, b + 1)
                if prev:
                    final_a(b - 1, 2)
                if nxt:
                    slot(items[6])
                if prev:
                    final_a(b - 1, 3)
                if nxt:
                    mixes(1, b + 1)
                    slot(items[7])
                if prev:
                    final_b(b - 1)

            chain(first_items, None)
            for it in first_items:
                slot(it)
            fin(first_items[-1])
            y_stage(0)
            center(1, 0)
            normalise(1, 0)
            mixes(1, 0)
            iteration(0, False, True, None)
            base, one = step.n, 8 * 3 + K + 2 * 4 + 2 + K
            with dve.Fori(1, B - 1) as b:
                step.rebase(base + one * (b - 1))
                iteration(b, True, True, body_items(b - 1)[-1])
                assert step.n == one, (step.n, one)
            step.rebase(base + one * (B - 2))
            iteration(B - 1, True, False, body_items(B - 2)[-1])
            residual(B - 1)
            center(2, B - 1)
            normalise(2, B - 1)
            mixes(2, B - 1)
            for m in range(K):
                final_a(B - 1, m)
            final_b(B - 1)
            part2_dve(dve, step)

        @block.tensor
        def _(pe):
            def product(out, w, x, m, kt, done):
                for k in range(kt):
                    ins = pe.matmul(out, w[:, k, m * P:(m + 1) * P], x[:, k], start=(k == 0), stop=(k == kt - 1))
                ins.then_inc(done, 1)

            pe.wait_ge(S['ones_ready'], 1)
            pe.wait_ge(S['params_loaded'], 32)
            pe.matmul(bank(7)[:, 0:B], ones, condT, start=True, stop=True).then_inc(S['cond_summed'], 1)
            pe.wait_ge(S['ones_ready'], 2)

            def xn(b):
                return XN[:, bass.ds(b, 1)].rearrange("p o k t -> p (o k) t")

            def mean(which, b):
                src = xn(b)
                if which == 1:
                    pe.wait_ge(S['y_tile'], 4 * b + 4)
                else:
                    pe.wait_ge(S['o_evac'], 4 * b + 4)
                for k in range(K):
                    ins = pe.matmul(bank(5), ones, src[:, k], start=(k == 0), stop=(k == K - 1))
                ins.then_inc(S[f'mean{which}_done'], 1)

            def var(which, b):
                src = MR if which == 1 else NR
                pe.wait_ge(S[f'sq{which}_ready'], b + 1)
                for k in range(K):
                    ins = pe.matmul(bank(6), ones, src[:, k], start=(k == 0), stop=(k == K - 1))
                ins.then_inc(S[f'var{which}_done'], 1)

            def rkv(b, m):
                if m == 0:
                    pe.wait_ge(S['mix1_ready'], 3 * b + 3)
                for n, (name, src, done, evac) in enumerate((('Wr', MR, 'r_mm', 'r_evac'), ('Wk', MK, 'k_mm', 'k_evac'),
                                                             ('Wv', MV, 'v_mm', 'v_evac'))):
                    if isinstance(b, int) and b == 0 and m == 0:
                        pe.wait_ge(w_loaded[name], 16)
                    pe.wait_ge(S[evac], 4 * b + m)
                    product(bank(n), W[name], src, m, K, S[done])

            def o_proj(b):
                pe.wait_ge(S['v_evac'], 4 * b + 4)
                if isinstance(b, int) and b == 0:
                    pe.wait_ge(w_loaded['Wout'], 16)
                for m in range(K):
                    if m < 2:
                        if not (isinstance(b, int) and b == 0):
                            pe.wait_ge(S['v2_evac'], 4 * b - 1 + m)
                    else:
                        pe.wait_ge(S['o_evac'], 4 * b + m - 1)
                    product(bank(3 + m % 2), W['Wout'], PROD, m, K, S['o_mm'])

            def r2(b):
                pe.wait_ge(S['mix2_ready'], 2 * b + 2)
                if isinstance(b, int) and b == 0:
                    for n in ('cWr', 'cWk', 'cWv'):
                        pe.wait_ge(w_loaded[n], 16)
                for m in range(K):
                    if m >= 2:
                        pe.wait_ge(S['r2_evac'], 4 * b + m - 1)
                    product(bank(3 + m % 2), W['cWr'], NR, m, K, S['r2_mm'])

            def k2(b):
                for m in range(K):
                    pe.wait_ge(*((S['r2_evac'], 4 * b + m + 3) if m < 2 else (S['k2_evac'], 4 * b + m - 1)))
                    product(bank(3 + m % 2), W['cWk'], NK, m, K, S['k2_mm'])

            def v2(b, m):
                if m == 0:
                    pe.wait_ge(S['k2_ready'], 2 * b + 2)
                if m >= 2:
                    pe.wait_ge(S['v2_evac'], 4 * b + m - 1)
                product(bank(3 + m % 2), W['cWv'], K2S, m, K, S['v2_mm'])

            def iteration(b, prev, nxt):
                rkv(b, 0)
                if prev:
                    mean(2, b - 1)
                rkv(b, 1)
                if prev:
                    var(2, b - 1)
                rkv(b, 2)
                rkv(b, 3)
                if prev:
                    r2(b - 1)
                    k2(b - 1)
                if nxt:
                    mean(1, b + 1)
                if prev:
                    v2(b - 1, 0)
                    v2(b - 1, 1)
                if nxt:
                    var(1, b + 1)
                if prev:
                    v2(b - 1, 2)
                    v2(b - 1, 3)
                o_proj(b)

            mean(1, 0)
            var(1, 0)
            iteration(0, False, True)
            with pe.Fori(1, B - 1) as b:
                iteration(b, True, True)
            iteration(B - 1, True, False)
            mean(2, B - 1)
            var(2, B - 1)
            r2(B - 1)
            k2(B - 1)
            for m in range(K):
                v2(B - 1, m)
            part2_pe(pe)


def kernel(**inputs):
    import numpy as np
    import concourse.bacc as bacc
    from concourse.bass_utils import run_bass_kernel_spmd

    f = {n: np.asarray(v) for n, v in inputs.items()}
    cols = lambda name: f[name].reshape(-1, P).T
    names = ['L0_cond_w', 'L0_cond2_w', 'L0_cond_u', 'L0_cond2_u', 'L0_attn_tm_u', 'L0_attn_ln1_g', 'L0_attn_ln1_b',
             'L0_attn_ln2_g', 'L0_attn_ln2_b', 'L0_attn_tm_mu_r', 'L0_attn_tm_mu_k', 'L0_attn_tm_mu_v',
             'L0_attn_cm_mu_r', 'L0_attn_cm_mu_k']
    arrays = {
        'xT': f['x'].transpose(0, 2, 1), 'fT': f['fside_BxSxS_0'].transpose(0, 2, 1), 'condT': f['cond_512'].T,
        'vectors': np.concatenate([cols(n) for n in names], axis=1),
        'Wr': f['L0_attn_tm_Wr'].T, 'Wk': f['L0_attn_tm_Wk'].T, 'Wv': f['L0_attn_tm_Wv'].T,
        'Wout': f['L0_attn_tm_Wout'].T, 'cWr': f['L0_attn_cm_Wr'].T, 'cWk': f['L0_attn_cm_Wk'].T,
        'cWv': f['L0_attn_cm_Wv'].T, 'gateT': f['L0_ffn_gate_w'].T, 'bias': f['L0_ffn_gate_bias'],
        'fc1T': f['L0_ffn_fc1_w'].T, 'fc2T': f['L0_ffn_fc2_w'].T,
        'w1T': f['L0_ffn_w1'].transpose(0, 2, 1), 'w2T': f['L0_ffn_w2'].transpose(0, 2, 1),
        'upT': f['L0_ffn_shared_up_w'].T, 'downT': f['L0_ffn_shared_down_w'].T,
    }
    arrays = {n: np.ascontiguousarray(a) for n, a in arrays.items()}
    nc = bacc.Bacc("TRN2", target_bir_lowering=False, num_devices=1)
    aps = {n: nc.dram_tensor(n, a.shape, F32, kind="ExternalInput").ap() for n, a in arrays.items()}
    b, t, c = f['x'].shape
    aps['out'] = nc.dram_tensor("out", (b, c, t), F32, kind="ExternalOutput").ap()
    build(nc, aps)
    got = run_bass_kernel_spmd(nc, [arrays], core_ids=[0]).results[0]["out"]
    return np.ascontiguousarray(got.transpose(0, 2, 1))
```

```python
import math
from contextlib import ExitStack

import concourse.bass as bass
from concourse import mybir

F32 = mybir.dt.float32
ALU = mybir.AluOpType
ACT = mybir.ActivationFunctionType
AX = mybir.AxisListType

P = 128
VECTORS = ['cond_w', 'cond2_w', 'cond_u', 'cond2_u', 'tm_u', 'ln1_g', 'ln1_b', 'ln2_g', 'ln2_b',
           'mu_r', 'mu_k', 'mu_v', 'cm_mu_r', 'cm_mu_k']
SQUARES = ['Wr', 'Wk', 'Wv', 'Wout', 'cWr', 'cWk', 'cWv']
KEY_CAP = 30.0
DEN_FLOOR = 1e-8
LN_EPS = 1e-5
ROUTED_SCALE = 2.5
GATE_SHIFT = -math.log(1e-8)


class Steps:

    def __init__(self, eng, sem):
        self.eng, self.sem, self.base, self.n = eng, sem, 0, 0

    def did(self, instruction):
        instruction.then_inc(self.sem, 1)
        self.n += 1

    def wait(self):
        self.eng.wait_ge(self.sem, self.base + self.n)

    def rebase(self, base):
        self.base, self.n = base, 0


def build(nc, A):
    B, C, T = A['xT'].shape
    K = C // P
    E = A['gateT'].shape[1]
    LAT = A['fc1T'].shape[1]
    KL = LAT // P
    INTER = A['w1T'].shape[2]
    KI = INTER // P
    SH = A['upT'].shape[1]
    KS = SH // P
    TT = T // P
    NT = B * TT
    G = 4
    EG = E // G
    TOPG, TOPK = 2, 8
    SLOT_BLOCKS = -(-((B * T * TOPK + E * (P - 1)) // P) // 4) * 4
    assert T == 512 and C == 512 and B == 4 and K == 4

    q2_dram = nc.dram_tensor("q2_scratch", [B, C, T], F32).ap()
    slots_in = nc.dram_tensor("slots_in", [SLOT_BLOCKS, P, LAT], F32).ap()
    slots_out = nc.dram_tensor("slots_out", [SLOT_BLOCKS, P, LAT], F32).ap()
    xs_dram = nc.dram_tensor("xs_scratch", [B, C, T], F32).ap()

    ctx = ExitStack()
    with ctx:
        limit = 212800 // 4
        arena = ctx.enter_context(nc.sbuf_tensor("arena", [P, limit], F32))
        psum = ctx.enter_context(nc.psum_tensor("banks", [P, 8, 512], F32))
        top = [0]

        def place(*dims):
            n = math.prod(dims)
            at = top[0]
            top[0] += (n + 7) // 8 * 8
            assert top[0] <= limit, (top[0], limit)
            v = arena[:, at:at + n]
            if len(dims) == 1:
                return v
            names = 'abcd'[:len(dims)]
            return v.rearrange(f"p ({' '.join(names)}) -> p {' '.join(names)}",
                               **{c: d for c, d in zip(names, dims)})

        def sem(name):
            return ctx.enter_context(nc.semaphore(name))

        ones = place(P)
        vec = place(len(VECTORS), K)
        small = place(64)
        tf = small[:, 0:4]
        out_scale = small[:, 4:8]
        decay_b = small[:, 8:12]
        eps_col = small[:, 12:13]
        tmu = small[:, 16:20]
        wexp = small[:, 24:32]
        wexp3 = wexp.rearrange("p (w k) -> p w k", w=2)
        condT = small[:, 32:36]
        decay = place(2, K, B)
        rest = place(2, K, B)
        scratch32 = place(2, K, B)
        ini = place(2, 2)
        XN = place(B, K, T)
        kept = top[0]

        W = {n: place(K, C) for n in SQUARES}
        H = place(K, T + 1)
        MR, MK, MV = (place(K, T) for _ in range(3))
        NR, NK = (place(K, T) for _ in range(2))
        PROD = place(K, T)
        R2S, K2S = (place(K, T) for _ in range(2))
        SRt, SKt = (place(T) for _ in range(2))
        XA = place(2, T)
        XF = place(2, T)
        QF = place(2, T)
        RS, TMP = (place(T) for _ in range(2))
        KV = place(2, T)
        EK, EV = (place(T) for _ in range(2))
        EU, EUV = (place(2, T) for _ in range(2))
        F = place(2, 2, T)
        INV = place(T)

        ZROW = NR[:, 0, 0:LAT]
        ZEROS = 8

        def V(name, k):
            return vec[:, VECTORS.index(name), k:k + 1]

        def bank(n):
            return psum[:, n, :]

        S = {n: sem(n) for n in '''
            params_loaded ones_ready cond_summed cond_ready coeffs_ready
            keys_clipped keys_exp ev_ready fwd_done scaled bwd_done den_ready num_ready inv_ready fin_done
            q2_stored0 q2_stored1 k_loaded0 k_loaded1
            xa_loaded0 xa_loaded1 sigx_ready y_ready y_tile
            z1_ready sq1_ready mean1_done var1_done rs1_ready norm1_ready h1_ready mix1_ready
            z2_ready sq2_ready mean2_done var2_done rs2_ready norm2_ready h2_ready mix2_ready
            r_mm k_mm v_mm o_mm r2_mm k2_mm v2_mm
            r_evac k_evac v_evac o_evac r2_evac k2_evac k2_ready v2_evac
            xf_loaded0 xf_loaded1 qf_loaded0 qf_loaded1 xnew_ready xnew_sig xs_ready xs_stored0 xs_stored1
            dve_step act_step pool_step sp_settled pool_settled
            up_loaded down_loaded fg_loaded bias_loaded fg_mm logits_copied rows_copied sig_ready
            selected ranked routed ident_ready slots_zeroed0 slots_zeroed1 zero_ready scattered
            up_mm up_relu up_ready down_mm down_evac w1_loaded w2_loaded
            xg_loaded0 xg_loaded1 xg_loaded2 xg_loaded3 y_stored0 y_stored1 y_stored2 y_stored3
            t1_mm xT_copied m1_mm h_relu h_ready t2_mm hT_copied m2_mm y_copied
            combined yT_mm yT_ready fc2_loaded fc2_mm out_ready out_stored0
            '''.split()}
        w_loaded = {n: sem("loaded_" + n) for n in SQUARES}
        xs_in = [sem(f"xs_in{b}") for b in range(B)]
        gathered = [sem(f"gathered{q}") for q in range(4)]

        def item(i, half, b, k, w, par, stored):
            return dict(i=i, half=half, b=b, k=k, w=w, par=par, stored=stored, prev=None)

        first_items = [item(k, k // 2, 0, k, 0, k % 2, 0) for k in range(K)]
        ORDER = [(1, 0)] + [(0, k) for k in range(K)] + [(1, k) for k in range(1, K)]

        def body_items(b):
            return [item(K + 8 * b + j, 2 + 4 * b + j // 2, b if w else b + 1, k, w, j % 2,
                         2 * b + (1 if j in (2, 4, 6, 7) else 0)) for j, (w, k) in enumerate(ORDER)]

        def last_items(b):
            return [item(K + 8 * b + k, 2 + 4 * b + k // 2, b, k, 1, k % 2, 2 * b + k // 2) for k in range(K)]

        def view(dram, b):
            return dram[b].rearrange("(k p) t -> p k t", p=P)

        NB = SLOT_BLOCKS
        NP = NB // 2
        top[0] = kept
        W1 = place(E, KL, INTER)
        top[0] = kept
        UPW = place(K, SH)
        DOWNW = place(KS, C)
        XS = place(B, K, T)
        assert top[0] == kept + E * KL * INTER
        region2 = top[0]
        W2 = place(E, KI, LAT)
        end2 = top[0]
        top[0] = region2
        FG = place(K, LAT + E)
        BIAS = place(E)
        SC, SB, SEL, EQ, PRE, RM, CW = (place(NT, E) for _ in range(7))
        M8 = place(NT * G, 8)
        GS, GM, OFF = (place(NT, G) for _ in range(3))
        RK, RE = (place(NT, G, G) for _ in range(2))
        LOWER = place(G, G)
        T8 = place(NT, 8)
        CNT, TOT = (place(NT) for _ in range(2))
        COL, INC = (place(E, NT) for _ in range(2))
        RM2 = place(E, NT)
        MANY = place(E, NT)
        NBK, ENDB, START = (place(E) for _ in range(3))
        EBL = place(NB, E)
        EQ3 = arena[:, top[0] - NB * E:top[0] - NB * E + NT * TOPK * E]\
            .rearrange("p (n j e) -> p n j e", n=NT, j=TOPK)
        EBF = place(NB)
        STRICT = place(P)
        JCOL = place(NT)
        ICOL = place(NB)
        assert top[0] <= end2, (top[0], end2)
        top[0] = region2
        GB = place(4, TOPK, LAT)
        FC2 = place(KL, C)
        YL = place(KL, T)
        YR = place(NT, LAT)
        YP = place(2, LAT)
        assert top[0] <= end2
        top[0] = end2
        HS = place(KS, T)
        XLR = place(NT, LAT)
        IDENT = place(P)
        ZERO = IDENT
        POS = place(NT, TOPK)
        POSU = POS.bitcast(mybir.dt.uint32)
        W8 = place(NT, TOPK)
        EB = place(NB)
        EBU = EB.bitcast(mybir.dt.uint32)
        after = top[0]
        top[0] = end2
        XGB = place(4, 2, LAT)
        YO = place(4, 2, LAT)
        XTB = place(2, 2, KL, P)
        HB = place(2, 2, INTER)
        HTB = place(2, 2, KI, P)
        assert top[0] <= end2 + KS * T + NT * LAT
        top[0] = after

        def ld(sp, dst, name):
            return sp.dma_start(dst, A[name].rearrange("(k p) d -> p k d", p=P))

        def load_shared(sp):
            ld(sp, UPW, 'upT').then_inc(S['up_loaded'], 16)
            ld(sp, DOWNW, 'downT').then_inc(S['down_loaded'], 16)

        def pair(dram, i):
            return dram[bass.ds(2 * i, 2)].rearrange("c p d -> p c d")

        def xg_load(sp, i, q, h):
            if not (isinstance(i, int) and i < 4):
                sp.wait_ge(S['t1_mm'], i - 3)
                sp.sem_inc(S['sp_settled'], 1)
            sp.dma_start(XGB[:, q], pair(slots_in, i)).then_inc(S[f'xg_loaded{q}'], 16)

        def y_store(sp, i, q, h):
            sp.wait_ge(S['y_copied'], i + 1)
            sp.sem_inc(S['sp_settled'], 1)
            sp.dma_start(pair(slots_out, i), YO[:, q]).then_inc(S[f'y_stored{q}'], 16)

        def part2_sp(sp):
            sp.wait_ge(S['v_mm'], 4 * B)
            ld(sp, UPW, 'upT').then_inc(S['up_loaded'], 16)
            sp.wait_ge(S['xs_stored0'], 16 * 2 * B)
            sp.wait_ge(S['xs_stored1'], 16 * 2 * B)
            sp.wait_ge(S['v2_mm'], 4 * B)
            ld(sp, FG[:, :, 0:LAT], 'fc1T').then_inc(S['fg_loaded'], 16)
            ld(sp, FG[:, :, LAT:], 'gateT').then_inc(S['fg_loaded'], 16)
            for b in range(B):
                sp.dma_start(XS[:, b], view(xs_dram, b)).then_inc(xs_in[b], 16)
            sp.dma_start(BIAS, A['bias'].partition_broadcast(P)).then_inc(S['bias_loaded'], 16)
            ld(sp, DOWNW, 'downT').then_inc(S['down_loaded'], 16)
            w1 = A['w1T'].rearrange("e (k p) i -> p e k i", p=P)
            w2 = A['w2T'].rearrange("e (k p) i -> p e k i", p=P)
            half, quarter = E // 2, E // 4
            sp.wait_ge(S['fg_mm'], NT)
            for e in range(half + quarter, E, quarter):
                sp.dma_start(W1[:, e:e + quarter], w1[:, e:e + quarter]).then_inc(S['w1_loaded'], 16)
            sp.wait_ge(S['routed'], 2)
            for e in range(0, E, quarter):
                sp.dma_start(W2[:, e:e + quarter], w2[:, e:e + quarter]).then_inc(S['w2_loaded'], 16)
            sp.wait_ge(S['up_mm'], KS * 2)
            sp.dma_start(W1[:, half:half + quarter], w1[:, half:half + quarter]).then_inc(S['w1_loaded'], 16)
            sp.dma_start(W1[:, 0:quarter], w1[:, 0:quarter]).then_inc(S['w1_loaded'], 16)
            sp.wait_ge(S['down_mm'], K * 2)
            sp.dma_start(W1[:, quarter:half], w1[:, quarter:half]).then_inc(S['w1_loaded'], 16)
            sp.wait_ge(S['scattered'], 16 * NT * TOPK)
            for i in range(4):
                xg_load(sp, i, i, 0)

            def step(i, q, h, more):
                if more:
                    xg_load(sp, i + 4, q, h)
                y_store(sp, i, q, h)

            with sp.Fori(0, NP // 4 - 1) as h:
                for q in range(4):
                    step(4 * h + q, q, h, True)
            for q in range(4):
                step(NP - 4 + q, q, NP // 4 - 1, False)
            sp.wait_ge(S['m2_mm'], NP)
            ld(sp, UPW, 'upT').then_inc(S['up_loaded'], 16)
            for b in range(2, B):
                sp.dma_start(XS[:, b], view(xs_dram, b)).then_inc(xs_in[b], 16)
            ld(sp, DOWNW, 'downT').then_inc(S['down_loaded'], 16)
            ld(sp, FC2, 'fc2T').then_inc(S['fc2_loaded'], 16)
            for b in range(B):
                for m in range(K):
                    sp.wait_ge(S['out_ready'], 4 * b + m + 1)
                    sp.dma_start(view(A['out'], b)[:, m, :], XN[:, b, m]).then_inc(S['out_stored0'], 16)
            sp.wait_ge(S['out_stored0'], 16 * B * K)

        def part3_pool(pool):
            pool.wait_ge(S['xs_stored0'], 16 * 2 * B)
            pool.wait_ge(S['xs_stored1'], 16 * 2 * B)
            pool.wait_ge(S['v2_mm'], 4 * B)
            pool.memset(IDENT, 0.0)
            pool.memset(STRICT, 1.0).then_inc(S['ident_ready'], 1)
            pool.wait_ge(S['ident_ready'], 1)
            pool.affine_select(out=IDENT, in_=IDENT, compare_op=ALU.not_equal, fill=1.0, base=0,
                               pattern=[[-1, P]], channel_multiplier=1)
            pool.affine_select(out=STRICT, in_=STRICT, compare_op=ALU.is_gt, fill=0.0, base=0,
                               pattern=[[1, P]], channel_multiplier=-1)
            pool.iota(JCOL, pattern=[[P, NT]], base=0, channel_multiplier=0, allow_small_or_imprecise_dtypes=True)
            pool.iota(ICOL, pattern=[[1, NB]], base=0, channel_multiplier=0,
                      allow_small_or_imprecise_dtypes=True).then_inc(S['ident_ready'], 1)
            pool.wait_ge(S['routed'], 1)
            pool.wait_ge(S['rows_copied'], NT)
            for q in range(2):
                pool.wait_ge(S[f'slots_zeroed{q}'], 16 * ZEROS // 2)
            rows_in = slots_in.rearrange("i p d -> (i p) d")
            rows_out = slots_out.rearrange("i p d -> (i p) d")
            for n in range(NT):
                for j in range(TOPK):
                    pool.indirect_dma_start(rows_in, bass.IndirectOffsetOnAxis(ap=POSU[:, n, j:j + 1], axis=0),
                                            XLR[:, n], None).then_inc(S['scattered'], 16)
            for q in range(4):
                pool.wait_ge(S[f'y_stored{q}'], 16 * (NP // 4))
            pool.wait_ge(S['m2_mm'], NP)
            for n in range(NT):
                if n >= 4:
                    pool.wait_ge(S['combined'], n - 3)
                for j in range(TOPK):
                    pool.indirect_dma_start(GB[:, n % 4, j], None, rows_out,
                                            bass.IndirectOffsetOnAxis(ap=POSU[:, n, j:j + 1], axis=0))\
                        .then_inc(gathered[n % 4], 16)

        def part2_pe(pe):
            def product(out, w, x, m, kt):
                for k in range(kt):
                    ins = pe.matmul(out, w[:, k, m * P:(m + 1) * P], x[k], start=(k == 0), stop=(k == kt - 1))
                return ins

            def shared(b):
                pe.wait_ge(S['up_loaded'], 16 if b < 2 else 32)
                pe.wait_ge(xs_in[b], 16 if b < 2 else 32)
                for m in range(KS):
                    n = KS * b + m
                    if n >= 3:
                        pe.wait_ge(S['up_relu'], n - 2)
                    product(bank(n % 3), UPW, [XS[:, b, k] for k in range(K)], m, K).then_inc(S['up_mm'], 1)
                pe.wait_ge(S['up_ready'], KS // 2 * (b + 1))
                pe.wait_ge(S['down_loaded'], 16 if b < 2 else 32)
                for m in range(K):
                    n = K * b + m
                    if n >= 2:
                        pe.wait_ge(S['down_evac'], n - 1)
                    product(bank(3 + n % 2), DOWNW, [HS[:, k] for k in range(KS)], m, KS).then_inc(S['down_mm'], 1)

            pe.wait_ge(S['fg_loaded'], 32)
            for n in range(NT):
                b, tt = divmod(n, TT)
                if tt == 0:
                    pe.wait_ge(xs_in[b], 16)
                if n >= 3:
                    pe.wait_ge(S['rows_copied'], n - 2)
                    pe.wait_ge(S['logits_copied'], n - 2)
                for k in range(K):
                    ins = pe.matmul(bank(5 + n % 3)[:, 0:LAT + E], XS[:, b, k, tt * P:(tt + 1) * P], FG[:, k],
                                    start=(k == 0), stop=(k == K - 1))
                ins.then_inc(S['fg_mm'], 1)
            shared(0)
            pe.wait_ge(S['selected'], 1)
            pe.wait_ge(S['ident_ready'], 2)
            pe.matmul(bank(5), STRICT, SEL.rearrange("p n e -> p (n e)"), start=True, stop=True)
            pe.matmul(bank(6), ones, SEL.rearrange("p n e -> p (n e)"), start=True, stop=True).then_inc(S['ranked'], 1)
            shared(1)

            def experts(i):
                return [nc.values_load(EBU[0:1, bass.ds(2 * i + c, 1)], engines=(mybir.EngineType.PE,), min_val=0,
                                       max_val=E - 1, skip_runtime_bounds_check_because="the routing caps it")
                        for c in range(2)]

            def t1(i, q, h):
                pe.wait_ge(S[f'xg_loaded{q}'], 16 * h + 16)
                if not (isinstance(i, int) and i < 2):
                    pe.wait_ge(S['xT_copied'], i - 1)
                for c in range(2):
                    for k in range(KL):
                        ins = pe.transpose(bank(q % 2)[:, (c * KL + k) * P:(c * KL + k + 1) * P],
                                           XGB[:, q, c, k * P:(k + 1) * P], IDENT)
                ins.then_inc(S['t1_mm'], 1)

            def m1(i, q, h, e):
                pe.wait_ge(S['xT_copied'], i + 1)
                if not (isinstance(i, int) and i < 2):
                    pe.wait_ge(S['h_relu'], i - 1)
                for c in range(2):
                    for k in range(KL):
                        ins = pe.matmul(bank(2 + q % 2)[:, c * INTER:(c + 1) * INTER], XTB[:, q % 2, c, k],
                                        W1[:, bass.ds(e[c], 1), k].rearrange("p o i -> p (o i)"),
                                        start=(k == 0), stop=(k == KL - 1))
                ins.then_inc(S['m1_mm'], 1)

            def t2(i, q, h):
                pe.wait_ge(S['h_ready'], i + 1)
                if not (isinstance(i, int) and i < 2):
                    pe.wait_ge(S['hT_copied'], i - 1)
                for c in range(2):
                    for k in range(KI):
                        ins = pe.transpose(bank(4 + q % 2)[:, (c * KI + k) * P:(c * KI + k + 1) * P],
                                           HB[:, q % 2, c, k * P:(k + 1) * P], IDENT)
                ins.then_inc(S['t2_mm'], 1)

            def m2(i, q, h, e):
                pe.wait_ge(S['hT_copied'], i + 1)
                if not (isinstance(i, int) and i < 2):
                    pe.wait_ge(S['y_copied'], i - 1)
                for c in range(2):
                    for k in range(KI):
                        ins = pe.matmul(bank(6 + q % 2)[:, c * LAT:(c + 1) * LAT], HTB[:, q % 2, c, k],
                                        W2[:, bass.ds(e[c], 1), k].rearrange("p o i -> p (o i)"),
                                        start=(k == 0), stop=(k == KI - 1))
                ins.then_inc(S['m2_mm'], 1)

            def four(h, first, last):
                known = {}
                for q in range(4):
                    def at(f, d, *more):
                        f(4 * h + q + d, (q + d) % 4, h + (q + d) // 4, *more)
                    if not (last and q > 1):
                        at(t1, 2)
                    if not (last and q > 2):
                        known[q + 1] = experts(4 * h + q + 1)
                        at(m1, 1, known[q + 1])
                    at(t2, 0)
                    if not (first and q == 0):
                        at(m2, -1, known[q - 1] if q - 1 in known else experts(4 * h + q - 1))

            pe.wait_ge(S['w1_loaded'], 64)
            pe.wait_ge(S['w2_loaded'], 64)
            pe.wait_ge(S['routed'], 2)
            pe.wait_ge(S['down_evac'], K * 2)
            pe.wait_ge(S['up_relu'], KS * 2)
            t1(0, 0, 0)
            t1(1, 1, 0)
            m1(0, 0, 0, experts(0))
            four(0, True, False)
            with pe.Fori(1, NP // 4 - 1) as h:
                four(h, False, False)
            four(NP // 4 - 1, False, True)
            m2(NP - 1, 3, NP // 4 - 1, experts(NP - 1))

            def latent(b):
                for tt in range(TT):
                    n = b * TT + tt
                    pe.wait_ge(S['combined'], n + 1)
                    if tt == 0 and b:
                        pe.wait_ge(S['yT_ready'], b)
                    for k in range(KL):
                        ins = pe.transpose(bank(5 + k)[:, tt * P:(tt + 1) * P], YR[:, n, k * P:(k + 1) * P], IDENT)
                    ins.then_inc(S['yT_mm'], 1)
                pe.wait_ge(S['yT_ready'], b + 1)
                for m in range(K):
                    n = K * b + m
                    if n >= 1:
                        pe.wait_ge(S['out_ready'], n)
                    product(bank(7), FC2, [YL[:, k] for k in range(KL)], m, KL).then_inc(S['fc2_mm'], 1)

            pe.wait_ge(S['y_copied'], NP)
            shared(2)
            pe.wait_ge(S['fc2_loaded'], 16)
            latent(0)
            shared(3)
            for b in range(1, B):
                latent(b)

        def part2_act(act, step):
            for n in range(NT):
                act.wait_ge(S['fg_mm'], n + 1)
                if n == 0:
                    act.wait_ge(S['xs_stored0'], 16 * 2 * B)
                    act.wait_ge(S['xs_stored1'], 16 * 2 * B)
                act.activation(SC[:, n], bank(5 + n % 3)[:, LAT:LAT + E], ACT.Copy).then_inc(S['logits_copied'], 1)
            act.wait_ge(S['logits_copied'], NT)
            act.activation(SC, SC, ACT.Sigmoid).then_inc(S['sig_ready'], 1)

            def shared(b):
                for m in range(KS):
                    n = KS * b + m
                    act.wait_ge(S['up_mm'], n + 1)
                    if m == 0 and b:
                        act.wait_ge(S['down_mm'], K * b)
                    act.activation(HS[:, m], bank(n % 3), ACT.Relu).then_inc(S['up_relu'], 1)
                    if m % 2:
                        act.wait_ge(S['up_relu'], n + 1)
                        act.activation(HS[:, m - 1:m + 1], HS[:, m - 1:m + 1], ACT.Square).then_inc(S['up_ready'], 1)

            shared(0)
            shared(1)

            def relu(i, q, h):
                act.wait_ge(S['m1_mm'], i + 1)
                if not (isinstance(i, int) and i < 2):
                    act.wait_ge(S['t2_mm'], i - 1)
                act.activation(HB[:, q % 2].rearrange("p c i -> p (c i)"), bank(2 + q % 2), ACT.Relu)\
                   .then_inc(S['h_relu'], 1)

            def hT(i, q, h):
                act.wait_ge(S['t2_mm'], i + 1)
                if not (isinstance(i, int) and i < 2):
                    act.wait_ge(S['m2_mm'], i - 1)
                act.activation(HTB[:, q % 2].rearrange("p c k s -> p (c k s)"), bank(4 + q % 2), ACT.Copy)\
                   .then_inc(S['hT_copied'], 1)

            def result(i, q, h):
                act.wait_ge(S['m2_mm'], i + 1)
                if not (isinstance(i, int) and i < 4):
                    act.wait_ge(S[f'y_stored{q}'], 16 * h)
                act.activation(YO[:, q].rearrange("p c d -> p (c d)"), bank(6 + q % 2), ACT.Copy)\
                   .then_inc(S['y_copied'], 1)

            def four(h, first, last):
                for q in range(4):
                    if not (last and q > 2):
                        relu(4 * h + q + 1, (q + 1) % 4, h + (q + 1) // 4)
                    hT(4 * h + q, q, h)
                    if not (first and q == 0):
                        result(4 * h + q - 1, (q + 3) % 4, h - (q == 0))

            relu(0, 0, 0)
            four(0, True, False)
            with act.Fori(1, NP // 4 - 1) as h:
                four(h, False, False)
            four(NP // 4 - 1, False, True)
            result(NP - 1, 3, NP // 4 - 1)
            for q in range(4):
                act.wait_ge(S[f'y_stored{q}'], 16 * (NP // 4))
            act.wait_ge(S['t2_mm'], NP)
            act.wait_ge(S['m2_mm'], NP)
            shared(2)
            shared(3)

        def part2_dve(dve, step):
            def did(ins):
                step.did(ins)
                step.wait()

            dve.wait_ge(S['xs_stored0'], 16 * 2 * B)
            dve.wait_ge(S['xs_stored1'], 16 * 2 * B)
            dve.memset(LOWER, 0.0)
            dve.memset(RM, 1.0)
            dve.memset(MANY, 1.0)
            did(dve.memset(RM2, 1.0))
            for g in range(1, G):
                dve.memset(LOWER[:, g, 0:g], 1.0)
            dve.memset(RM2[:, :, 0], 0.0)
            did(dve.memset(RM[:, :, 0], 0.0))
            for n in range(NT):
                dve.wait_ge(S['fg_mm'], n + 1)
                dve.wait_ge(S['logits_copied'], n + 1)
                dve.tensor_copy(XLR[:, n], bank(5 + n % 3)[:, 0:LAT]).then_inc(S['rows_copied'], 1)
            dve.wait_ge(S['sig_ready'], 1)
            dve.wait_ge(S['bias_loaded'], 16)
            bias = BIAS.rearrange("p (o e) -> p o e", o=1).to_broadcast([P, NT, E])
            did(dve.tensor_tensor(SB, SC, bias, ALU.add))
            groups = SB.rearrange("p n (g e) -> p (n g) e", g=G)
            for j in range(NT * G):
                ins = dve.max(M8[:, j], groups[:, j])
            did(ins)
            did(dve.tensor_tensor(GS.rearrange("p n g -> p (n g)"), M8[:, :, 0], M8[:, :, 1], ALU.add))
            own = GS.rearrange("p n (g o) -> p n g o", o=1).to_broadcast([P, NT, G, G])
            other = GS.rearrange("p n (o g) -> p n o g", o=1).to_broadcast([P, NT, G, G])
            dve.tensor_tensor(RK, other, own, ALU.is_gt)
            did(dve.tensor_tensor(RE, other, own, ALU.is_equal))
            low = LOWER.rearrange("p (o g) h -> p o g h", o=1).to_broadcast([P, NT, G, G])
            did(dve.tensor_tensor(RE, RE, low, ALU.mult))
            did(dve.tensor_tensor(RK, RK, RE, ALU.add))
            did(dve.tensor_reduce(GM, RK, AX.X, ALU.add))
            did(dve.tensor_scalar(GM, GM, float(TOPG), None, ALU.is_lt))
            did(dve.tensor_scalar(OFF, GM, 1e30, -1e30, ALU.mult, ALU.add))
            spread = lambda v: v.rearrange("p n (g o) -> p (n g) o", o=1).to_broadcast([P, NT * G, EG])
            did(dve.tensor_tensor(groups, groups, spread(GM), ALU.mult))
            did(dve.tensor_tensor(groups, groups, spread(OFF), ALU.add))
            for n in range(NT):
                ins = dve.max(T8[:, n], SB[:, n])
            did(ins)
            eighth = T8[:, :, TOPK - 1:TOPK].to_broadcast([P, NT, E])
            dve.tensor_tensor(SEL, SB, eighth, ALU.is_gt)
            did(dve.tensor_tensor(EQ, SB, eighth, ALU.is_equal))
            dve.tensor_reduce(CNT, SEL, AX.X, ALU.add)
            flat = lambda v: v.rearrange("p n e -> p (n e)")
            did(dve.tensor_tensor_scan(flat(PRE), flat(RM), flat(EQ), 0.0, ALU.mult, ALU.add))
            did(dve.tensor_scalar(CNT, CNT, -1.0, float(TOPK), ALU.mult, ALU.add))
            over = lambda v: v.rearrange("p (n o) -> p n o", o=1).to_broadcast([P, NT, E])
            did(dve.tensor_tensor(PRE, PRE, over(CNT), ALU.is_le))
            did(dve.tensor_tensor(EQ, EQ, PRE, ALU.mult))
            ins = dve.tensor_tensor(SEL, SEL, EQ, ALU.add)
            ins.then_inc(S['selected'], 1)
            dve.wait_ge(S['selected'], 1)
            did(dve.tensor_tensor(CW, SEL, SC, ALU.mult))
            did(dve.tensor_reduce(TOT, CW, AX.X, ALU.add))
            did(dve.reciprocal(TOT, TOT))
            did(dve.tensor_scalar(TOT, TOT, ROUTED_SCALE, None, ALU.mult))
            did(dve.tensor_tensor(CW, CW, over(TOT), ALU.mult))
            down(dve, 0)
            dve.wait_ge(S['ranked'], 1)
            did(dve.tensor_scalar(COL, bank(6).rearrange("p (n e) -> p e n", n=NT), float(C), None, ALU.mult))
            did(dve.tensor_tensor_scan(flat(INC), flat(RM2), flat(COL), 0.0, ALU.mult, ALU.add))
            total = INC[:, :, NT - 1:NT].to_broadcast([P, E, NT])
            ramp = JCOL.rearrange("p (o j) -> p o j", o=1).to_broadcast([P, E, NT])
            dve.wait_ge(S['ident_ready'], 2)
            did(dve.tensor_tensor(PRE.rearrange("p n e -> p (n e)").rearrange("p (e n) -> p e n", n=NT), total, ramp, ALU.is_gt))
            did(dve.tensor_reduce(NBK, PRE.rearrange("p n e -> p (n e)").rearrange("p (e n) -> p e n", n=NT), AX.X, ALU.add))
            did(dve.tensor_tensor_scan(ENDB, MANY[:, 0:2].rearrange("p a n -> p (a n)"), NBK, 0.0, ALU.mult, ALU.add))
            did(dve.tensor_tensor(START, ENDB, NBK, ALU.subtract))
            did(dve.tensor_scalar(START, START, float(P), 1.0, ALU.mult, ALU.add))
            did(dve.tensor_tensor(INC, INC, COL, ALU.subtract))
            did(dve.tensor_tensor(INC, INC, START.rearrange("p (e o) -> p e o", o=1).to_broadcast([P, E, NT]), ALU.add))
            did(dve.tensor_tensor(SB, bank(5).rearrange("p (n e) -> p n e", n=NT), INC.rearrange("p e n -> p n e"), ALU.add))
            did(dve.tensor_tensor(SB, SB, SEL, ALU.mult))
            for n in range(NT):
                ins = dve.max(T8[:, n], SB[:, n])
            did(ins)
            dve.tensor_scalar(POSU, T8, -1.0, None, ALU.add).then_inc(S['routed'], 1)
            rows = SB.rearrange("p n (o e) -> p n o e", o=1).to_broadcast([P, NT, TOPK, E])
            eight = T8.rearrange("p n (j o) -> p n j o", o=1).to_broadcast([P, NT, TOPK, E])
            did(dve.tensor_tensor(EQ3, rows, eight, ALU.is_equal))
            did(dve.tensor_tensor(EQ3, EQ3, CW.rearrange("p n (o e) -> p n o e", o=1).to_broadcast([P, NT, TOPK, E]), ALU.mult))
            did(dve.tensor_reduce(W8, EQ3, AX.X, ALU.add))
            ends = ENDB.rearrange("p (o e) -> p o e", o=1).to_broadcast([P, NB, E])
            did(dve.tensor_tensor(EBL, ends, ICOL.rearrange("p (i o) -> p i o", o=1).to_broadcast([P, NB, E]), ALU.is_le))
            did(dve.tensor_reduce(EBF, EBL, AX.X, ALU.add))
            dve.tensor_scalar(EBU, EBF, float(E - 1), None, ALU.min).then_inc(S['routed'], 1)
            down(dve, 1)

            def xT(i, q, h):
                dve.wait_ge(S['t1_mm'], i + 1)
                if not (isinstance(i, int) and i < 2):
                    dve.wait_ge(S['m1_mm'], i - 1)
                dve.tensor_copy(XTB[:, q % 2].rearrange("p c k s -> p (c k s)"), bank(q % 2)).then_inc(S['xT_copied'], 1)

            def hidden(i, q, h):
                dve.wait_ge(S['h_relu'], i + 1)
                dve.tensor_tensor(HB[:, q % 2], HB[:, q % 2], HB[:, q % 2], ALU.mult).then_inc(S['h_ready'], 1)

            def four(h, last):
                for q in range(4):
                    if not (last and q > 1):
                        xT(4 * h + q + 2, (q + 2) % 4, h + (q + 2) // 4)
                    if not (last and q > 2):
                        hidden(4 * h + q + 1, (q + 1) % 4, h + (q + 1) // 4)

            xT(0, 0, 0)
            xT(1, 1, 0)
            hidden(0, 0, 0)
            four(0, False)
            with dve.Fori(1, NP // 4 - 1) as h:
                four(h, False)
            four(NP // 4 - 1, True)

            def combine(n):
                dve.wait_ge(gathered[n % 4], 16 * TOPK * (n // 4 + 1))
                for j in range(0, TOPK, 2):
                    for c in range(2):
                        g, w, acc = GB[:, n % 4, j + c], W8[:, n, j + c:j + c + 1], (YR[:, n], YP[:, n % 2])[c]
                        if j == 0:
                            step.did(dve.tensor_scalar(acc, g, w, None, ALU.mult))
                        else:
                            step.did(dve.scalar_tensor_tensor(acc, g, w, acc, ALU.mult, ALU.add))
                    step.wait()
                dve.tensor_tensor(YR[:, n], YR[:, n], YP[:, n % 2], ALU.add)\
                   .then_inc(S['combined'], 1)

            def out(b):
                dve.wait_ge(S['yT_mm'], TT * (b + 1))
                if b:
                    dve.wait_ge(S['fc2_mm'], 4 * b)
                for k in range(KL):
                    ins = dve.tensor_copy(YL[:, k], bank(5 + k))
                ins.then_inc(S['yT_ready'], 1)
                for m in range(K):
                    dve.wait_ge(S['fc2_mm'], 4 * b + m + 1)
                    dve.wait_ge(S['down_evac'], 4 * b + m + 1)
                    dve.tensor_tensor(XN[:, b, m], XN[:, b, m], bank(7), ALU.add).then_inc(S['out_ready'], 1)

            for n in range(NT // 4 + 1):
                combine(n)
            for m in range(K):
                combine(NT // 4 + 1 + m)
                down_tile(dve, 2, m)
            out(0)
            for m in range(K):
                combine(NT // 2 + 1 + m)
                down_tile(dve, 3, m)
            out(1)
            for n in range(NT // 2 + 1 + K, NT):
                combine(n)
            for b in range(2, B):
                out(b)

        def down_tile(dve, b, m):
            n = K * b + m
            dve.wait_ge(S['down_mm'], n + 1)
            dve.tensor_tensor(XN[:, b, m], XN[:, b, m], bank(3 + n % 2), ALU.add).then_inc(S['down_evac'], 1)

        def down(dve, b):
            for m in range(K):
                down_tile(dve, b, m)

        block = ctx.enter_context(nc.Block())

        @block.sync
        def _(sp):
            sp.dma_start(vec, A['vectors'].rearrange("p (v k) -> p v k", k=K)).then_inc(S['params_loaded'], 16)
            sp.dma_start(condT, A['condT']).then_inc(S['params_loaded'], 16)

            def settle():
                sp.sem_inc(S['sp_settled'], 1)

            def load_key(it):
                par = it['par']
                if not (isinstance(it['i'], int) and it['i'] < 2):
                    sp.wait_ge(S['ev_ready'], it['i'] - 1)
                settle()
                sp.dma_start(KV[:, par], view(A['fT'], it['b'])[:, it['k'], :]).then_inc(S[f'k_loaded{par}'], 16)

            def store_q2(it):
                par = it['par']
                sp.wait_ge(S['fin_done'], it['i'] + 1)
                settle()
                sp.dma_start(view(q2_dram, it['b'])[:, it['k'], :], F[:, par, 0]).then_inc(S[f'q2_stored{par}'], 16)

            def load_x(b, k):
                if not (isinstance(b, int) and b == 0 and k < 2):
                    sp.wait_ge(S['y_tile'], 4 * b + k - 1)
                settle()
                sp.dma_start(XA[:, k % 2], view(A['xT'], b)[:, k, :]).then_inc(S[f'xa_loaded{k % 2}'], 16)

            def load_final(b, m):
                first = isinstance(b, int) and b == 0 and m < 2
                if m == 0:
                    sp.wait_ge(S['q2_stored0'], 16 * (2 * b + 2))
                    sp.wait_ge(S['q2_stored1'], 16 * (2 * b + 2))
                    settle()
                if not first:
                    sp.wait_ge(S['xnew_ready'], 4 * b + max(0, m - 1))
                settle()
                sp.dma_start(XF[:, m % 2], view(A['xT'], b)[:, m, :]).then_inc(S[f'xf_loaded{m % 2}'], 16)
                if not first:
                    sp.wait_ge(S[f'xs_stored{m % 2}'], 16 * (2 * b + m // 2))
                settle()
                sp.dma_start(QF[:, m % 2], view(q2_dram, b)[:, m, :]).then_inc(S[f'qf_loaded{m % 2}'], 16)

            def store_xs(b, m):
                sp.wait_ge(S['xs_ready'], 4 * b + m + 1)
                settle()
                sp.dma_start(view(xs_dram, b)[:, m, :], QF[:, m % 2]).then_inc(S[f'xs_stored{m % 2}'], 16)

            def final(b):
                for m in range(K):
                    store_xs(b, m)
                    if m + 2 < K:
                        load_final(b, m + 2)

            def zero_slots(z):
                per = SLOT_BLOCKS // ZEROS
                if z == 0:
                    sp.wait_ge(S['zero_ready'], 1)
                sp.dma_start(slots_in[z * per:(z + 1) * per].rearrange("i p d -> p i d"),
                             ZROW.rearrange("p (o d) -> p o d", o=1).to_broadcast([P, per, LAT]))\
                  .then_inc(S[f'slots_zeroed{z % 2}'], 16)

            def iteration(b, prev, nxt, before):
                items = body_items(b) if nxt else last_items(b)
                for n, it in enumerate(items):
                    if n + 1 < len(items):
                        load_key(items[n + 1])
                    earlier = items[n - 1] if n else before
                    if earlier is not None and earlier['w'] == 1:
                        store_q2(earlier)
                    if not prev:
                        zero_slots(n)
                    if nxt and n == 2:
                        load_x(b + 1, 0)
                        load_x(b + 1, 1)
                    if nxt and n == 5:
                        load_x(b + 1, 2)
                        load_x(b + 1, 3)
                    if prev and n == (5 if nxt else 1):
                        load_final(b - 1, 0)
                        load_final(b - 1, 1)
                if nxt:
                    load_key(last_items(b + 1)[0])
                else:
                    store_q2(items[-1])
                if prev:
                    final(b - 1)

            for it in first_items[:2]:
                load_key(it)
            for n in SQUARES[:3]:
                sp.dma_start(W[n], A[n].rearrange("(k p) d -> p k d", p=P)).then_inc(w_loaded[n], 16)
            for it in first_items[2:]:
                load_key(it)
            load_key(body_items(0)[0])
            load_x(0, 0)
            load_x(0, 1)
            for n in SQUARES[3:]:
                sp.dma_start(W[n], A[n].rearrange("(k p) d -> p k d", p=P)).then_inc(w_loaded[n], 16)
            load_x(0, 2)
            load_x(0, 3)
            iteration(0, False, True, None)
            with sp.Fori(1, B - 1) as b:
                iteration(b, True, True, body_items(b - 1)[-1])
            iteration(B - 1, True, False, body_items(B - 2)[-1])
            load_final(B - 1, 0)
            load_final(B - 1, 1)
            final(B - 1)
            part2_sp(sp)

        @block.gpsimd
        def _(pool):
            step = Steps(pool, S['pool_step'])
            pool.wait_ge(S['params_loaded'], 32)

            def settle():
                pool.sem_inc(S['pool_settled'], 1)

            def pre(it):
                i, k, w, par = it['i'], it['k'], it['w'], it['par']
                pool.wait_ge(S[f'k_loaded{par}'], 16 * it['half'] + 16)
                pool.wait_ge(S['fwd_done'], i)
                settle()
                pool.tensor_scalar(EK, KV[:, par], KEY_CAP, None, ALU.min)
                pool.tensor_scalar(EU[:, par], KV[:, par], V('cond2_u' if w else 'cond_u', k), KEY_CAP,
                                   ALU.add, ALU.min).then_inc(S['keys_clipped'], 1)

            def mid(it):
                i, par = it['i'], it['par']
                pool.wait_ge(S['keys_exp'], i + 1)
                pool.tensor_tensor(EV, EK, KV[:, par], ALU.mult)
                pool.tensor_tensor(EUV[:, par], EU[:, par], KV[:, par], ALU.mult).then_inc(S['ev_ready'], 1)

            def post(it):
                i, par = it['i'], it['par']
                pool.wait_ge(S['bwd_done'], i + 1)
                step.did(pool.tensor_tensor(F[:, par, 1], F[:, par, 1], EU[:, par], ALU.add))
                step.wait()
                settle()
                pool.tensor_scalar(F[:, par, 1], F[:, par, 1], DEN_FLOOR, None, ALU.max).then_inc(S['den_ready'], 1)
                pool.tensor_tensor(F[:, par, 0], F[:, par, 0], EUV[:, par], ALU.add).then_inc(S['num_ready'], 1)

            def slots(items, following):
                for n, it in enumerate(items):
                    nx = items[n + 1] if n + 1 < len(items) else following
                    if nx is not None:
                        pre(nx)
                        mid(nx)
                    post(it)

            pre(first_items[0])
            mid(first_items[0])
            slots(first_items, last_items(0)[0])
            slots(body_items(0), last_items(1)[0])
            base = step.n
            with pool.Fori(1, B - 1) as b:
                step.rebase(base + 8 * (b - 1))
                slots(body_items(b), last_items(b + 1)[0])
                assert step.n == 8
            step.rebase(base + 8 * (B - 2))
            slots(last_items(B - 1), None)
            part3_pool(pool)

        @block.scalar
        def _(act):
            step = Steps(act, S['act_step'])
            act.wait_ge(S['params_loaded'], 32)
            ww = vec[:, 0:2, :].rearrange("p w k -> p (w k)")
            step.did(act.activation(wexp, ww, ACT.Exp))
            step.wait()
            step.did(act.activation(wexp, wexp, ACT.Exp, scale=-1.0))
            act.wait_ge(S['cond_summed'], 1)
            act.activation(tf, bank(7)[:, 0:B], ACT.Sigmoid).then_inc(S['cond_ready'], 1)

            def pre(it):
                i, par = it['i'], it['par']
                act.wait_ge(S['keys_clipped'], i + 1)
                act.activation(EK, EK, ACT.Exp)
                act.activation(EU[:, par], EU[:, par], ACT.Exp).then_inc(S['keys_exp'], 1)

            def mid(it):
                i, par = it['i'], it['par']
                act.wait_ge(S['fwd_done'], i + 1)
                act.activation(F[:, par], F[:, par], ACT.Identity,
                               scale=rest[:, it['w'], it['k'], bass.ds(it['b'], 1)]).then_inc(S['scaled'], 1)

            def post(it):
                i, par = it['i'], it['par']
                act.wait_ge(S['den_ready'], i + 1)
                act.wait_ge(S['fin_done'], i)
                step.did(act.activation(INV, F[:, par, 1], ACT.Ln))
                step.wait()
                act.activation(INV, INV, ACT.Exp, scale=-1.0).then_inc(S['inv_ready'], 1)

            def slot(it, nx):
                mid(it)
                if nx is not None:
                    pre(nx)
                post(it)

            def gates(b, m):
                act.wait_ge(S['v_evac'], 4 * b + m)
                act.wait_ge(S['r_mm'], 4 * b + m + 1)
                act.activation(SRt, bank(0), ACT.Sigmoid).then_inc(S['r_evac'], 1)
                act.wait_ge(S['k_mm'], 4 * b + m + 1)
                act.activation(SKt, bank(1), ACT.Sigmoid, bias=tmu[:, m:m + 1]).then_inc(S['k_evac'], 1)

            def square(which, b):
                act.wait_ge(S[f'z{which}_ready'], b + 1)
                if which == 2:
                    for q in range(2):
                        act.wait_ge(S[f'slots_zeroed{q}'], 16 * ZEROS // 2)
                dst = MR if which == 1 else NR
                act.activation(dst, H[:, :, 1:T + 1], ACT.Square).then_inc(S[f'sq{which}_ready'], 1)

            def rsqrt(which, b):
                act.wait_ge(S[f'var{which}_done'], b + 1)
                step.did(act.activation(RS, bank(6), ACT.Ln, bias=eps_col))
                step.wait()
                act.activation(RS, RS, ACT.Exp, scale=-0.5).then_inc(S[f'rs{which}_ready'], 1)

            def affine(which, b):
                act.wait_ge(S[f'norm{which}_ready'], b + 1)
                for k in range(K):
                    ins = act.activation(H[:, k, 1:T + 1], H[:, k, 1:T + 1], ACT.Identity,
                                         scale=V(f'ln{which}_g', k), bias=V(f'ln{which}_b', k))
                ins.then_inc(S[f'h{which}_ready'], 1)

            def sig_x(b):
                for k in range(K):
                    act.wait_ge(S[f'xa_loaded{k % 2}'], 16 * (2 * b + k // 2 + 1))
                    act.activation(XA[:, k % 2], XA[:, k % 2], ACT.Sigmoid).then_inc(S['sigx_ready'], 1)

            def receptance2(b, m):
                act.wait_ge(S['r2_mm'], 4 * b + m + 1)
                if m == 0:
                    act.wait_ge(S['xnew_ready'], 4 * b)
                act.activation(R2S[:, m], bank(3 + m % 2), ACT.Sigmoid).then_inc(S['r2_evac'], 1)

            def key2(b, m):
                act.wait_ge(S['k2_mm'], 4 * b + m + 1)
                if m == 0:
                    act.wait_ge(S['v2_mm'], 4 * b)
                act.activation(K2S[:, m], bank(3 + m % 2), ACT.Relu).then_inc(S['k2_evac'], 1)
                if m % 2:
                    act.wait_ge(S['k2_evac'], 4 * b + m + 1)
                    act.activation(K2S[:, m - 1:m + 1], K2S[:, m - 1:m + 1], ACT.Square).then_inc(S['k2_ready'], 1)

            def sig_new(b):
                for m in range(K):
                    act.wait_ge(S['xnew_ready'], 4 * b + m + 1)
                    if not (isinstance(b, int) and b == 0 and m == 0):
                        act.wait_ge(S['xs_ready'], 4 * b + max(0, m - 1))
                    act.activation((TMP, RS)[m % 2], XN[:, bass.ds(b, 1), m].rearrange("p o t -> p (o t)"), ACT.Sigmoid).then_inc(S['xnew_sig'], 1)

            def front(b):
                sig_x(b)
                square(1, b)
                rsqrt(1, b)
                affine(1, b)

            def iteration(b, prev, nxt):
                items = body_items(b) if nxt else last_items(b)
                nexts = items[1:] + [last_items(b + 1)[0] if nxt else None]
                gates(b, 0)
                if prev:
                    square(2, b - 1)
                slot(items[0], nexts[0])
                gates(b, 1)
                if prev:
                    rsqrt(2, b - 1)
                    affine(2, b - 1)
                slot(items[1], nexts[1])
                gates(b, 2)
                slot(items[2], nexts[2])
                gates(b, 3)
                slot(items[3], nexts[3])
                if nxt:
                    slot(items[4], nexts[4])
                    sig_x(b + 1)
                if prev:
                    for m in range(K):
                        receptance2(b - 1, m)
                if nxt:
                    slot(items[5], nexts[5])
                if prev:
                    for m in range(K):
                        key2(b - 1, m)
                if nxt:
                    square(1, b + 1)
                    rsqrt(1, b + 1)
                    affine(1, b + 1)
                    slot(items[6], nexts[6])
                    slot(items[7], nexts[7])
                if prev:
                    sig_new(b - 1)

            pre(first_items[0])
            for it, nx in zip(first_items, first_items[1:] + [last_items(0)[0]]):
                slot(it, nx)
            front(0)
            iteration(0, False, True)
            base, one = step.n, 8 + 2
            with act.Fori(1, B - 1) as b:
                step.rebase(base + one * (b - 1))
                iteration(b, True, True)
                assert step.n == one, step.n
            step.rebase(base + one * (B - 2))
            iteration(B - 1, True, False)
            square(2, B - 1)
            rsqrt(2, B - 1)
            affine(2, B - 1)
            for m in range(K):
                receptance2(B - 1, m)
            for m in range(K):
                key2(B - 1, m)
            sig_new(B - 1)
            part2_act(act, step)

        @block.vector
        def _(dve):
            step = Steps(dve, S['dve_step'])
            dve.memset(ZROW, 0.0).then_inc(S['zero_ready'], 1)
            dve.memset(H[:, :, 0:1], 0.0)
            dve.memset(eps_col, LN_EPS)
            dve.memset(ones, 1.0).then_inc(S['ones_ready'], 1)
            dve.wait_ge(S['params_loaded'], 32)
            dve.wait_ge(S['ones_ready'], 1)
            dve.tensor_scalar(tmu, vec[:, VECTORS.index('tm_u')], GATE_SHIFT, None, ALU.add)
            dve.wait_ge(S['cond_ready'], 1)
            dve.memset(ones, 1.0 / C).then_inc(S['ones_ready'], 1)
            step.did(dve.tensor_scalar(decay_b, tf, 0.5, 0.5, ALU.mult, ALU.add))
            step.did(dve.tensor_scalar(out_scale, tf, -0.2, -0.8, ALU.mult, ALU.add))
            step.wait()
            for b in range(B):
                step.did(dve.tensor_scalar(decay[:, :, :, b], wexp3, decay_b[:, b:b + 1], None, ALU.mult))
            step.wait()
            step.did(dve.tensor_scalar(scratch32, decay, -1.0, 1.0, ALU.mult, ALU.add))
            step.did(dve.tensor_scalar(rest, decay, 1.0, None, ALU.add))
            step.wait()
            step.did(dve.tensor_tensor(rest, rest, scratch32, ALU.mult))
            step.wait()

            def dcol(it):
                return decay[:, it['w'], it['k'], bass.ds(it['b'], 1)]

            def xn(b, m):
                return XN[:, bass.ds(b, 1), m].rearrange("p o t -> p (o t)")

            def xn_all(b):
                return XN[:, bass.ds(b, 1)].rearrange("p o k t -> p (o k) t")

            def fwd(it):
                i, par = it['i'], it['par']
                dve.wait_ge(S['ev_ready'], i + 1)
                if not (isinstance(i, int) and i < 2):
                    dve.wait_ge(S['fin_done'], i - 1)
                if not (isinstance(it['stored'], int) and it['stored'] == 0):
                    dve.wait_ge(S[f'q2_stored{par}'], 16 * it['stored'])
                d = dcol(it).to_broadcast([P, T])
                dve.tensor_tensor_scan(F[:, par, 0], d, EV, 0.0, ALU.mult, ALU.add)
                step.did(dve.tensor_tensor_scan(F[:, par, 1], d, EK, 0.0, ALU.mult, ALU.add))
                step.wait()
                dve.tensor_scalar(ini[:, par], F[:, par, :, T - 1], dcol(it), None, ALU.mult)\
                   .then_inc(S['fwd_done'], 1)

            def bwd(it):
                i, par = it['i'], it['par']
                dve.wait_ge(S['scaled'], i + 1)
                d = dcol(it).to_broadcast([P, T])
                for n in range(2):
                    ins = dve.tensor_tensor_scan(F[:, par, n, ::-1], d, F[:, par, n, ::-1],
                                                 ini[:, par, n:n + 1], ALU.mult, ALU.add)
                ins.then_inc(S['bwd_done'], 1)

            def fin(it):
                i, par = it['i'], it['par']
                dve.wait_ge(S['inv_ready'], i + 1)
                step.did(dve.tensor_tensor(F[:, par, 1], F[:, par, 1], INV, ALU.mult))
                dve.wait_ge(S['num_ready'], i + 1)
                step.did(dve.tensor_tensor(F[:, par, 0], F[:, par, 0], INV, ALU.mult))
                step.wait()
                dst = F[:, par, 0] if it['w'] else xn(it['b'], it['k'])
                dve.scalar_tensor_tensor(dst, F[:, par, 1], 2.0, F[:, par, 0], ALU.subtract, ALU.mult)\
                   .then_inc(S['fin_done'], 1)

            def slot(it):
                fwd(it)
                if it['prev'] is not None:
                    fin(it['prev'])
                bwd(it)

            def product(b, m):
                dve.wait_ge(S['k_evac'], 4 * b + m + 1)
                step.did(dve.tensor_tensor(PROD[:, m], SRt, SKt, ALU.mult))
                dve.wait_ge(S['v_mm'], 4 * b + m + 1)
                step.wait()
                dve.tensor_tensor(PROD[:, m], PROD[:, m], bank(2), ALU.mult).then_inc(S['v_evac'], 1)

            def y_stage(b):
                for k in range(K):
                    dve.wait_ge(S['sigx_ready'], 4 * b + k + 1)
                    if k == 0:
                        dve.wait_ge(S['fin_done'], K if isinstance(b, int) and b == 0 else 8 * b + 1)
                    ins = dve.scalar_tensor_tensor(xn(b, k), XA[:, k % 2], out_scale[:, bass.ds(b, 1)], xn(b, k),
                                                   ALU.mult, ALU.mult)
                    ins.then_inc(S['y_tile'], 1)

            def residual(b):
                for m in range(K):
                    dve.wait_ge(S['o_mm'], 4 * b + m + 1)
                    dve.tensor_tensor(xn(b, m), xn(b, m), bank(3 + m % 2), ALU.add).then_inc(S['o_evac'], 1)

            def center(which, b):
                dve.wait_ge(S[f'mean{which}_done'], b + 1)
                mean = psum[:, 5:6, :].to_broadcast([P, K, T])
                dve.tensor_tensor(H[:, :, 1:T + 1], xn_all(b), mean, ALU.subtract).then_inc(S[f'z{which}_ready'], 1)

            def normalise(which, b):
                dve.wait_ge(S[f'rs{which}_ready'], b + 1)
                step.did(dve.scalar_tensor_tensor(TMP, bank(6), eps_col, RS, ALU.add, ALU.mult))
                step.wait()
                step.did(dve.tensor_tensor(TMP, TMP, RS, ALU.mult))
                step.wait()
                step.did(dve.tensor_scalar(TMP, TMP, -0.5, 1.5, ALU.mult, ALU.add))
                step.wait()
                step.did(dve.tensor_tensor(RS, RS, TMP, ALU.mult))
                step.wait()
                rs = RS.rearrange("p (o t) -> p o t", o=1).to_broadcast([P, K, T])
                dve.tensor_tensor(H[:, :, 1:T + 1], H[:, :, 1:T + 1], rs, ALU.mult)\
                   .then_inc(S[f'norm{which}_ready'], 1)

            def mixes(which, b):
                dve.wait_ge(S[f'h{which}_ready'], b + 1)
                names, outs = ((['mu_r', 'mu_k', 'mu_v'], [MR, MK, MV]) if which == 1 else
                               (['cm_mu_r', 'cm_mu_k'], [NR, NK]))
                diff = outs[-1]
                step.did(dve.tensor_tensor(diff, H[:, :, 1:T + 1], H[:, :, 0:T], ALU.subtract))
                step.wait()
                for name, out in zip(names, outs):
                    for k in range(K):
                        ins = dve.scalar_tensor_tensor(out[:, k], diff[:, k], V(name, k), H[:, k, 0:T],
                                                       ALU.mult, ALU.add)
                    ins.then_inc(S[f'mix{which}_ready'], 1)

            def final_a(b, m):
                dve.wait_ge(S['v2_mm'], 4 * b + m + 1)
                dve.wait_ge(S['r2_evac'], 4 * b + m + 1)
                dve.tensor_tensor(R2S[:, m], R2S[:, m], bank(3 + m % 2), ALU.mult).then_inc(S['v2_evac'], 1)

            def x_new(b, m):
                dve.wait_ge(S['v2_evac'], 4 * b + m + 1)
                step.did(dve.tensor_tensor(xn(b, m), xn(b, m), R2S[:, m], ALU.add))
                dve.wait_ge(S[f'xf_loaded{m % 2}'], 16 * (2 * b + m // 2 + 1))
                step.wait()
                dve.tensor_tensor(xn(b, m), xn(b, m), XF[:, m % 2], ALU.add).then_inc(S['xnew_ready'], 1)

            def x_side(b, m):
                dve.wait_ge(S['xnew_sig'], 4 * b + m + 1)
                dve.wait_ge(S[f'qf_loaded{m % 2}'], 16 * (2 * b + m // 2 + 1))
                dve.scalar_tensor_tensor(QF[:, m % 2], (TMP, RS)[m % 2], out_scale[:, bass.ds(b, 1)], QF[:, m % 2],
                                         ALU.mult, ALU.mult).then_inc(S['xs_ready'], 1)

            def final_b(b):
                x_new(b, 0)
                x_new(b, 1)
                x_side(b, 0)
                x_new(b, 2)
                x_side(b, 1)
                x_new(b, 3)
                x_side(b, 2)
                x_side(b, 3)

            def chain(items, before):
                for n, it in enumerate(items):
                    it['prev'] = items[n - 1] if n else before
                return items

            def iteration(b, prev, nxt, before):
                items = chain(body_items(b) if nxt else last_items(b), before)
                if prev:
                    residual(b - 1)
                    center(2, b - 1)
                slot(items[0])
                product(b, 0)
                if prev:
                    normalise(2, b - 1)
                slot(items[1])
                product(b, 1)
                if prev:
                    mixes(2, b - 1)
                slot(items[2])
                product(b, 2)
                slot(items[3])
                product(b, 3)
                if nxt:
                    slot(items[4])
                    fin(items[4])
                    items[5]['prev'] = None
                    y_stage(b + 1)
                    slot(items[5])
                    center(1, b + 1)
                else:
                    fin(items[3])
                if prev:
                    final_a(b - 1, 0)
                    final_a(b - 1, 1)
                if nxt:
                    normalise(1, b + 1)
                if prev:
                    final_a(b - 1, 2)
                if nxt:
                    slot(items[6])
                if prev:
                    final_a(b - 1, 3)
                if nxt:
                    mixes(1, b + 1)
                    slot(items[7])
                if prev:
                    final_b(b - 1)

            chain(first_items, None)
            for it in first_items:
                slot(it)
            fin(first_items[-1])
            y_stage(0)
            center(1, 0)
            normalise(1, 0)
            mixes(1, 0)
            iteration(0, False, True, None)
            base, one = step.n, 8 * 3 + K + 2 * 4 + 2 + K
            with dve.Fori(1, B - 1) as b:
                step.rebase(base + one * (b - 1))
                iteration(b, True, True, body_items(b - 1)[-1])
                assert step.n == one, (step.n, one)
            step.rebase(base + one * (B - 2))
            iteration(B - 1, True, False, body_items(B - 2)[-1])
            residual(B - 1)
            center(2, B - 1)
            normalise(2, B - 1)
            mixes(2, B - 1)
            for m in range(K):
                final_a(B - 1, m)
            final_b(B - 1)
            part2_dve(dve, step)

        @block.tensor
        def _(pe):
            def product(out, w, x, m, kt, done):
                for k in range(kt):
                    ins = pe.matmul(out, w[:, k, m * P:(m + 1) * P], x[:, k], start=(k == 0), stop=(k == kt - 1))
                ins.then_inc(done, 1)

            pe.wait_ge(S['ones_ready'], 1)
            pe.wait_ge(S['params_loaded'], 32)
            pe.matmul(bank(7)[:, 0:B], ones, condT, start=True, stop=True).then_inc(S['cond_summed'], 1)
            pe.wait_ge(S['ones_ready'], 2)

            def xn(b):
                return XN[:, bass.ds(b, 1)].rearrange("p o k t -> p (o k) t")

            def mean(which, b):
                src = xn(b)
                if which == 1:
                    pe.wait_ge(S['y_tile'], 4 * b + 4)
                else:
                    pe.wait_ge(S['o_evac'], 4 * b + 4)
                for k in range(K):
                    ins = pe.matmul(bank(5), ones, src[:, k], start=(k == 0), stop=(k == K - 1))
                ins.then_inc(S[f'mean{which}_done'], 1)

            def var(which, b):
                src = MR if which == 1 else NR
                pe.wait_ge(S[f'sq{which}_ready'], b + 1)
                for k in range(K):
                    ins = pe.matmul(bank(6), ones, src[:, k], start=(k == 0), stop=(k == K - 1))
                ins.then_inc(S[f'var{which}_done'], 1)

            def rkv(b, m):
                if m == 0:
                    pe.wait_ge(S['mix1_ready'], 3 * b + 3)
                for n, (name, src, done, evac) in enumerate((('Wr', MR, 'r_mm', 'r_evac'), ('Wk', MK, 'k_mm', 'k_evac'),
                                                             ('Wv', MV, 'v_mm', 'v_evac'))):
                    if isinstance(b, int) and b == 0 and m == 0:
                        pe.wait_ge(w_loaded[name], 16)
                    pe.wait_ge(S[evac], 4 * b + m)
                    product(bank(n), W[name], src, m, K, S[done])

            def o_proj(b):
                pe.wait_ge(S['v_evac'], 4 * b + 4)
                if isinstance(b, int) and b == 0:
                    pe.wait_ge(w_loaded['Wout'], 16)
                for m in range(K):
                    if m < 2:
                        if not (isinstance(b, int) and b == 0):
                            pe.wait_ge(S['v2_evac'], 4 * b - 1 + m)
                    else:
                        pe.wait_ge(S['o_evac'], 4 * b + m - 1)
                    product(bank(3 + m % 2), W['Wout'], PROD, m, K, S['o_mm'])

            def r2(b):
                pe.wait_ge(S['mix2_ready'], 2 * b + 2)
                if isinstance(b, int) and b == 0:
                    for n in ('cWr', 'cWk', 'cWv'):
                        pe.wait_ge(w_loaded[n], 16)
                for m in range(K):
                    if m >= 2:
                        pe.wait_ge(S['r2_evac'], 4 * b + m - 1)
                    product(bank(3 + m % 2), W['cWr'], NR, m, K, S['r2_mm'])

            def k2(b):
                for m in range(K):
                    pe.wait_ge(*((S['r2_evac'], 4 * b + m + 3) if m < 2 else (S['k2_evac'], 4 * b + m - 1)))
                    product(bank(3 + m % 2), W['cWk'], NK, m, K, S['k2_mm'])

            def v2(b, m):
                if m == 0:
                    pe.wait_ge(S['k2_ready'], 2 * b + 2)
                if m >= 2:
                    pe.wait_ge(S['v2_evac'], 4 * b + m - 1)
                product(bank(3 + m % 2), W['cWv'], K2S, m, K, S['v2_mm'])

            def iteration(b, prev, nxt):
                rkv(b, 0)
                if prev:
                    mean(2, b - 1)
                rkv(b, 1)
                if prev:
                    var(2, b - 1)
                rkv(b, 2)
                rkv(b, 3)
                if prev:
                    r2(b - 1)
                    k2(b - 1)
                if nxt:
                    mean(1, b + 1)
                if prev:
                    v2(b - 1, 0)
                    v2(b - 1, 1)
                if nxt:
                    var(1, b + 1)
                if prev:
                    v2(b - 1, 2)
                    v2(b - 1, 3)
                o_proj(b)

            mean(1, 0)
            var(1, 0)
            iteration(0, False, True)
            with pe.Fori(1, B - 1) as b:
                iteration(b, True, True)
            iteration(B - 1, True, False)
            mean(2, B - 1)
            var(2, B - 1)
            r2(B - 1)
            k2(B - 1)
            for m in range(K):
                v2(B - 1, m)
            part2_pe(pe)


def kernel(**inputs):
    import numpy as np
    import concourse.bacc as bacc
    from concourse.bass_utils import run_bass_kernel_spmd

    f = {n: np.asarray(v) for n, v in inputs.items()}
    cols = lambda name: f[name].reshape(-1, P).T
    names = ['L0_cond_w', 'L0_cond2_w', 'L0_cond_u', 'L0_cond2_u', 'L0_attn_tm_u', 'L0_attn_ln1_g', 'L0_attn_ln1_b',
             'L0_attn_ln2_g', 'L0_attn_ln2_b', 'L0_attn_tm_mu_r', 'L0_attn_tm_mu_k', 'L0_attn_tm_mu_v',
             'L0_attn_cm_mu_r', 'L0_attn_cm_mu_k']
    arrays = {
        'xT': f['x'].transpose(0, 2, 1), 'fT': f['fside_BxSxS_0'].transpose(0, 2, 1), 'condT': f['cond_512'].T,
        'vectors': np.concatenate([cols(n) for n in names], axis=1),
        'Wr': f['L0_attn_tm_Wr'].T, 'Wk': f['L0_attn_tm_Wk'].T, 'Wv': f['L0_attn_tm_Wv'].T,
        'Wout': f['L0_attn_tm_Wout'].T, 'cWr': f['L0_attn_cm_Wr'].T, 'cWk': f['L0_attn_cm_Wk'].T,
        'cWv': f['L0_attn_cm_Wv'].T, 'gateT': f['L0_ffn_gate_w'].T, 'bias': f['L0_ffn_gate_bias'],
        'fc1T': f['L0_ffn_fc1_w'].T, 'fc2T': f['L0_ffn_fc2_w'].T,
        'w1T': f['L0_ffn_w1'].transpose(0, 2, 1), 'w2T': f['L0_ffn_w2'].transpose(0, 2, 1),
        'upT': f['L0_ffn_shared_up_w'].T, 'downT': f['L0_ffn_shared_down_w'].T,
    }
    arrays = {n: np.ascontiguousarray(a) for n, a in arrays.items()}
    nc = bacc.Bacc("TRN2", target_bir_lowering=False, num_devices=1)
    aps = {n: nc.dram_tensor(n, a.shape, F32, kind="ExternalInput").ap() for n, a in arrays.items()}
    b, t, c = f['x'].shape
    aps['out'] = nc.dram_tensor("out", (b, c, t), F32, kind="ExternalOutput").ap()
    build(nc, aps)
    got = run_bass_kernel_spmd(nc, [arrays], core_ids=[0]).results[0]["out"]
    return np.ascontiguousarray(got.transpose(0, 2, 1))
```

```python
import math
from contextlib import ExitStack

import concourse.bass as bass
from concourse import mybir

F32 = mybir.dt.float32
ALU = mybir.AluOpType
ACT = mybir.ActivationFunctionType
AX = mybir.AxisListType

P = 128
VECTORS = ['cond_w', 'cond2_w', 'cond_u', 'cond2_u', 'tm_u', 'ln1_g', 'ln1_b', 'ln2_g', 'ln2_b',
           'mu_r', 'mu_k', 'mu_v', 'cm_mu_r', 'cm_mu_k']
SQUARES = ['Wr', 'Wk', 'Wv', 'Wout', 'cWr', 'cWk', 'cWv']
KEY_CAP = 30.0
DEN_FLOOR = 1e-8
LN_EPS = 1e-5
ROUTED_SCALE = 2.5
GATE_SHIFT = -math.log(1e-8)


class Steps:

    def __init__(self, eng, sem):
        self.eng, self.sem, self.base, self.n = eng, sem, 0, 0

    def did(self, instruction):
        instruction.then_inc(self.sem, 1)
        self.n += 1

    def wait(self):
        self.eng.wait_ge(self.sem, self.base + self.n)

    def rebase(self, base):
        self.base, self.n = base, 0


def build(nc, A):
    B, C, T = A['xT'].shape
    K = C // P
    E = A['gateT'].shape[1]
    LAT = A['fc1T'].shape[1]
    KL = LAT // P
    INTER = A['w1T'].shape[2]
    KI = INTER // P
    SH = A['upT'].shape[1]
    KS = SH // P
    TT = T // P
    NT = B * TT
    G = 4
    EG = E // G
    TOPG, TOPK = 2, 8
    SLOT_BLOCKS = -(-((B * T * TOPK + E * (P - 1)) // P) // 4) * 4
    assert T == 512 and C == 512 and B == 4 and K == 4

    q2_dram = nc.dram_tensor("q2_scratch", [B, C, T], F32).ap()
    slots_in = nc.dram_tensor("slots_in", [SLOT_BLOCKS, P, LAT], F32).ap()
    slots_out = nc.dram_tensor("slots_out", [SLOT_BLOCKS, P, LAT], F32).ap()
    xs_dram = nc.dram_tensor("xs_scratch", [B, C, T], F32).ap()

    ctx = ExitStack()
    with ctx:
        limit = 212800 // 4
        arena = ctx.enter_context(nc.sbuf_tensor("arena", [P, limit], F32))
        psum = ctx.enter_context(nc.psum_tensor("banks", [P, 8, 512], F32))
        top = [0]

        def place(*dims):
            n = math.prod(dims)
            at = top[0]
            top[0] += (n + 7) // 8 * 8
            assert top[0] <= limit, (top[0], limit)
            v = arena[:, at:at + n]
            if len(dims) == 1:
                return v
            names = 'abcd'[:len(dims)]
            return v.rearrange(f"p ({' '.join(names)}) -> p {' '.join(names)}",
                               **{c: d for c, d in zip(names, dims)})

        def sem(name):
            return ctx.enter_context(nc.semaphore(name))

        ones = place(P)
        vec = place(len(VECTORS), K)
        small = place(64)
        tf = small[:, 0:4]
        out_scale = small[:, 4:8]
        decay_b = small[:, 8:12]
        eps_col = small[:, 12:13]
        tmu = small[:, 16:20]
        wexp = small[:, 24:32]
        wexp3 = wexp.rearrange("p (w k) -> p w k", w=2)
        condT = small[:, 32:36]
        decay = place(2, K, B)
        rest = place(2, K, B)
        scratch32 = place(2, K, B)
        ini = place(2, 2)
        XN = place(B, K, T)
        kept = top[0]

        W = {n: place(K, C) for n in SQUARES}
        H = place(K, T + 1)
        MR, MK, MV = (place(K, T) for _ in range(3))
        NR, NK = (place(K, T) for _ in range(2))
        PROD = place(K, T)
        R2S = place(K, T)
        K2S = MK
        SIGS = place(2, T)
        SRt, SKt = SIGS[:, 0], SIGS[:, 1]
        XA = place(2, T)
        XF = place(K, T)
        QF = place(2, T)
        RS, TMP = (place(T) for _ in range(2))
        def q2_again(b, m):
            return SIGS[:, m - 2] if isinstance(b, int) and b == B - 1 and m >= 2 else QF[:, m % 2]

        def qf_loaded(b, m):
            if isinstance(b, int) and b == B - 1 and m >= 2:
                return S[f'last_q2_loaded{m}'], 16, 16
            return S[f'qf_loaded{m % 2}'], 16, 16 * (2 * b + m // 2 + 1)

        def xs_out(b, m):
            return XS[:, b, m] if isinstance(b, int) and b == B - 1 else QF[:, m % 2]

        at_keys = top[0]
        KV = place(2, T)
        EK, EV = (place(T) for _ in range(2))
        EU, EUV = (place(2, T) for _ in range(2))
        F = place(2, 2, T)
        INV = place(T)
        Q2 = place(2, T)

        ZROW = NR[:, 0, 0:LAT]
        ZEROS = 8

        RKV = ((0, 1, 2), (3, 4, 7))
        R2_BANK, K2_BANK, V2_BANK, O_BANK = (3, 4, 7, 0), (1, 2, 3, 4), (7, 0, 1, 2), (3, 4, 7, 3)

        def V(name, k):
            return vec[:, VECTORS.index(name), k:k + 1]

        def bank(n):
            return psum[:, n, :]

        S = {n: sem(n) for n in '''
            params_loaded ones_ready cond_summed cond_ready
            keys_clipped keys_exp ev_ready euv_ready fwd_done bwd_done den_ready num_ready inv_ready scaled_by_inv fin_done
            gates_ready
            q2_stored0 q2_stored1 k_loaded0 k_loaded1
            first_x_loaded xa_loaded0 xa_loaded1 sigx_ready y_tile
            z1_ready sq1_ready mean1_done var1_done rs1_ready norm1_ready h1_ready mix1_ready
            z2_ready sq2_ready mean2_done var2_done rs2_ready norm2_ready h2_ready mix2_ready
            r_mm k_mm v_mm o_mm r2_mm k2_mm v2_mm
            r_evac k_evac v_evac o_evac r2_evac k2_evac k2_ready v2_evac
            xf_loaded x_summed qf_loaded0 qf_loaded1 last_q2_loaded2 last_q2_loaded3
            xnew_ready xnew_sig xs_ready xs_stored0 xs_stored1
            dve_step act_step sp_settled
            up_loaded down_loaded fg_loaded bias_loaded fg_mm logits_copied rows_copied sig_ready
            selected ranked routed ident_ready slots_zeroed0 slots_zeroed1 zero_ready scattered
            up_mm up_relu up_ready down_mm down_evac w1_loaded w2_loaded
            xg_loaded0 xg_loaded1 xg_loaded2 xg_loaded3 y_stored0 y_stored1 y_stored2 y_stored3
            t1_mm xT_copied m1_mm h_relu h_ready t2_mm hT_copied m2_mm y_copied
            combined yT_mm yT_ready fc2_loaded fc2_mm out_ready out_stored0
            '''.split()}
        w_loaded = {n: sem("loaded_" + n) for n in SQUARES}
        xs_in = [sem(f"xs_in{b}") for b in range(B)]
        gathered = [sem(f"gathered{q}") for q in range(4)]

        def item(i, half, b, k, w, par):
            return dict(i=i, half=half, b=b, k=k, w=w, par=par, prev=None)

        first_items = [item(k, k // 2, 0, k, 0, k % 2) for k in range(K)]
        ORDER = [(1, 0)] + [(0, k) for k in range(K)] + [(1, k) for k in range(1, K)]

        def body_items(b):
            return [item(8 * b + j, 4 * b + j // 2, b - 1 if w else b + 1, k, w, j % 2)
                    for j, (w, k) in enumerate(ORDER)]

        second_items = [item(K + k, (K + k) // 2, 1, k, 0, k % 2) for k in range(K)]
        last_items = [item(8 * (B - 1) + j, 4 * (B - 1) + j // 2, B - 2 + j // K, j % K, 1, j % 2) for j in range(8)]

        def view(dram, b):
            return dram[b].rearrange("(k p) t -> p k t", p=P)

        NB = SLOT_BLOCKS
        NP = NB // 2
        top[0] = kept
        W1 = place(E, KL, INTER)
        top[0] = kept
        XS = place(B, K, T)
        UPW = place(K, SH)
        DOWNW = place(KS, C)
        assert top[0] == kept + E * KL * INTER
        region2 = top[0]
        W2 = place(E, KI, LAT)
        end2 = top[0]
        top[0] = region2
        place(8)
        FG = place(K, LAT + E)
        BIAS = place(E)
        SC = place(NT, E)
        assert top[0] <= region2 + K * T
        SB, SEL, EQ, PRE, RM, CW = (place(NT, E) for _ in range(6))
        M8 = place(NT * G, 8)
        GS, GM, OFF = (place(NT, G) for _ in range(3))
        RK, RE = (place(NT, G, G) for _ in range(2))
        LOWER = place(G, G)
        T8 = place(NT, 8)
        CNT, TOT = (place(NT) for _ in range(2))
        COL, INC = (place(E, NT) for _ in range(2))
        RM2 = place(E, NT)
        MANY = place(E, NT)
        NBK, ENDB, START = (place(E) for _ in range(3))
        EBL = place(NB, E)
        EQ3 = arena[:, top[0] - NB * E:top[0] - NB * E + NT * TOPK * E]\
            .rearrange("p (n j e) -> p n j e", n=NT, j=TOPK)
        EBF = place(NB)
        STRICT = place(P)
        JCOL = place(NT)
        ICOL = place(NB)
        assert top[0] <= end2, (top[0], end2)
        top[0] = region2
        GB = place(4, TOPK, LAT)
        FC2 = place(KL, C)
        YL = place(KL, T)
        YR = place(NT, LAT)
        YP = place(2, LAT)
        assert top[0] <= end2
        top[0] = end2
        HS = place(KS, T)
        assert top[0] <= at_keys
        top[0] = at_keys
        XLR = place(NT, LAT)
        rings_end = top[0]
        IDENT = place(P)
        POS = place(NT, TOPK)
        POSU = POS.bitcast(mybir.dt.uint32)
        W8 = place(NT, TOPK)
        EB = place(NB)
        EBU = EB.bitcast(mybir.dt.uint32)
        after = top[0]
        top[0] = end2
        XGB = place(4, 2, LAT)
        YO = place(4, 2, LAT)
        XTB = place(2, 2, KL, P)
        HB = place(2, 2, INTER)
        HTB = place(2, 2, KI, P)
        assert top[0] <= rings_end
        top[0] = after

        def ld(sp, dst, name):
            return sp.dma_start(dst, A[name].rearrange("(k p) d -> p k d", p=P))

        def pair(dram, i):
            return dram[bass.ds(2 * i, 2)].rearrange("c p d -> p c d")

        def xg_load(sp, i, q, h):
            if not (isinstance(i, int) and i < 4):
                sp.wait_ge(S['t1_mm'], i - 3)
                sp.sem_inc(S['sp_settled'], 1)
            sp.dma_start(XGB[:, q], pair(slots_in, i)).then_inc(S[f'xg_loaded{q}'], 16)

        def y_store(sp, i, q, h):
            sp.wait_ge(S['y_copied'], i + 1)
            sp.sem_inc(S['sp_settled'], 1)
            sp.dma_start(pair(slots_out, i), YO[:, q]).then_inc(S[f'y_stored{q}'], 16)

        def part2_early_sp(sp, bs):
            if 0 in bs:
                sp.wait_ge(S['v_mm'], 4 * B)
                ld(sp, FG[:, :, 0:LAT], 'fc1T').then_inc(S['fg_loaded'], 16)
                ld(sp, FG[:, :, LAT:], 'gateT').then_inc(S['fg_loaded'], 16)
                sp.dma_start(BIAS, A['bias'].partition_broadcast(P)).then_inc(S['bias_loaded'], 16)
            for q in range(2):
                sp.wait_ge(S[f'xs_stored{q}'], 16 * 2 * (bs[-1] + 1))
            for b in bs:
                sp.dma_start(XS[:, b], view(xs_dram, b)).then_inc(xs_in[b], 16)
            if 0 not in bs:
                sp.wait_ge(S['k2_mm'], 4 * B)
                ld(sp, UPW, 'upT').then_inc(S['up_loaded'], 16)

        def part2_sp(sp):
            sp.wait_ge(S['xs_stored0'], 16 * 2 * B)
            sp.wait_ge(S['xs_stored1'], 16 * 2 * B)
            ld(sp, DOWNW, 'downT').then_inc(S['down_loaded'], 16)
            w1 = A['w1T'].rearrange("e (k p) i -> p e k i", p=P)
            w2 = A['w2T'].rearrange("e (k p) i -> p e k i", p=P)
            quarter = E // 4

            def load_w1(n):
                sp.dma_start(W1[:, n * quarter:(n + 1) * quarter], w1[:, n * quarter:(n + 1) * quarter])\
                  .then_inc(S['w1_loaded'], 16)

            sp.wait_ge(S['routed'], 2)
            for e in range(0, E, quarter):
                sp.dma_start(W2[:, e:e + quarter], w2[:, e:e + quarter]).then_inc(S['w2_loaded'], 16)
            sp.wait_ge(S['up_mm'], KS * 2)
            load_w1(0)
            sp.wait_ge(S['up_mm'], KS * 3)
            load_w1(1)
            load_w1(2)
            sp.wait_ge(S['down_mm'], K * 3)
            load_w1(3)
            sp.wait_ge(S['scattered'], 16 * NT * TOPK)
            for i in range(4):
                xg_load(sp, i, i, 0)

            def step(i, q, h, more):
                if more:
                    xg_load(sp, i + 4, q, h)
                y_store(sp, i, q, h)

            with sp.Fori(0, NP // 4 - 1) as h:
                for q in range(4):
                    step(4 * h + q, q, h, True)
            for q in range(4):
                step(NP - 4 + q, q, NP // 4 - 1, False)
            sp.wait_ge(S['m2_mm'], NP)
            ld(sp, UPW, 'upT').then_inc(S['up_loaded'], 16)
            sp.dma_start(XS[:, B - 1], view(xs_dram, B - 1)).then_inc(xs_in[B - 1], 16)
            ld(sp, DOWNW, 'downT').then_inc(S['down_loaded'], 16)
            ld(sp, FC2, 'fc2T').then_inc(S['fc2_loaded'], 16)
            for b in range(B):
                for m in range(K):
                    sp.wait_ge(S['out_ready'], 4 * b + m + 1)
                    sp.dma_start(view(A['out'], b)[:, m, :], XN[:, b, m]).then_inc(S['out_stored0'], 16)
            sp.wait_ge(S['out_stored0'], 16 * B * K)

        def part3_pool(pool):
            pool.wait_ge(S['xs_stored0'], 16 * 2 * B)
            pool.wait_ge(S['xs_stored1'], 16 * 2 * B)
            pool.wait_ge(S['v2_mm'], 4 * B)
            pool.memset(IDENT, 0.0)
            pool.memset(STRICT, 1.0).then_inc(S['ident_ready'], 1)
            pool.wait_ge(S['ident_ready'], 1)
            pool.affine_select(out=IDENT, in_=IDENT, compare_op=ALU.not_equal, fill=1.0, base=0,
                               pattern=[[-1, P]], channel_multiplier=1)
            pool.affine_select(out=STRICT, in_=STRICT, compare_op=ALU.is_gt, fill=0.0, base=0,
                               pattern=[[1, P]], channel_multiplier=-1)
            pool.iota(JCOL, pattern=[[P, NT]], base=0, channel_multiplier=0, allow_small_or_imprecise_dtypes=True)
            pool.iota(ICOL, pattern=[[1, NB]], base=0, channel_multiplier=0,
                      allow_small_or_imprecise_dtypes=True).then_inc(S['ident_ready'], 1)
            pool.wait_ge(S['routed'], 1)
            pool.wait_ge(S['rows_copied'], NT)
            for q in range(2):
                pool.wait_ge(S[f'slots_zeroed{q}'], 16 * ZEROS // 2)
            rows_in = slots_in.rearrange("i p d -> (i p) d")
            rows_out = slots_out.rearrange("i p d -> (i p) d")
            for n in range(NT):
                for j in range(TOPK):
                    pool.indirect_dma_start(rows_in, bass.IndirectOffsetOnAxis(ap=POSU[:, n, j:j + 1], axis=0),
                                            XLR[:, n], None).then_inc(S['scattered'], 16)
            for q in range(4):
                pool.wait_ge(S[f'y_stored{q}'], 16 * (NP // 4))
            pool.wait_ge(S['m2_mm'], NP)
            for n in range(NT):
                if n >= 4:
                    pool.wait_ge(S['combined'], n - 3)
                for j in range(TOPK):
                    pool.indirect_dma_start(GB[:, n % 4, j], None, rows_out,
                                            bass.IndirectOffsetOnAxis(ap=POSU[:, n, j:j + 1], axis=0))\
                        .then_inc(gathered[n % 4], 16)

        FG_BANK = [n % 3 if n < 8 else 5 + n % 3 for n in range(NT)]

        def fg_tiles(pe, tiles):
            for n in tiles:
                b, tt = divmod(n, TT)
                if n == 0:
                    pe.wait_ge(S['fg_loaded'], 32)
                if tt == 0:
                    pe.wait_ge(*((xs_in[b], 16) if b < B - 1 else (S['xs_ready'], 4 * B)))
                if n == 8:
                    pe.wait_ge(S['v2_evac'], 4 * B)
                if 3 <= n < 8 or n >= 11:
                    pe.wait_ge(S['rows_copied'], n - 2)
                    pe.wait_ge(S['logits_copied'], n - 2)
                for k in range(K):
                    ins = pe.matmul(bank(FG_BANK[n])[:, 0:LAT + E], XS[:, b, k, tt * P:(tt + 1) * P], FG[:, k],
                                    start=(k == 0), stop=(k == K - 1))
                ins.then_inc(S['fg_mm'], 1)

        def logits(act, tiles):
            for n in tiles:
                act.wait_ge(S['fg_mm'], n + 1)
                act.activation(SC[:, n], bank(FG_BANK[n])[:, LAT:LAT + E], ACT.Copy).then_inc(S['logits_copied'], 1)

        def rows(dve, tiles):
            for n in tiles:
                dve.wait_ge(S['logits_copied'], n + 1)
                dve.tensor_copy(XLR[:, n], bank(FG_BANK[n])[:, 0:LAT]).then_inc(S['rows_copied'], 1)

        def part2_pe(pe):
            def product(out, w, x, m, kt):
                for k in range(kt):
                    ins = pe.matmul(out, w[:, k, m * P:(m + 1) * P], x[k], start=(k == 0), stop=(k == kt - 1))
                return ins

            def shared(b, between=lambda: None, after=KS - 1):
                pe.wait_ge(S['up_loaded'], 16 if b < 3 else 32)
                pe.wait_ge(xs_in[b], 16)
                for m in range(KS):
                    n = KS * b + m
                    if n >= 3:
                        pe.wait_ge(S['up_relu'], n - 2)
                    product(bank(n % 3), UPW, [XS[:, b, k] for k in range(K)], m, K).then_inc(S['up_mm'], 1)
                    if m == after:
                        between()
                pe.wait_ge(S['up_ready'], KS // 2 * (b + 1))
                pe.wait_ge(S['down_loaded'], 16 if b < 3 else 32)
                for m in range(K):
                    n = K * b + m
                    if n >= 2:
                        pe.wait_ge(S['down_evac'], n - 1)
                    product(bank(3 + n % 2), DOWNW, [HS[:, k] for k in range(KS)], m, KS).then_inc(S['down_mm'], 1)

            fg_tiles(pe, range(8, NT))
            def ranks():
                pe.wait_ge(S['selected'], 1)
                pe.wait_ge(S['ident_ready'], 2)
                pe.matmul(bank(5), STRICT, SEL.rearrange("p n e -> p (n e)"), start=True, stop=True)
                pe.matmul(bank(6), ones, SEL.rearrange("p n e -> p (n e)"), start=True, stop=True)\
                  .then_inc(S['ranked'], 1)

            shared(0, ranks, 5)
            shared(1)
            shared(2)

            def experts(i):
                return [nc.values_load(EBU[0:1, bass.ds(2 * i + c, 1)], engines=(mybir.EngineType.PE,), min_val=0,
                                       max_val=E - 1, skip_runtime_bounds_check_because="the routing caps it")
                        for c in range(2)]

            def t1(i, q, h):
                pe.wait_ge(S[f'xg_loaded{q}'], 16 * h + 16)
                if not (isinstance(i, int) and i < 2):
                    pe.wait_ge(S['xT_copied'], i - 1)
                for c in range(2):
                    for k in range(KL):
                        ins = pe.transpose(bank(q % 2)[:, (c * KL + k) * P:(c * KL + k + 1) * P],
                                           XGB[:, q, c, k * P:(k + 1) * P], IDENT)
                ins.then_inc(S['t1_mm'], 1)

            def m1(i, q, h, e):
                pe.wait_ge(S['xT_copied'], i + 1)
                if not (isinstance(i, int) and i < 2):
                    pe.wait_ge(S['h_relu'], i - 1)
                for c in range(2):
                    for k in range(KL):
                        ins = pe.matmul(bank(2 + q % 2)[:, c * INTER:(c + 1) * INTER], XTB[:, q % 2, c, k],
                                        W1[:, bass.ds(e[c], 1), k].rearrange("p o i -> p (o i)"),
                                        start=(k == 0), stop=(k == KL - 1))
                ins.then_inc(S['m1_mm'], 1)

            def t2(i, q, h):
                pe.wait_ge(S['h_ready'], i + 1)
                if not (isinstance(i, int) and i < 2):
                    pe.wait_ge(S['hT_copied'], i - 1)
                for c in range(2):
                    for k in range(KI):
                        ins = pe.transpose(bank(4 + q % 2)[:, (c * KI + k) * P:(c * KI + k + 1) * P],
                                           HB[:, q % 2, c, k * P:(k + 1) * P], IDENT)
                ins.then_inc(S['t2_mm'], 1)

            def m2(i, q, h, e):
                pe.wait_ge(S['hT_copied'], i + 1)
                if not (isinstance(i, int) and i < 2):
                    pe.wait_ge(S['y_copied'], i - 1)
                for c in range(2):
                    for k in range(KI):
                        ins = pe.matmul(bank(6 + q % 2)[:, c * LAT:(c + 1) * LAT], HTB[:, q % 2, c, k],
                                        W2[:, bass.ds(e[c], 1), k].rearrange("p o i -> p (o i)"),
                                        start=(k == 0), stop=(k == KI - 1))
                ins.then_inc(S['m2_mm'], 1)

            def four(h, first, last):
                known = {}
                for q in range(4):
                    def at(f, d, *more):
                        f(4 * h + q + d, (q + d) % 4, h + (q + d) // 4, *more)
                    if not (last and q > 2):
                        known[q + 1] = experts(4 * h + q + 1)
                    if q < 2 and not (first and q == 0):
                        known[q - 1] = experts(4 * h + q - 1)
                    if not (last and q > 1):
                        at(t1, 2)
                    if not (last and q > 2):
                        at(m1, 1, known[q + 1])
                    at(t2, 0)
                    if not (first and q == 0):
                        at(m2, -1, known[q - 1])

            pe.wait_ge(S['w1_loaded'], 64)
            pe.wait_ge(S['w2_loaded'], 64)
            pe.wait_ge(S['routed'], 2)
            pe.wait_ge(S['down_evac'], K * 3)
            pe.wait_ge(S['up_relu'], KS * 3)
            t1(0, 0, 0)
            t1(1, 1, 0)
            m1(0, 0, 0, experts(0))
            four(0, True, False)
            with pe.Fori(1, NP // 4 - 1) as h:
                four(h, False, False)
            four(NP // 4 - 1, False, True)
            m2(NP - 1, 3, NP // 4 - 1, experts(NP - 1))

            def latent(b):
                if b == 0:
                    pe.wait_ge(S['fc2_loaded'], 16)
                    pe.wait_ge(S['up_relu'], KS * B)
                for tt in range(TT):
                    n = b * TT + tt
                    pe.wait_ge(S['combined'], n + 1)
                    if tt == 0 and b:
                        pe.wait_ge(S['yT_ready'], b)
                    for k in range(KL):
                        ins = pe.transpose(bank(5 + k)[:, tt * P:(tt + 1) * P], YR[:, n, k * P:(k + 1) * P], IDENT)
                    ins.then_inc(S['yT_mm'], 1)
                pe.wait_ge(S['yT_ready'], b + 1)
                for m in range(K):
                    n = K * b + m
                    if n >= 2:
                        pe.wait_ge(S['out_ready'], n - 1)
                    product(bank((7, 0)[m % 2]), FC2, [YL[:, k] for k in range(KL)], m, KL).then_inc(S['fc2_mm'], 1)

            pe.wait_ge(S['y_copied'], NP)
            shared(3, lambda: latent(0))
            for b in range(1, B):
                latent(b)

        def part2_act(act, step):
            logits(act, range(8, NT))
            act.wait_ge(S['xs_stored0'], 16 * 2 * B)
            act.wait_ge(S['xs_stored1'], 16 * 2 * B)
            act.wait_ge(S['logits_copied'], NT)
            act.activation(SC, SC, ACT.Sigmoid).then_inc(S['sig_ready'], 1)

            def shared(b):
                for m in range(KS):
                    n = KS * b + m
                    act.wait_ge(S['up_mm'], n + 1)
                    if m == 0 and b:
                        act.wait_ge(S['down_mm'], K * b)
                    act.activation(HS[:, m], bank(n % 3), ACT.Relu).then_inc(S['up_relu'], 1)
                    if m % 2:
                        act.wait_ge(S['up_relu'], n + 1)
                        act.activation(HS[:, m - 1:m + 1], HS[:, m - 1:m + 1], ACT.Square).then_inc(S['up_ready'], 1)

            shared(0)
            shared(1)
            shared(2)

            def relu(i, q, h):
                act.wait_ge(S['m1_mm'], i + 1)
                if not (isinstance(i, int) and i < 2):
                    act.wait_ge(S['t2_mm'], i - 1)
                act.activation(HB[:, q % 2].rearrange("p c i -> p (c i)"), bank(2 + q % 2), ACT.Relu)\
                   .then_inc(S['h_relu'], 1)

            def hT(i, q, h):
                act.wait_ge(S['t2_mm'], i + 1)
                if not (isinstance(i, int) and i < 2):
                    act.wait_ge(S['m2_mm'], i - 1)
                act.activation(HTB[:, q % 2].rearrange("p c k s -> p (c k s)"), bank(4 + q % 2), ACT.Copy)\
                   .then_inc(S['hT_copied'], 1)

            def result(i, q, h):
                act.wait_ge(S['m2_mm'], i + 1)
                if not (isinstance(i, int) and i < 4):
                    act.wait_ge(S[f'y_stored{q}'], 16 * h)
                act.activation(YO[:, q].rearrange("p c d -> p (c d)"), bank(6 + q % 2), ACT.Copy)\
                   .then_inc(S['y_copied'], 1)

            def four(h, first, last):
                for q in range(4):
                    if not (last and q > 2):
                        relu(4 * h + q + 1, (q + 1) % 4, h + (q + 1) // 4)
                    hT(4 * h + q, q, h)
                    if not (first and q == 0):
                        result(4 * h + q - 1, (q + 3) % 4, h - (q == 0))

            relu(0, 0, 0)
            four(0, True, False)
            four(1, False, False)
            with act.Fori(2, NP // 4 - 1) as h:
                four(h, False, False)
            four(NP // 4 - 1, False, True)
            result(NP - 1, 3, NP // 4 - 1)
            for q in range(4):
                act.wait_ge(S[f'y_stored{q}'], 16 * (NP // 4))
            act.wait_ge(S['t2_mm'], NP)
            act.wait_ge(S['m2_mm'], NP)
            shared(3)

        def part2_dve(dve, step):
            def did(ins):
                step.did(ins)
                step.wait()

            rows(dve, range(8, NT))
            dve.wait_ge(S['xs_stored0'], 16 * 2 * B)
            dve.wait_ge(S['xs_stored1'], 16 * 2 * B)
            dve.memset(LOWER, 0.0)
            dve.memset(RM, 1.0)
            dve.memset(MANY, 1.0)
            did(dve.memset(RM2, 1.0))
            for g in range(1, G):
                dve.memset(LOWER[:, g, 0:g], 1.0)
            dve.memset(RM2[:, :, 0], 0.0)
            did(dve.memset(RM[:, :, 0], 0.0))
            dve.wait_ge(S['sig_ready'], 1)
            dve.wait_ge(S['bias_loaded'], 16)
            bias = BIAS.rearrange("p (o e) -> p o e", o=1).to_broadcast([P, NT, E])
            did(dve.tensor_tensor(SB, SC, bias, ALU.add))
            groups = SB.rearrange("p n (g e) -> p (n g) e", g=G)
            for j in range(NT * G):
                ins = dve.max(M8[:, j], groups[:, j])
            did(ins)
            did(dve.tensor_tensor(GS.rearrange("p n g -> p (n g)"), M8[:, :, 0], M8[:, :, 1], ALU.add))
            own = GS.rearrange("p n (g o) -> p n g o", o=1).to_broadcast([P, NT, G, G])
            other = GS.rearrange("p n (o g) -> p n o g", o=1).to_broadcast([P, NT, G, G])
            dve.tensor_tensor(RK, other, own, ALU.is_gt)
            did(dve.tensor_tensor(RE, other, own, ALU.is_equal))
            low = LOWER.rearrange("p (o g) h -> p o g h", o=1).to_broadcast([P, NT, G, G])
            did(dve.tensor_tensor(RE, RE, low, ALU.mult))
            did(dve.tensor_tensor(RK, RK, RE, ALU.add))
            did(dve.tensor_reduce(GM, RK, AX.X, ALU.add))
            did(dve.tensor_scalar(GM, GM, float(TOPG), None, ALU.is_lt))
            did(dve.tensor_scalar(OFF, GM, 1e30, -1e30, ALU.mult, ALU.add))
            spread = lambda v: v.rearrange("p n (g o) -> p (n g) o", o=1).to_broadcast([P, NT * G, EG])
            did(dve.tensor_tensor(groups, groups, spread(GM), ALU.mult))
            did(dve.tensor_tensor(groups, groups, spread(OFF), ALU.add))
            for n in range(NT):
                ins = dve.max(T8[:, n], SB[:, n])
            did(ins)
            eighth = T8[:, :, TOPK - 1:TOPK].to_broadcast([P, NT, E])
            dve.tensor_tensor(SEL, SB, eighth, ALU.is_gt)
            did(dve.tensor_tensor(EQ, SB, eighth, ALU.is_equal))
            dve.tensor_reduce(CNT, SEL, AX.X, ALU.add)
            flat = lambda v: v.rearrange("p n e -> p (n e)")
            did(dve.tensor_tensor_scan(flat(PRE), flat(RM), flat(EQ), 0.0, ALU.mult, ALU.add))
            did(dve.tensor_scalar(CNT, CNT, -1.0, float(TOPK), ALU.mult, ALU.add))
            over = lambda v: v.rearrange("p (n o) -> p n o", o=1).to_broadcast([P, NT, E])
            did(dve.tensor_tensor(PRE, PRE, over(CNT), ALU.is_le))
            did(dve.tensor_tensor(EQ, EQ, PRE, ALU.mult))
            ins = dve.tensor_tensor(SEL, SEL, EQ, ALU.add)
            ins.then_inc(S['selected'], 1)
            dve.wait_ge(S['selected'], 1)
            dve.wait_ge(S['ranked'], 1)
            did(dve.tensor_scalar(COL, bank(6).rearrange("p (n e) -> p e n", n=NT), float(C), None, ALU.mult))
            did(dve.tensor_tensor_scan(flat(INC), flat(RM2), flat(COL), 0.0, ALU.mult, ALU.add))
            total = INC[:, :, NT - 1:NT].to_broadcast([P, E, NT])
            ramp = JCOL.rearrange("p (o j) -> p o j", o=1).to_broadcast([P, E, NT])
            dve.wait_ge(S['ident_ready'], 2)
            did(dve.tensor_tensor(PRE.rearrange("p n e -> p (n e)").rearrange("p (e n) -> p e n", n=NT), total, ramp, ALU.is_gt))
            did(dve.tensor_reduce(NBK, PRE.rearrange("p n e -> p (n e)").rearrange("p (e n) -> p e n", n=NT), AX.X, ALU.add))
            did(dve.tensor_tensor_scan(ENDB, MANY[:, 0:2].rearrange("p a n -> p (a n)"), NBK, 0.0, ALU.mult, ALU.add))
            did(dve.tensor_tensor(START, ENDB, NBK, ALU.subtract))
            did(dve.tensor_scalar(START, START, float(P), 1.0, ALU.mult, ALU.add))
            did(dve.tensor_tensor(INC, INC, COL, ALU.subtract))
            did(dve.tensor_tensor(INC, INC, START.rearrange("p (e o) -> p e o", o=1).to_broadcast([P, E, NT]), ALU.add))
            did(dve.tensor_tensor(SB, bank(5).rearrange("p (n e) -> p n e", n=NT), INC.rearrange("p e n -> p n e"), ALU.add))
            did(dve.tensor_tensor(SB, SB, SEL, ALU.mult))
            for n in range(NT):
                ins = dve.max(T8[:, n], SB[:, n])
            did(ins)
            dve.tensor_scalar(POSU, T8, -1.0, None, ALU.add).then_inc(S['routed'], 1)
            down(dve, 0)
            did(dve.tensor_tensor(CW, SEL, SC, ALU.mult))
            did(dve.tensor_reduce(TOT, CW, AX.X, ALU.add))
            did(dve.reciprocal(TOT, TOT))
            did(dve.tensor_scalar(TOT, TOT, ROUTED_SCALE, None, ALU.mult))
            did(dve.tensor_tensor(CW, CW, over(TOT), ALU.mult))
            slot_rows = SB.rearrange("p n (o e) -> p n o e", o=1).to_broadcast([P, NT, TOPK, E])
            eight = T8.rearrange("p n (j o) -> p n j o", o=1).to_broadcast([P, NT, TOPK, E])
            did(dve.tensor_tensor(EQ3, slot_rows, eight, ALU.is_equal))
            did(dve.tensor_tensor(EQ3, EQ3, CW.rearrange("p n (o e) -> p n o e", o=1).to_broadcast([P, NT, TOPK, E]), ALU.mult))
            did(dve.tensor_reduce(W8, EQ3, AX.X, ALU.add))
            ends = ENDB.rearrange("p (o e) -> p o e", o=1).to_broadcast([P, NB, E])
            did(dve.tensor_tensor(EBL, ends, ICOL.rearrange("p (i o) -> p i o", o=1).to_broadcast([P, NB, E]), ALU.is_le))
            did(dve.tensor_reduce(EBF, EBL, AX.X, ALU.add))
            dve.tensor_scalar(EBU, EBF, float(E - 1), None, ALU.min).then_inc(S['routed'], 1)
            down(dve, 1)
            down(dve, 2)

            def xT(i, q, h):
                dve.wait_ge(S['t1_mm'], i + 1)
                if not (isinstance(i, int) and i < 2):
                    dve.wait_ge(S['m1_mm'], i - 1)
                dve.tensor_copy(XTB[:, q % 2].rearrange("p c k s -> p (c k s)"), bank(q % 2)).then_inc(S['xT_copied'], 1)

            def hidden(i, q, h):
                dve.wait_ge(S['h_relu'], i + 1)
                dve.tensor_tensor(HB[:, q % 2], HB[:, q % 2], HB[:, q % 2], ALU.mult).then_inc(S['h_ready'], 1)

            def four(h, last):
                for q in range(4):
                    if not (last and q > 1):
                        xT(4 * h + q + 2, (q + 2) % 4, h + (q + 2) // 4)
                    if not (last and q > 2):
                        hidden(4 * h + q + 1, (q + 1) % 4, h + (q + 1) // 4)

            xT(0, 0, 0)
            xT(1, 1, 0)
            hidden(0, 0, 0)
            four(0, False)
            with dve.Fori(1, NP // 4 - 1) as h:
                four(h, False)
            four(NP // 4 - 1, True)

            def combine(n):
                dve.wait_ge(gathered[n % 4], 16 * TOPK * (n // 4 + 1))
                for j in range(0, TOPK, 2):
                    for c in range(2):
                        g, w, acc = GB[:, n % 4, j + c], W8[:, n, j + c:j + c + 1], (YR[:, n], YP[:, n % 2])[c]
                        if j == 0:
                            step.did(dve.tensor_scalar(acc, g, w, None, ALU.mult))
                        else:
                            step.did(dve.scalar_tensor_tensor(acc, g, w, acc, ALU.mult, ALU.add))
                    step.wait()
                dve.tensor_tensor(YR[:, n], YR[:, n], YP[:, n % 2], ALU.add)\
                   .then_inc(S['combined'], 1)

            def out(b):
                dve.wait_ge(S['yT_mm'], TT * (b + 1))
                if b:
                    dve.wait_ge(S['fc2_mm'], 4 * b)
                for k in range(KL):
                    ins = dve.tensor_copy(YL[:, k], bank(5 + k))
                ins.then_inc(S['yT_ready'], 1)
                for m in range(K):
                    dve.wait_ge(S['fc2_mm'], 4 * b + m + 1)
                    if m == 0:
                        dve.wait_ge(S['down_evac'], 4 * b + 4)
                    dve.tensor_tensor(XN[:, b, m], XN[:, b, m], bank((7, 0)[m % 2]), ALU.add).then_inc(S['out_ready'], 1)

            for n in range(TT):
                combine(n)
            out(0)
            for m in range(K):
                combine(TT + m)
                down_tile(dve, B - 1, m)
            out(1)
            for b in range(2, B):
                for tt in range(TT):
                    combine(b * TT + tt)
                out(b)

        def down_tile(dve, b, m):
            n = K * b + m
            dve.wait_ge(S['down_mm'], n + 1)
            dve.tensor_tensor(XN[:, b, m], XN[:, b, m], bank(3 + n % 2), ALU.add).then_inc(S['down_evac'], 1)

        def down(dve, b):
            for m in range(K):
                down_tile(dve, b, m)

        block = ctx.enter_context(nc.Block())

        @block.sync
        def _(sp):
            sp.dma_start(vec, A['vectors'].rearrange("p (v k) -> p v k", k=K)).then_inc(S['params_loaded'], 16)
            sp.dma_start(condT, A['condT']).then_inc(S['params_loaded'], 16)

            def settle():
                sp.sem_inc(S['sp_settled'], 1)

            def load_key(it):
                par = it['par']
                if not (isinstance(it['i'], int) and it['i'] < 2):
                    sp.wait_ge(S['euv_ready'], it['i'] - 1)
                settle()
                sp.dma_start(KV[:, par], view(A['fT'], it['b'])[:, it['k'], :]).then_inc(S[f'k_loaded{par}'], 16)

            def store_q2(it):
                ring = it['k'] % 2
                sp.wait_ge(S['fin_done'], it['i'] + 1)
                settle()
                sp.dma_start(view(q2_dram, it['b'])[:, it['k'], :], Q2[:, ring]).then_inc(S[f'q2_stored{ring}'], 16)

            def load_x(b, k):
                if not (isinstance(b, int) and b == 1 and k < 2):
                    sp.wait_ge(S['y_tile'], 4 * b + k - 1)
                settle()
                sp.dma_start(XA[:, k % 2], view(A['xT'], b)[:, k, :]).then_inc(S[f'xa_loaded{k % 2}'], 16)

            def load_x_again(b):
                sp.dma_start(XF, view(A['xT'], b)).then_inc(S['xf_loaded'], 16)

            def load_final(b, m):
                if m == 0:
                    sp.wait_ge(S['q2_stored0'], 16 * (2 * b + 2))
                    sp.wait_ge(S['q2_stored1'], 16 * (2 * b + 2))
                    settle()
                if isinstance(b, int) and b == B - 1 and m >= 2:
                    sp.wait_ge(S['gates_ready'], 4 * B)
                elif m >= 2:
                    sp.wait_ge(S[f'xs_stored{m % 2}'], 16 * (2 * b + m // 2))
                settle()
                sp.dma_start(q2_again(b, m), view(q2_dram, b)[:, m, :]).then_inc(*qf_loaded(b, m)[:2])

            def store_xs(b, m):
                sp.wait_ge(S['xs_ready'], 4 * b + m + 1)
                settle()
                sp.dma_start(view(xs_dram, b)[:, m, :], xs_out(b, m)).then_inc(S[f'xs_stored{m % 2}'], 16)

            def final(b):
                for m in range(K):
                    store_xs(b, m)
                    if m + 2 < K and not (isinstance(b, int) and b == B - 1):
                        load_final(b, m + 2)
                for q in range(2):
                    sp.wait_ge(S[f'xs_stored{q}'], 16 * (2 * b + 2))
                settle()

            def zero_slots(z):
                per = SLOT_BLOCKS // ZEROS
                if z == 0:
                    sp.wait_ge(S['zero_ready'], 1)
                sp.dma_start(slots_in[z * per:(z + 1) * per].rearrange("i p d -> p i d"),
                             ZROW.rearrange("p (o d) -> p o d", o=1).to_broadcast([P, per, LAT]))\
                  .then_inc(S[f'slots_zeroed{z % 2}'], 16)

            def iteration(b, prev, nxt, items, following):
                for n, it in enumerate(items):
                    nx = items[n + 1] if n + 1 < len(items) else following
                    if nx is not None:
                        load_key(nx)
                    if n and items[n - 1]['w']:
                        store_q2(items[n - 1])
                    if not prev:
                        zero_slots(2 * n)
                        zero_slots(2 * n + 1)
                    if nxt and n == 1:
                        load_x(b + 1, 0)
                        load_x(b + 1, 1)
                    if nxt and prev and n == 5:
                        load_x(b + 1, 2)
                        load_x(b + 1, 3)
                    if not nxt and n == K:
                        load_x_again(b - 1)
                        load_final(b - 1, 0)
                        load_final(b - 1, 1)
                if prev:
                    store_q2(items[-1])
                else:
                    load_x(b + 1, 2)
                    load_x(b + 1, 3)
                if not nxt:
                    part2_early_sp(sp, range(B - 2))
                elif prev:
                    load_x_again(b - 1)
                    load_final(b - 1, 0)
                    load_final(b - 1, 1)
                if prev:
                    final(b - 1)

            for it in first_items[:2]:
                load_key(it)
            for n in SQUARES[:3]:
                sp.dma_start(W[n], A[n].rearrange("(k p) d -> p k d", p=P)).then_inc(w_loaded[n], 16)
            for it in first_items[2:]:
                load_key(it)
            load_key(second_items[0])
            sp.dma_start(XF, view(A['xT'], 0)).then_inc(S['first_x_loaded'], 16)
            for n in SQUARES[3:]:
                sp.dma_start(W[n], A[n].rearrange("(k p) d -> p k d", p=P)).then_inc(w_loaded[n], 16)
            iteration(0, False, True, second_items, body_items(1)[0])
            with sp.Fori(1, B - 1) as b:
                iteration(b, True, True, body_items(b), body_items(b + 1)[0])
            iteration(B - 1, True, False, last_items, None)
            load_x_again(B - 1)
            for m in range(K):
                load_final(B - 1, m)
            part2_early_sp(sp, range(B - 2, B - 1))
            final(B - 1)
            part2_sp(sp)

        @block.gpsimd
        def _(pool):
            def mid(it):
                i, par = it['i'], it['par']
                pool.wait_ge(S['keys_exp'], i + 1)
                if not (isinstance(i, int) and i < 2):
                    pool.wait_ge(S['num_ready'], i - 1)
                pool.tensor_tensor(EV, EK, KV[:, par], ALU.mult).then_inc(S['ev_ready'], 1)
                pool.tensor_tensor(EUV[:, par], EU[:, par], KV[:, par], ALU.mult).then_inc(S['euv_ready'], 1)

            def post(it):
                i, par = it['i'], it['par']
                pool.wait_ge(S['bwd_done'], i + 1)
                pool.wait_ge(S['euv_ready'], i + 1)
                pool.tensor_tensor(F[:, par, 0], F[:, par, 0], EUV[:, par], ALU.add).then_inc(S['num_ready'], 1)
                pool.wait_ge(S['inv_ready'], i + 1)
                pool.tensor_tensor(F[:, par, 1], F[:, par, 1], INV, ALU.mult)
                pool.wait_ge(S['num_ready'], i + 1)
                pool.tensor_tensor(F[:, par, 0], F[:, par, 0], INV, ALU.mult).then_inc(S['scaled_by_inv'], 1)

            def gate_product(b, m):
                pool.wait_ge(S['k_evac'], 4 * b + m + 1)
                if m == 0 and not (isinstance(b, int) and b == 0):
                    pool.wait_ge(S['o_mm'], 4 * b)
                pool.tensor_tensor(PROD[:, m], SRt, SKt, ALU.mult).then_inc(S['gates_ready'], 1)

            FIRST, USUAL = {1: (0,), 3: (1,), 4: (2, 3)}, {0: (0,), 1: (1,), 2: (2, 3)}

            def slots(items, following, b=None, gates={}):
                for n, it in enumerate(items):
                    nx = items[n + 1] if n + 1 < len(items) else following
                    for m in gates.get(n, ()):
                        gate_product(b, m)
                    if nx is not None:
                        mid(nx)
                    post(it)
                for m in gates.get(len(items), ()):
                    gate_product(b, m)

            def add_mix(b):
                pool.wait_ge(S['xf_loaded'], 16 * (b + 1))
                for m in range(K):
                    pool.wait_ge(S['v2_evac'], 4 * b + m + 1)
                    pool.tensor_tensor(XF[:, m], XF[:, m], R2S[:, m], ALU.add).then_inc(S['x_summed'], 1)

            mid(first_items[0])
            slots(first_items, second_items[0])
            slots(second_items, body_items(1)[0], 0, FIRST)
            with pool.Fori(1, B - 1) as b:
                slots(body_items(b), body_items(b + 1)[0], b, USUAL)
                add_mix(b - 1)
            slots(last_items, None, B - 1, USUAL)
            add_mix(B - 2)
            add_mix(B - 1)
            part3_pool(pool)

        @block.scalar
        def _(act):
            step = Steps(act, S['act_step'])
            act.wait_ge(S['params_loaded'], 32)
            ww = vec[:, 0:2, :].rearrange("p w k -> p (w k)")
            step.did(act.activation(wexp, ww, ACT.Exp))
            step.wait()
            step.did(act.activation(wexp, wexp, ACT.Exp, scale=-1.0))
            act.wait_ge(S['cond_summed'], 1)
            act.activation(tf, bank(7)[:, 0:B], ACT.Sigmoid).then_inc(S['cond_ready'], 1)

            def pre(it):
                i, par = it['i'], it['par']
                act.wait_ge(S['keys_clipped'], i + 1)
                act.activation(EK, EK, ACT.Exp)
                act.activation(EU[:, par], EU[:, par], ACT.Exp).then_inc(S['keys_exp'], 1)

            def post(it):
                i, par = it['i'], it['par']
                act.wait_ge(S['den_ready'], i + 1)
                act.wait_ge(S['scaled_by_inv'], i)
                step.did(act.activation(INV, F[:, par, 1], ACT.Ln))
                step.wait()
                act.activation(INV, INV, ACT.Exp, scale=-1.0).then_inc(S['inv_ready'], 1)

            def slot(it, nx):
                if nx is not None:
                    pre(nx)
                post(it)

            def gates(b, m):
                act.wait_ge(S['gates_ready'], 4 * b + m)
                act.wait_ge(S['r_mm'], 4 * b + m + 1)
                act.activation(SRt, bank(RKV[m % 2][0]), ACT.Sigmoid).then_inc(S['r_evac'], 1)
                act.wait_ge(S['k_mm'], 4 * b + m + 1)
                act.activation(SKt, bank(RKV[m % 2][1]), ACT.Sigmoid, bias=tmu[:, m:m + 1]).then_inc(S['k_evac'], 1)

            def square(which, b):
                act.wait_ge(S[f'z{which}_ready'], b + 1)
                if which == 2:
                    for q in range(2):
                        act.wait_ge(S[f'slots_zeroed{q}'], 16 * ZEROS // 2)
                dst = MR if which == 1 else NR
                act.activation(dst, H[:, :, 1:T + 1], ACT.Square).then_inc(S[f'sq{which}_ready'], 1)

            def rsqrt(which, b):
                act.wait_ge(S[f'var{which}_done'], b + 1)
                if which == 2 and isinstance(b, int):
                    act.wait_ge(S['xs_ready'], 4 * b)
                step.did(act.activation(RS, bank(6), ACT.Ln, bias=eps_col))
                step.wait()
                act.activation(RS, RS, ACT.Exp, scale=-0.5).then_inc(S[f'rs{which}_ready'], 1)

            def affine(which, b):
                act.wait_ge(S[f'norm{which}_ready'], b + 1)
                for k in range(K):
                    ins = act.activation(H[:, k, 1:T + 1], H[:, k, 1:T + 1], ACT.Identity,
                                         scale=V(f'ln{which}_g', k), bias=V(f'ln{which}_b', k))
                ins.then_inc(S[f'h{which}_ready'], 1)

            def sig_first_x():
                act.wait_ge(S['first_x_loaded'], 16)
                for k in range(K):
                    ins = act.activation(XF[:, k], XF[:, k], ACT.Sigmoid)
                    ins.then_inc(S['sigx_ready'], 1)

            def sig_x(b, ks=range(K)):
                for k in ks:
                    act.wait_ge(S[f'xa_loaded{k % 2}'], 16 * (2 * (b - 1) + k // 2 + 1))
                    act.activation(XA[:, k % 2], XA[:, k % 2], ACT.Sigmoid).then_inc(S['sigx_ready'], 1)

            def receptance2(b, m):
                act.wait_ge(S['r2_mm'], 4 * b + m + 1)
                act.activation(R2S[:, m], bank(R2_BANK[m]), ACT.Sigmoid).then_inc(S['r2_evac'], 1)

            def key2(b, m):
                act.wait_ge(S['k2_mm'], 4 * b + m + 1)
                act.activation(K2S[:, m], bank(K2_BANK[m]), ACT.Relu).then_inc(S['k2_evac'], 1)
                if m % 2:
                    act.wait_ge(S['k2_evac'], 4 * b + m + 1)
                    act.activation(K2S[:, m - 1:m + 1], K2S[:, m - 1:m + 1], ACT.Square).then_inc(S['k2_ready'], 1)

            def sig_new(b):
                for m in range(K):
                    act.wait_ge(S['xnew_ready'], 4 * b + m + 1)
                    if m >= 2:
                        act.wait_ge(S['xs_ready'], 4 * b + m - 1)
                    act.activation((TMP, RS)[m % 2], XN[:, bass.ds(b, 1), m].rearrange("p o t -> p (o t)"), ACT.Sigmoid).then_inc(S['xnew_sig'], 1)

            def front(b):
                square(1, b)
                rsqrt(1, b)
                affine(1, b)

            def ln_exp():
                act.preload_act_table_set("natural_log_exp_and_others")

            def iteration(b, nxt):
                items = body_items(b) if nxt else last_items
                nexts = items[1:] + [body_items(b + 1)[0] if nxt else None]
                gates(b, 0)
                square(2, b - 1)
                ln_exp()
                slot(items[0], nexts[0])
                gates(b, 1)
                ln_exp()
                rsqrt(2, b - 1)
                affine(2, b - 1)
                slot(items[1], nexts[1])
                gates(b, 2)
                gates(b, 3)
                if nxt:
                    sig_x(b + 1, (0, 1))
                ln_exp()
                slot(items[2], nexts[2])
                slot(items[3], nexts[3])
                slot(items[4], nexts[4])
                for m in range(K):
                    receptance2(b - 1, m)
                if nxt:
                    sig_x(b + 1, (2, 3))
                key2(b - 1, 0)
                key2(b - 1, 1)
                ln_exp()
                slot(items[5], nexts[5])
                key2(b - 1, 2)
                key2(b - 1, 3)
                if nxt:
                    square(1, b + 1)
                slot(items[6], nexts[6])
                slot(items[7], nexts[7])
                if nxt:
                    rsqrt(1, b + 1)
                    affine(1, b + 1)
                sig_new(b - 1)

            ln_exp()
            pre(first_items[0])
            for it, nx in zip(first_items, first_items[1:] + [second_items[0]]):
                slot(it, nx)
                if it['k'] == K - 1:
                    sig_first_x()
                    ln_exp()
            front(0)
            items = second_items + [body_items(1)[0]]
            for n in range(K):
                if n in (1, 3):
                    gates(0, n // 2)
                    ln_exp()
                slot(items[n], items[n + 1])
            gates(0, 2)
            sig_x(1, (0, 1))
            gates(0, 3)
            sig_x(1, (2, 3))
            ln_exp()
            square(1, 1)
            rsqrt(1, 1)
            affine(1, 1)
            base, one = step.n, 8 + 2
            with act.Fori(1, B - 1) as b:
                step.rebase(base + one * (b - 1))
                iteration(b, True)
                assert step.n == one, step.n
            step.rebase(base + one * (B - 2))
            iteration(B - 1, False)
            logits(act, range(0, 2))
            square(2, B - 1)
            logits(act, range(2, 4))
            rsqrt(2, B - 1)
            logits(act, range(4, 6))
            affine(2, B - 1)
            logits(act, range(6, 8))
            for m in range(K):
                receptance2(B - 1, m)
            for m in range(K):
                key2(B - 1, m)
            sig_new(B - 1)
            part2_act(act, step)

        @block.vector
        def _(dve):
            step = Steps(dve, S['dve_step'])
            dve.memset(ZROW, 0.0).then_inc(S['zero_ready'], 1)
            dve.memset(H[:, :, 0:1], 0.0)
            dve.memset(eps_col, LN_EPS)
            dve.memset(ones, 1.0).then_inc(S['ones_ready'], 1)
            dve.wait_ge(S['params_loaded'], 32)
            dve.wait_ge(S['ones_ready'], 1)
            dve.tensor_scalar(tmu, vec[:, VECTORS.index('tm_u')], GATE_SHIFT, None, ALU.add)
            dve.wait_ge(S['cond_ready'], 1)
            dve.memset(ones, 1.0 / C).then_inc(S['ones_ready'], 1)
            step.did(dve.tensor_scalar(decay_b, tf, 0.5, 0.5, ALU.mult, ALU.add))
            step.did(dve.tensor_scalar(out_scale, tf, -0.2, -0.8, ALU.mult, ALU.add))
            step.wait()
            for b in range(B):
                step.did(dve.tensor_scalar(decay[:, :, :, b], wexp3, decay_b[:, b:b + 1], None, ALU.mult))
            step.wait()
            step.did(dve.tensor_scalar(scratch32, decay, -1.0, 1.0, ALU.mult, ALU.add))
            step.did(dve.tensor_scalar(rest, decay, 1.0, None, ALU.add))
            step.wait()
            step.did(dve.tensor_tensor(rest, rest, scratch32, ALU.mult))
            step.wait()

            def dcol(it):
                return decay[:, it['w'], it['k'], bass.ds(it['b'], 1)]

            def xn(b, m):
                return XN[:, bass.ds(b, 1), m].rearrange("p o t -> p (o t)")

            def xn_all(b):
                return XN[:, bass.ds(b, 1)].rearrange("p o k t -> p (o k) t")

            def clip(it):
                k, par = it['k'], it['par']
                dve.wait_ge(S[f'k_loaded{par}'], 16 * it['half'] + 16)
                step.wait()
                dve.tensor_scalar(EK, KV[:, par], KEY_CAP, None, ALU.min)
                dve.tensor_scalar(EU[:, par], KV[:, par], V('cond2_u' if it['w'] else 'cond_u', k), KEY_CAP,
                                  ALU.add, ALU.min).then_inc(S['keys_clipped'], 1)

            def fwd(it):
                i, par = it['i'], it['par']
                dve.wait_ge(S['ev_ready'], i + 1)
                if not (isinstance(i, int) and i < 2):
                    dve.wait_ge(S['fin_done'], i - 1)
                d = dcol(it).to_broadcast([P, T])
                dve.tensor_tensor_scan(F[:, par, 0], d, EV, 0.0, ALU.mult, ALU.add)
                step.did(dve.tensor_tensor_scan(F[:, par, 1], d, EK, 0.0, ALU.mult, ALU.add))
                step.wait()
                dve.tensor_scalar(ini[:, par], F[:, par, :, T - 1], dcol(it), None, ALU.mult)\
                   .then_inc(S['fwd_done'], 1)

            def bwd(it):
                i, par = it['i'], it['par']
                step.wait()
                d = dcol(it).to_broadcast([P, T])
                for n in range(2):
                    ins = dve.tensor_tensor_scan(F[:, par, n, ::-1], d, F[:, par, n, ::-1],
                                                 ini[:, par, n:n + 1], ALU.mult, ALU.add)
                ins.then_inc(S['bwd_done'], 1)
                dve.wait_ge(S['bwd_done'], i + 1)
                step.did(dve.tensor_tensor(F[:, par, 1], F[:, par, 1], EU[:, par], ALU.add))
                step.wait()
                dve.tensor_scalar(F[:, par, 1], F[:, par, 1], DEN_FLOOR, None, ALU.max).then_inc(S['den_ready'], 1)

            def fin(it):
                i, k, par = it['i'], it['k'], it['par']
                dve.wait_ge(S['scaled_by_inv'], i + 1)
                if it['w'] and (k >= 2 or isinstance(it['b'], int) and it['b'] == B - 1):
                    dve.wait_ge(S[f'q2_stored{k % 2}'], 16 * (2 * it['b'] + k // 2))
                dst = Q2[:, k % 2] if it['w'] else xn(it['b'], k)
                dve.scalar_tensor_tensor(dst, F[:, par, 1], 2.0, F[:, par, 0], ALU.subtract, ALU.mult)\
                   .then_inc(S['fin_done'], 1)

            def slot(it):
                fwd(it)
                if it['next'] is not None:
                    clip(it['next'])
                dve.wait_ge(S['fwd_done'], it['i'] + 1)
                step.did(dve.tensor_scalar(F[:, it['par']], F[:, it['par']], rest[:, it['w'], it['k'], bass.ds(it['b'], 1)],
                                           None, ALU.mult))
                if it['prev'] is not None:
                    fin(it['prev'])
                bwd(it)

            def product(b, m):
                dve.wait_ge(S['gates_ready'], 4 * b + m + 1)
                dve.wait_ge(S['v_mm'], 4 * b + m + 1)
                dve.tensor_tensor(PROD[:, m], PROD[:, m], bank(RKV[m % 2][2]), ALU.mult).then_inc(S['v_evac'], 1)

            def y_stage(b, ks=range(K)):
                for k in ks:
                    dve.wait_ge(S['sigx_ready'], 4 * b + k + 1)
                    if k == 0:
                        dve.wait_ge(S['fin_done'], K if isinstance(b, int) and b == 0 else 8 * b - 3)
                    sig = XF[:, k] if isinstance(b, int) and b == 0 else XA[:, k % 2]
                    ins = dve.scalar_tensor_tensor(xn(b, k), sig, out_scale[:, bass.ds(b, 1)], xn(b, k),
                                                   ALU.mult, ALU.mult)
                    ins.then_inc(S['y_tile'], 1)

            def residual(b, m):
                dve.wait_ge(S['o_mm'], 4 * b + m + 1)
                dve.tensor_tensor(xn(b, m), xn(b, m), bank(O_BANK[m]), ALU.add).then_inc(S['o_evac'], 1)

            def center(which, b):
                dve.wait_ge(S[f'mean{which}_done'], b + 1)
                mean = psum[:, 5:6, :].to_broadcast([P, K, T])
                dve.tensor_tensor(H[:, :, 1:T + 1], xn_all(b), mean, ALU.subtract).then_inc(S[f'z{which}_ready'], 1)

            def normalise(which, b):
                dve.wait_ge(S[f'rs{which}_ready'], b + 1)
                step.did(dve.scalar_tensor_tensor(TMP, bank(6), eps_col, RS, ALU.add, ALU.mult))
                step.wait()
                step.did(dve.tensor_tensor(TMP, TMP, RS, ALU.mult))
                step.wait()
                step.did(dve.tensor_scalar(TMP, TMP, -0.5, 1.5, ALU.mult, ALU.add))
                step.wait()
                step.did(dve.tensor_tensor(RS, RS, TMP, ALU.mult))
                step.wait()
                rs = RS.rearrange("p (o t) -> p o t", o=1).to_broadcast([P, K, T])
                dve.tensor_tensor(H[:, :, 1:T + 1], H[:, :, 1:T + 1], rs, ALU.mult)\
                   .then_inc(S[f'norm{which}_ready'], 1)

            def mixes(which, b, between=lambda n: None):
                dve.wait_ge(S[f'h{which}_ready'], b + 1)
                names, outs = ((['mu_r', 'mu_k', 'mu_v'], [MR, MK, MV]) if which == 1 else
                               (['cm_mu_r', 'cm_mu_k'], [NR, NK]))
                diff = outs[-1]
                step.did(dve.tensor_tensor(diff, H[:, :, 1:T + 1], H[:, :, 0:T], ALU.subtract))
                step.wait()
                for n, (name, out) in enumerate(zip(names, outs)):
                    for k in range(K):
                        ins = dve.scalar_tensor_tensor(out[:, k], diff[:, k], V(name, k), H[:, k, 0:T],
                                                       ALU.mult, ALU.add)
                    ins.then_inc(S[f'mix{which}_ready'], 1)
                    between(n)

            def final_a(b, m):
                dve.wait_ge(S['v2_mm'], 4 * b + m + 1)
                dve.wait_ge(S['r2_evac'], 4 * b + m + 1)
                dve.tensor_tensor(R2S[:, m], R2S[:, m], bank(V2_BANK[m]), ALU.mult).then_inc(S['v2_evac'], 1)

            def x_new(b, m):
                dve.wait_ge(S['x_summed'], 4 * b + m + 1)
                dve.tensor_tensor(xn(b, m), xn(b, m), XF[:, m], ALU.add).then_inc(S['xnew_ready'], 1)

            def x_side(b, m):
                dve.wait_ge(S['xnew_sig'], 4 * b + m + 1)
                sem, _, value = qf_loaded(b, m)
                dve.wait_ge(sem, value)
                dve.scalar_tensor_tensor(xs_out(b, m), (TMP, RS)[m % 2], out_scale[:, bass.ds(b, 1)], q2_again(b, m),
                                         ALU.mult, ALU.mult).then_inc(S['xs_ready'], 1)

            def x_new_all(b):
                for m in range(K):
                    x_new(b, m)

            def x_sides(b, ms):
                for m in ms:
                    x_side(b, m)

            def chain(items, following):
                for n, it in enumerate(items):
                    it['prev'] = items[n - 1] if n else None
                    it['next'] = items[n + 1] if n + 1 < len(items) else following
                return items

            def iteration(b, nxt):
                items = chain(body_items(b) if nxt else last_items, body_items(b + 1)[0] if nxt else None)
                center(2, b - 1)
                slot(items[0])
                product(b, 0)
                normalise(2, b - 1)
                slot(items[1])
                product(b, 1)
                mixes(2, b - 1)
                product(b, 2)
                product(b, 3)
                slot(items[2])
                slot(items[3])
                slot(items[4])
                if nxt:
                    fin(items[4])
                    items[5]['prev'] = None
                    y_stage(b + 1)
                slot(items[5])
                if nxt:
                    center(1, b + 1)
                slot(items[6])
                slot(items[7])
                if nxt:
                    normalise(1, b + 1)
                fin(items[7])
                for m in range(K):
                    final_a(b - 1, m)
                if nxt:
                    mixes(1, b + 1, between=lambda n: residual(b, n) if n < 2 else None)
                else:
                    residual(b, 0)
                    residual(b, 1)
                residual(b, 2)
                residual(b, 3)
                x_new_all(b - 1)
                x_sides(b - 1, (0, 1))
                if not nxt:
                    center(2, b)
                    rows(dve, range(0, 4))
                x_sides(b - 1, (2, 3))

            chain(first_items, second_items[0])
            clip(first_items[0])
            for it in first_items:
                slot(it)
            fin(first_items[-1])
            y_stage(0)
            center(1, 0)
            normalise(1, 0)
            mixes(1, 0)
            items = chain(second_items, body_items(1)[0])
            slot(items[0])
            product(0, 0)
            slot(items[1])
            slot(items[2])
            product(0, 1)
            slot(items[3])
            fin(items[3])
            product(0, 2)
            y_stage(1, (0, 1))
            product(0, 3)
            y_stage(1, (2, 3))
            center(1, 1)
            normalise(1, 1)
            mixes(1, 1, between=lambda n: residual(0, n) if n < 2 else None)
            residual(0, 2)
            residual(0, 3)
            base, one = step.n, 8 * 3 + 2 * 4 + 2
            with dve.Fori(1, B - 1) as b:
                step.rebase(base + one * (b - 1))
                iteration(b, True)
                assert step.n == one, (step.n, one)
            step.rebase(base + one * (B - 2))
            iteration(B - 1, False)
            normalise(2, B - 1)
            rows(dve, range(4, 6))
            mixes(2, B - 1)
            rows(dve, range(6, 8))
            for m in range(K):
                final_a(B - 1, m)
            x_new_all(B - 1)
            x_sides(B - 1, range(K))
            part2_dve(dve, step)

        @block.tensor
        def _(pe):
            def product(out, w, x, m, kt, done):
                for k in range(kt):
                    ins = pe.matmul(out, w[:, k, m * P:(m + 1) * P], x[:, k], start=(k == 0), stop=(k == kt - 1))
                ins.then_inc(done, 1)

            pe.wait_ge(S['ones_ready'], 1)
            pe.wait_ge(S['params_loaded'], 32)
            pe.matmul(bank(7)[:, 0:B], ones, condT, start=True, stop=True).then_inc(S['cond_summed'], 1)
            pe.wait_ge(S['ones_ready'], 2)

            def xn(b):
                return XN[:, bass.ds(b, 1)].rearrange("p o k t -> p (o k) t")

            def mean(which, b):
                src = xn(b)
                if not isinstance(b, int):
                    pe.wait_ge(S['y_tile' if which == 1 else 'o_evac'], 4 * b + 4)
                for k in range(K):
                    if isinstance(b, int):
                        pe.wait_ge(S['y_tile' if which == 1 else 'o_evac'], 4 * b + k + 1)
                    ins = pe.matmul(bank(5), ones, src[:, k], start=(k == 0), stop=(k == K - 1))
                ins.then_inc(S[f'mean{which}_done'], 1)

            def var(which, b):
                src = MR if which == 1 else NR
                pe.wait_ge(S[f'sq{which}_ready'], b + 1)
                for k in range(K):
                    ins = pe.matmul(bank(6), ones, src[:, k], start=(k == 0), stop=(k == K - 1))
                ins.then_inc(S[f'var{which}_done'], 1)

            def rkv(b, m):
                later = not (isinstance(b, int) and b == 0)
                if later and m == 1:
                    pe.wait_ge(S['o_evac'], 4 * b)
                for n, (name, src, done, evac) in enumerate((('Wr', MR, 'r_mm', 'r_evac'), ('Wk', MK, 'k_mm', 'k_evac'),
                                                             ('Wv', MV, 'v_mm', 'v_evac'))):
                    if isinstance(b, int) and b == 0 and m == 0:
                        pe.wait_ge(w_loaded[name], 16)
                    if m == 0:
                        pe.wait_ge(S['mix1_ready'], 3 * b + n + 1)
                    if later or m > 1:
                        pe.wait_ge(S[evac], 4 * b + m - 1)
                    product(bank(RKV[m % 2][n]), W[name], src, m, K, S[done])

            def o_proj(b):
                pe.wait_ge(S['v_evac'], 4 * b + 4)
                if isinstance(b, int) and b == 0:
                    pe.wait_ge(w_loaded['Wout'], 16)
                for m in range(K):
                    if not (isinstance(b, int) and b == 0):
                        if m < 2:
                            pe.wait_ge(S['k2_evac'], 4 * b + m - 1)
                        else:
                            pe.wait_ge(S['v2_evac'], 4 * b + (-3 if m == 2 else 0))
                    if m == 3:
                        pe.wait_ge(S['o_evac'], 4 * b + 1)
                    product(bank(O_BANK[m]), W['Wout'], PROD, m, K, S['o_mm'])

            def r2(b):
                pe.wait_ge(S['mix2_ready'], 2 * b + 1)
                if not (isinstance(b, int) and b == B - 1):
                    pe.wait_ge(S['r_evac'], 4 * b + 8)
                    pe.wait_ge(S['k_evac'], 4 * b + 8)
                if isinstance(b, int) and b == 0:
                    for n in ('cWr', 'cWk', 'cWv'):
                        pe.wait_ge(w_loaded[n], 16)
                for m in range(K):
                    if m == 2 and not (isinstance(b, int) and b == B - 1):
                        pe.wait_ge(S['v_evac'], 4 * b + 8)
                    if m == 3 and isinstance(b, int) and b == B - 1:
                        pe.wait_ge(S['rows_copied'], 8)
                        pe.wait_ge(S['logits_copied'], 8)
                    product(bank(R2_BANK[m]), W['cWr'], NR, m, K, S['r2_mm'])

            def k2(b):
                pe.wait_ge(S['mix2_ready'], 2 * b + 2)
                for m in range(K):
                    if m >= 2:
                        pe.wait_ge(S['r2_evac'], 4 * b + m - 1)
                    product(bank(K2_BANK[m]), W['cWk'], NK, m, K, S['k2_mm'])

            def v2(b, m):
                if m == 0:
                    pe.wait_ge(S['k2_ready'], 2 * b + 2)
                    pe.wait_ge(S['r2_evac'], 4 * b + 4)
                product(bank(V2_BANK[m]), W['cWv'], K2S, m, K, S['v2_mm'])

            def iteration(b, prev, nxt):
                rkv(b, 0)
                if prev:
                    mean(2, b - 1)
                rkv(b, 1)
                if prev:
                    var(2, b - 1)
                rkv(b, 2)
                rkv(b, 3)
                if prev:
                    r2(b - 1)
                    k2(b - 1)
                if nxt:
                    mean(1, b + 1)
                if prev:
                    v2(b - 1, 0)
                    v2(b - 1, 1)
                if nxt:
                    var(1, b + 1)
                if prev:
                    v2(b - 1, 2)
                    v2(b - 1, 3)
                o_proj(b)

            mean(1, 0)
            var(1, 0)
            iteration(0, False, True)
            with pe.Fori(1, B - 1) as b:
                iteration(b, True, True)
            iteration(B - 1, True, False)
            mean(2, B - 1)
            fg_tiles(pe, range(0, 4))
            var(2, B - 1)
            fg_tiles(pe, range(4, 8))
            r2(B - 1)
            k2(B - 1)
            for m in range(K):
                v2(B - 1, m)
            part2_pe(pe)


def kernel(**inputs):
    import numpy as np
    import concourse.bacc as bacc
    from concourse.bass_utils import run_bass_kernel_spmd

    f = {n: np.asarray(v) for n, v in inputs.items()}
    cols = lambda name: f[name].reshape(-1, P).T
    names = ['L0_cond_w', 'L0_cond2_w', 'L0_cond_u', 'L0_cond2_u', 'L0_attn_tm_u', 'L0_attn_ln1_g', 'L0_attn_ln1_b',
             'L0_attn_ln2_g', 'L0_attn_ln2_b', 'L0_attn_tm_mu_r', 'L0_attn_tm_mu_k', 'L0_attn_tm_mu_v',
             'L0_attn_cm_mu_r', 'L0_attn_cm_mu_k']
    arrays = {
        'xT': f['x'].transpose(0, 2, 1), 'fT': f['fside_BxSxS_0'].transpose(0, 2, 1), 'condT': f['cond_512'].T,
        'vectors': np.concatenate([cols(n) for n in names], axis=1),
        'Wr': f['L0_attn_tm_Wr'].T, 'Wk': f['L0_attn_tm_Wk'].T, 'Wv': f['L0_attn_tm_Wv'].T,
        'Wout': f['L0_attn_tm_Wout'].T, 'cWr': f['L0_attn_cm_Wr'].T, 'cWk': f['L0_attn_cm_Wk'].T,
        'cWv': f['L0_attn_cm_Wv'].T, 'gateT': f['L0_ffn_gate_w'].T, 'bias': f['L0_ffn_gate_bias'],
        'fc1T': f['L0_ffn_fc1_w'].T, 'fc2T': f['L0_ffn_fc2_w'].T,
        'w1T': f['L0_ffn_w1'].transpose(0, 2, 1), 'w2T': f['L0_ffn_w2'].transpose(0, 2, 1),
        'upT': f['L0_ffn_shared_up_w'].T, 'downT': f['L0_ffn_shared_down_w'].T,
    }
    arrays = {n: np.ascontiguousarray(a) for n, a in arrays.items()}
    nc = bacc.Bacc("TRN2", target_bir_lowering=False, num_devices=1)
    aps = {n: nc.dram_tensor(n, a.shape, F32, kind="ExternalInput").ap() for n, a in arrays.items()}
    b, t, c = f['x'].shape
    aps['out'] = nc.dram_tensor("out", (b, c, t), F32, kind="ExternalOutput").ap()
    build(nc, aps)
    got = run_bass_kernel_spmd(nc, [arrays], core_ids=[0]).results[0]["out"]
    return np.ascontiguousarray(got.transpose(0, 2, 1))
```
